# Optimizing a Trainium2 kernel written in Bass

```python
import numpy as np
import jax
import jax.numpy as jnp

def _softmax(x, axis=-1):
    return jax.nn.softmax(x, axis=axis)

def _gelu(x):
    return jax.nn.gelu(x, approximate=True)

def _silu(x):
    return jax.nn.silu(x)

def _sigmoid(x):
    return jax.nn.sigmoid(x)

def _layernorm(x, axis=-1, eps=1e-05):
    m = jnp.mean(x, axis=axis, keepdims=True)
    v = jnp.var(x, axis=axis, keepdims=True)
    return (x - m) / jnp.sqrt(v + eps)

def _scatter_add(tgt, idx, src, axis=0):
    return tgt.at[idx].add(src)

def _segment_sum(src, seg, n):
    return jax.ops.segment_sum(src, seg, n)
kernel_name = 'mk_adaln_d2_jaxref_r8_e52c53'

def setup_inputs(seed: int=0):
    np.random.seed(seed)
    _w = jnp.asarray

    def _L0_attn_setup():
        import jax, jax.numpy as jnp
        import numpy as np
        HK, HV, DK, DV, K_CONV, CHUNK = (16, 32, 128, 128, 4, 64)
        DIM = 256
        EPS = 1e-06

        def _l2norm(x):
            return x * jax.lax.rsqrt(jnp.sum(x * x, -1, keepdims=True) + EPS)

        def _chunk_gated_delta_rule(q, k, v, g, beta):
            B, T, H, Dk = q.shape
            Dv = v.shape[-1]
            N = T // CHUNK
            scale = Dk ** (-0.5)

            def to_c(x):
                x = jnp.moveaxis(x, 1, 2)
                x = x.reshape(x.shape[0], x.shape[1], N, CHUNK, *x.shape[3:])
                return jnp.moveaxis(x, 2, 0)
            qc, kc, vc = (to_c(q), to_c(k), to_c(v))
            gc, bc = (to_c(g), to_c(beta))
            G = jnp.cumsum(gc, -1)
            diff = G[..., :, None] - G[..., None, :]
            strict = jnp.tril(jnp.ones((CHUNK, CHUNK), bool), -1)
            incl = jnp.tril(jnp.ones((CHUNK, CHUNK), bool))
            M = jnp.where(strict, bc[..., :, None] * jnp.exp(diff) * jnp.einsum('nbhtd,nbhsd->nbhts', kc, kc), 0.0)
            A = jnp.where(incl, scale * jnp.exp(diff) * jnp.einsum('nbhtd,nbhsd->nbhts', qc, kc), 0.0)
            I = jnp.eye(CHUNK, dtype=q.dtype)
            Tinv = jax.scipy.linalg.solve_triangular(I + M, jnp.broadcast_to(I, M.shape), lower=True)
            u0 = jnp.einsum('nbhts,nbhsd->nbhtd', Tinv, bc[..., None] * vc)
            w = jnp.einsum('nbhts,nbhsd->nbhtd', Tinv, (bc * jnp.exp(G))[..., None] * kc)
            kd = jnp.exp(G[..., -1:] - G)[..., None] * kc
            qd = scale * jnp.exp(G)[..., None] * qc
            gC = G[..., -1]

            def step(S, xs):
                u0_, w_, A_, kd_, qd_, gC_ = xs
                u = u0_ - jnp.einsum('bhcd,bhde->bhce', w_, S)
                o = jnp.einsum('bhts,bhse->bhte', A_, u) + jnp.einsum('bhcd,bhde->bhce', qd_, S)
                S = jnp.exp(gC_)[..., None, None] * S + jnp.einsum('bhcd,bhce->bhde', kd_, u)
                return (S, o)
            S0 = jnp.zeros((B, H, Dk, Dv), q.dtype)
            _, o = jax.lax.scan(step, S0, (u0, w, A, kd, qd, gC))
            o = jnp.moveaxis(o, 0, 2).reshape(B, H, T, Dv)
            return jnp.moveaxis(o, 1, 2)
        key = jax.random.key(seed)
        ks = jax.random.split(key, 8)
        B, T, D = (1, 512, DIM)
        key_dim, value_dim = (HK * DK, HV * DV)
        conv_dim = 2 * key_dim + value_dim
        s = 0.02
        return {'hidden_states': jax.random.normal(ks[0], (B, T, D), jnp.float32), 'W_qkvz': jax.random.normal(ks[1], (D, 2 * key_dim + 2 * value_dim), jnp.float32) * s, 'W_ba': jax.random.normal(ks[2], (D, 2 * HV), jnp.float32) * s, 'conv_w': jax.random.normal(ks[3], (conv_dim, K_CONV), jnp.float32) * 0.1, 'dt_bias': jnp.ones((HV,), jnp.float32), 'A_log': jnp.log(jax.random.uniform(ks[4], (HV,), jnp.float32, 0.001, 16.0)), 'norm_weight': jnp.ones((DV,), jnp.float32), 'W_out': jax.random.normal(ks[5], (value_dim, D), jnp.float32) * s}
    _L0_attn_in = _L0_attn_setup()

    def _L0_ffn_setup():
        import jax, jax.numpy as jnp
        import numpy as np
        DIM = 256
        N_EXPERTS = 8
        TOP_K = 2
        key = jax.random.key(seed)
        ks = jax.random.split(key, 5)
        x = jax.random.normal(ks[0], (4, 512, DIM), dtype=jnp.float32)
        W_up = jax.random.normal(ks[1], (DIM, DIM), dtype=jnp.float32) * (1.0 / np.sqrt(DIM))
        W_down = jax.random.normal(ks[2], (DIM, DIM), dtype=jnp.float32) * (1.0 / np.sqrt(DIM))
        W_gate = jax.random.normal(ks[3], (N_EXPERTS, DIM), dtype=jnp.float32) * (1.0 / np.sqrt(DIM))
        W_expert = jax.random.normal(ks[4], (DIM, DIM), dtype=jnp.float32) * (1.0 / np.sqrt(DIM))
        return {'x': x, 'W_up': W_up, 'W_down': W_down, 'W_gate': W_gate, 'W_expert': W_expert}
    _L0_ffn_in = _L0_ffn_setup()
    _L0_c = _w((lambda *s: np.random.randn(*s).astype(np.float32) * 0.05)(2, 256))
    _L0_wmod = _w((lambda *s: np.random.randn(*s).astype(np.float32) * 0.05)(256, 6 * 256) * 256 ** (-0.5))

    def _L1_attn_setup():
        import jax, jax.numpy as jnp
        import numpy as np
        B, S, HID = (2, 256, 256)
        NH, NG = (32, 8)
        HD = HID // NH
        KV = HD * NG
        key = jax.random.key(seed)
        ks = jax.random.split(key, 9)
        w = lambda k, shp: jax.random.normal(k, shp, dtype=jnp.float32) * 0.02
        return {'hidden_state': jax.random.normal(ks[0], (B, S, HID), dtype=jnp.float32), 'Wq': w(ks[1], (HID, HID)), 'bq': jnp.zeros((HID,), jnp.float32), 'Wk': w(ks[2], (HID, KV)), 'bk': jnp.zeros((KV,), jnp.float32), 'Wv': w(ks[3], (HID, KV)), 'bv': jnp.zeros((KV,), jnp.float32), 'Wo': w(ks[4], (HID, HID)), 'bo': jnp.zeros((HID,), jnp.float32)}
    _L1_attn_in = _L1_attn_setup()

    def _L1_ffn_setup():
        import jax, jax.numpy as jnp
        import numpy as np
        H = 256
        F = 176
        E = 8
        TOPK = 2
        key = jax.random.key(seed)
        ks = jax.random.split(key, 5)
        s = 1.0 / np.sqrt(H)
        hidden_states = jax.random.normal(ks[0], (1, 256, H), dtype=jnp.float32)
        gate_w = jax.random.uniform(ks[1], (H, E), jnp.float32, -s, s)
        w_gate = jax.random.uniform(ks[2], (E, H, F), jnp.float32, -s, s)
        w_up = jax.random.uniform(ks[3], (E, H, F), jnp.float32, -s, s)
        w_down = jax.random.uniform(ks[4], (E, F, H), jnp.float32, -1.0 / np.sqrt(F), 1.0 / np.sqrt(F))
        return {'hidden_states': hidden_states, 'gate_w': gate_w, 'w_gate': w_gate, 'w_up': w_up, 'w_down': w_down}
    _L1_ffn_in = _L1_ffn_setup()
    _L1_c = _w((lambda *s: np.random.randn(*s).astype(np.float32) * 0.05)(2, 256))
    _L1_wmod = _w((lambda *s: np.random.randn(*s).astype(np.float32) * 0.05)(256, 6 * 256) * 256 ** (-0.5))
    _d = {'L0_attn_hidden_states': _L0_attn_in['hidden_states'], 'L0_attn_W_qkvz': _L0_attn_in['W_qkvz'], 'L0_attn_W_ba': _L0_attn_in['W_ba'], 'L0_attn_conv_w': _L0_attn_in['conv_w'], 'L0_attn_dt_bias': _L0_attn_in['dt_bias'], 'L0_attn_A_log': _L0_attn_in['A_log'], 'L0_attn_norm_weight': _L0_attn_in['norm_weight'], 'L0_attn_W_out': _L0_attn_in['W_out'], 'L0_ffn_W_up': _L0_ffn_in['W_up'], 'L0_ffn_W_down': _L0_ffn_in['W_down'], 'L0_ffn_W_gate': _L0_ffn_in['W_gate'], 'L0_ffn_W_expert': _L0_ffn_in['W_expert'], 'L0_c': _L0_c, 'L0_wmod': _L0_wmod, 'L1_attn_Wq': _L1_attn_in['Wq'], 'L1_attn_bq': _L1_attn_in['bq'], 'L1_attn_Wk': _L1_attn_in['Wk'], 'L1_attn_bk': _L1_attn_in['bk'], 'L1_attn_Wv': _L1_attn_in['Wv'], 'L1_attn_bv': _L1_attn_in['bv'], 'L1_attn_Wo': _L1_attn_in['Wo'], 'L1_attn_bo': _L1_attn_in['bo'], 'L1_ffn_gate_w': _L1_ffn_in['gate_w'], 'L1_ffn_w_gate': _L1_ffn_in['w_gate'], 'L1_ffn_w_up': _L1_ffn_in['w_up'], 'L1_ffn_w_down': _L1_ffn_in['w_down'], 'L1_c': _L1_c, 'L1_wmod': _L1_wmod}
    _x0 = _d['L0_attn_hidden_states']
    _d['L0_attn_hidden_states'] = jax.random.normal(jax.random.fold_in(jax.random.key(seed), 1), (2, 1024, 256), dtype=_x0.dtype)
    del _x0
    return _d

def reference(L0_attn_hidden_states, L0_attn_W_qkvz, L0_attn_W_ba, L0_attn_conv_w, L0_attn_dt_bias, L0_attn_A_log, L0_attn_norm_weight, L0_attn_W_out, L0_ffn_W_up, L0_ffn_W_down, L0_ffn_W_gate, L0_ffn_W_expert, L0_c, L0_wmod, L1_attn_Wq, L1_attn_bq, L1_attn_Wk, L1_attn_bk, L1_attn_Wv, L1_attn_bv, L1_attn_Wo, L1_attn_bo, L1_ffn_gate_w, L1_ffn_w_gate, L1_ffn_w_up, L1_ffn_w_down, L1_c, L1_wmod):

    def _L0_attn_ref(hidden_states, W_qkvz, W_ba, conv_w, dt_bias, A_log, norm_weight, W_out):
        import jax, jax.numpy as jnp
        import numpy as np
        HK, HV, DK, DV, K_CONV, CHUNK = (16, 32, 128, 128, 4, 64)
        DIM = 256
        EPS = 1e-06

        def _l2norm(x):
            return x * jax.lax.rsqrt(jnp.sum(x * x, -1, keepdims=True) + EPS)

        def _chunk_gated_delta_rule(q, k, v, g, beta):
            B, T, H, Dk = q.shape
            Dv = v.shape[-1]
            N = T // CHUNK
            scale = Dk ** (-0.5)

            def to_c(x):
                x = jnp.moveaxis(x, 1, 2)
                x = x.reshape(x.shape[0], x.shape[1], N, CHUNK, *x.shape[3:])
                return jnp.moveaxis(x, 2, 0)
            qc, kc, vc = (to_c(q), to_c(k), to_c(v))
            gc, bc = (to_c(g), to_c(beta))
            G = jnp.cumsum(gc, -1)
            diff = G[..., :, None] - G[..., None, :]
            strict = jnp.tril(jnp.ones((CHUNK, CHUNK), bool), -1)
            incl = jnp.tril(jnp.ones((CHUNK, CHUNK), bool))
            M = jnp.where(strict, bc[..., :, None] * jnp.exp(diff) * jnp.einsum('nbhtd,nbhsd->nbhts', kc, kc), 0.0)
            A = jnp.where(incl, scale * jnp.exp(diff) * jnp.einsum('nbhtd,nbhsd->nbhts', qc, kc), 0.0)
            I = jnp.eye(CHUNK, dtype=q.dtype)
            Tinv = jax.scipy.linalg.solve_triangular(I + M, jnp.broadcast_to(I, M.shape), lower=True)
            u0 = jnp.einsum('nbhts,nbhsd->nbhtd', Tinv, bc[..., None] * vc)
            w = jnp.einsum('nbhts,nbhsd->nbhtd', Tinv, (bc * jnp.exp(G))[..., None] * kc)
            kd = jnp.exp(G[..., -1:] - G)[..., None] * kc
            qd = scale * jnp.exp(G)[..., None] * qc
            gC = G[..., -1]

            def step(S, xs):
                u0_, w_, A_, kd_, qd_, gC_ = xs
                u = u0_ - jnp.einsum('bhcd,bhde->bhce', w_, S)
                o = jnp.einsum('bhts,bhse->bhte', A_, u) + jnp.einsum('bhcd,bhde->bhce', qd_, S)
                S = jnp.exp(gC_)[..., None, None] * S + jnp.einsum('bhcd,bhce->bhde', kd_, u)
                return (S, o)
            S0 = jnp.zeros((B, H, Dk, Dv), q.dtype)
            _, o = jax.lax.scan(step, S0, (u0, w, A, kd, qd, gC))
            o = jnp.moveaxis(o, 0, 2).reshape(B, H, T, Dv)
            return jnp.moveaxis(o, 1, 2)
        B, T, D = hidden_states.shape
        ratio = HV // HK
        key_dim = HK * DK
        qkvz = hidden_states @ W_qkvz
        ba = hidden_states @ W_ba
        qkvz = qkvz.reshape(B, T, HK, 2 * DK + 2 * ratio * DV)
        q = qkvz[..., :DK]
        k = qkvz[..., DK:2 * DK]
        v = qkvz[..., 2 * DK:2 * DK + ratio * DV].reshape(B, T, HV, DV)
        z = qkvz[..., 2 * DK + ratio * DV:].reshape(B, T, HV, DV)
        ba = ba.reshape(B, T, HK, 2 * ratio)
        b = ba[..., :ratio].reshape(B, T, HV)
        a = ba[..., ratio:].reshape(B, T, HV)
        mixed = jnp.concatenate([q.reshape(B, T, -1), k.reshape(B, T, -1), v.reshape(B, T, -1)], -1)
        xp = jnp.pad(mixed, ((0, 0), (K_CONV - 1, 0), (0, 0)))
        conv = sum((conv_w[:, j] * xp[:, j:j + T, :] for j in range(K_CONV)))
        mixed = jax.nn.silu(conv)
        q = mixed[..., :key_dim].reshape(B, T, HK, DK)
        k = mixed[..., key_dim:2 * key_dim].reshape(B, T, HK, DK)
        v = mixed[..., 2 * key_dim:].reshape(B, T, HV, DV)
        beta = jax.nn.sigmoid(b)
        g = -jnp.exp(A_log) * jax.nn.softplus(a + dt_bias)
        q = _l2norm(q)
        k = _l2norm(k)
        q = jnp.repeat(q, ratio, axis=2)
        k = jnp.repeat(k, ratio, axis=2)
        o = _chunk_gated_delta_rule(q, k, v, g, beta)
        xg = o * jax.nn.silu(z)
        xg = xg * jax.lax.rsqrt(jnp.mean(xg * xg, -1, keepdims=True) + 1e-06) * norm_weight
        return xg.reshape(B, T, -1) @ W_out

    def _L0_ffn_ref(x, W_up, W_down, W_gate, W_expert):
        import jax, jax.numpy as jnp
        import numpy as np
        DIM = 256
        N_EXPERTS = 8
        TOP_K = 2
        logits = jnp.einsum('bsd,ed->bse', x, W_gate)
        routing_weights, selected_experts = jax.lax.top_k(logits, TOP_K)
        shared_out = jnp.einsum('bsd,od->bso', jax.nn.relu(jnp.einsum('bsd,od->bso', x, W_up)), W_down)
        rw = jax.nn.softmax(routing_weights, axis=-1)
        expert_out = jnp.einsum('bsd,do->bso', x, W_expert)
        moe_out = jnp.sum(rw, axis=-1, keepdims=True) * expert_out
        return shared_out + moe_out

    def _L1_attn_ref(hidden_state, Wq, bq, Wk, bk, Wv, bv, Wo, bo):
        import jax, jax.numpy as jnp
        import numpy as np
        B, S, HID = (2, 256, 256)
        NH, NG = (32, 8)
        HD = HID // NH
        KV = HD * NG
        bs, seq, _ = hidden_state.shape
        rep = NH // NG
        q = hidden_state @ Wq + bq
        k = hidden_state @ Wk + bk
        v = hidden_state @ Wv + bv
        q = q.reshape(bs, seq, NH, HD).transpose(0, 2, 1, 3)
        k = k.reshape(bs, seq, NG, HD).transpose(0, 2, 1, 3)
        v = v.reshape(bs, seq, NG, HD).transpose(0, 2, 1, 3)
        k = jnp.repeat(k, rep, axis=1)
        v = jnp.repeat(v, rep, axis=1)
        scores = jnp.einsum('bhqd,bhkd->bhqk', q, k) / jnp.sqrt(jnp.float32(HD))
        probs = jax.nn.softmax(scores, axis=-1)
        out = jnp.einsum('bhqk,bhkd->bhqd', probs, v)
        out = out.transpose(0, 2, 1, 3).reshape(bs, seq, HID)
        return out @ Wo + bo

    def _L1_ffn_ref(hidden_states, gate_w, w_gate, w_up, w_down):
        import jax, jax.numpy as jnp
        import numpy as np
        H = 256
        F = 176
        E = 8
        TOPK = 2
        b, s, h = hidden_states.shape
        x = hidden_states.reshape(-1, h)
        logits = x @ gate_w
        probs = jax.nn.softmax(logits.astype(jnp.float32), axis=-1)
        topw, sel = jax.lax.top_k(probs, TOPK)
        topw = topw / jnp.sum(topw, axis=-1, keepdims=True)
        topw = topw.astype(hidden_states.dtype)
        combine = jnp.sum(jax.nn.one_hot(sel, E, dtype=topw.dtype) * topw[..., None], axis=1)
        g = jnp.einsum('th,ehf->etf', x, w_gate)
        u = jnp.einsum('th,ehf->etf', x, w_up)
        a = jax.nn.silu(g) * u
        y = jnp.einsum('etf,efh->eth', a, w_down)
        out = jnp.einsum('eth,te->th', y, combine)
        return out.reshape(b, s, h)
    x = L0_attn_hidden_states
    mod = (_silu(L0_c) @ L0_wmod).reshape(L0_c.shape[0], 6, 1, -1)
    sa, ca, ga, sb, cb, gb = (mod[:, 0], mod[:, 1], mod[:, 2], mod[:, 3], mod[:, 4], mod[:, 5])
    ga = (2 * (ga >= 0) - 1) * jnp.maximum(jnp.abs(ga), 0.25)
    gb = (2 * (gb >= 0) - 1) * jnp.maximum(jnp.abs(gb), 0.25)
    h = _layernorm(x, axis=-1) * (1 + ca) + sa
    x = x + ga * _L0_attn_ref(h, L0_attn_W_qkvz, L0_attn_W_ba, L0_attn_conv_w, L0_attn_dt_bias, L0_attn_A_log, L0_attn_norm_weight, L0_attn_W_out)
    h = _layernorm(x, axis=-1) * (1 + cb) + sb
    x = x + gb * _L0_ffn_ref(h, L0_ffn_W_up, L0_ffn_W_down, L0_ffn_W_gate, L0_ffn_W_expert)
    mod = (_silu(L1_c) @ L1_wmod).reshape(L1_c.shape[0], 6, 1, -1)
    sa, ca, ga, sb, cb, gb = (mod[:, 0], mod[:, 1], mod[:, 2], mod[:, 3], mod[:, 4], mod[:, 5])
    ga = (2 * (ga >= 0) - 1) * jnp.maximum(jnp.abs(ga), 0.25)
    gb = (2 * (gb >= 0) - 1) * jnp.maximum(jnp.abs(gb), 0.25)
    h = _layernorm(x, axis=-1) * (1 + ca) + sa
    x = x + ga * _L1_attn_ref(h, L1_attn_Wq, L1_attn_bq, L1_attn_Wk, L1_attn_bk, L1_attn_Wv, L1_attn_bv, L1_attn_Wo, L1_attn_bo)
    h = _layernorm(x, axis=-1) * (1 + cb) + sb
    x = x + gb * _L1_ffn_ref(h, L1_ffn_gate_w, L1_ffn_w_gate, L1_ffn_w_up, L1_ffn_w_down)
    return x

_drawn_inputs = setup_inputs


def setup_inputs(seed=0):
    import zlib

    import numpy as np

    out = dict(_drawn_inputs(seed))
    spreads = {'L0_attn_dt_bias': (1.0, 0.6),
     'L0_attn_norm_weight': (1.0, 0.6),
     'L1_attn_bq': (0.0, 0.8),
     'L1_attn_bk': (0.0, 0.8),
     'L1_attn_bv': (0.0, 0.8),
     'L1_attn_bo': (0.0, 0.346)}
    factors = {'L0_attn_W_qkvz': 8.0,
     'L0_attn_W_ba': 8.0,
     'L0_attn_conv_w': 8.0,
     'L0_attn_A_log': 8.0,
     'L0_attn_W_out': 8.0,
     'L0_ffn_W_gate': 8.0,
     'L1_attn_Wq': 8.0,
     'L1_attn_Wk': 8.0,
     'L1_attn_Wv': 8.0,
     'L1_attn_Wo': 7.226,
     'L1_ffn_gate_w': 3.605,
     'L1_ffn_w_gate': 3.239,
     'L1_ffn_w_up': 3.134,
     'L1_ffn_w_down': 3.13}
    for name, (base, spread) in spreads.items():
        noise = np.random.default_rng([zlib.crc32(name.encode()), seed]).standard_normal(out[name].shape)
        drawn = base * np.exp(spread * noise) if base else spread * noise
        out[name] = jnp.asarray(drawn.astype(out[name].dtype))
    for name, factor in factors.items():
        out[name] = (out[name] * factor).astype(out[name].dtype)
    return out
```

```python
from contextlib import ExitStack

import numpy as np
import concourse.bass as bass
from concourse import mybir

F32 = mybir.dt.float32
BF16 = mybir.dt.bfloat16
I32 = mybir.dt.int32
U32 = mybir.dt.uint32
ALU = mybir.AluOpType
ACT = mybir.ActivationFunctionType
AX = mybir.AxisListType

P = 128
DIM = 256
KT = DIM // P
B = 2
T = 1024
CH = T // P
HK = 16
RATIO = 2
STEPS = HK * CH
M = B * RATIO
LEVELS = 7
WCOL = 768
QKV = 512
LN_EPS = 1e-5
EPS = 1e-6


def half(x, level, second):
    s = 1 << level
    return x.rearrange("p (q two s) -> p q two s", two=2, s=s)[:, :, int(second), :]


class Shared:
    pass


def wait_apart(eng, sh, s, value):
    eng.wait_ge(s, value)
    eng.sem_inc(sh.apart, 1)


def setup_phase(nc, A, sh, sem):
    with ExitStack() as ctx:
        def sb(name, shape, dt=F32):
            return ctx.enter_context(nc.sbuf_tensor(name, shape, dt))

        wmod = sb("wmod", [P, 2, KT, 6 * DIM])
        c_t = sb("c_t", [P, 2, KT, B])
        c_exp = sb("c_exp", [P, 2 * KT * B])
        c_silu = sb("c_silu", [P, 2, KT, B])
        c_rep = sb("c_rep", [P, 2, KT, B, P])
        sign = sb("sign", [P, 2 * 2 * B * DIM])
        mag = sb("mag", [P, 2 * 2 * B * DIM])
        psum = [ctx.enter_context(nc.psum_tensor(f"mod_ps{k}", [P, 512], F32)) for k in range(5)]
        loaded, c_e, c_s, c_r, mods, gates_ps, gates_sb, done, sgn = (
            sem(n) for n in ("set_loaded", "set_cexp", "set_csilu", "set_crep", "set_mods", "set_gps",
                             "set_gsb", "set_done", "set_sign"))
        block = ctx.enter_context(nc.Block())
        count = [0]

        @block.sync
        def _(sp):
            loads = [
                (c_t[:, 0], A["c0"]), (c_t[:, 1], A["c1"]),
                (wmod[:, 0], A["L0_wmod"].rearrange("(k p) n -> p k n", p=P)),
                (wmod[:, 1], A["L1_wmod"].rearrange("(k p) n -> p k n", p=P)),
                (sh.masks[:], A["masks"]), (sh.level_masks[:], A["level_masks"]),
            ] + [(sh.x[:, :, b], A["L0_attn_hidden_states"][b].rearrange("(c p) d -> p c d", p=P)) for b in range(B)]
            for dst, src in loads:
                sp.dma_start(dst, src).then_inc(loaded, 16)
                count[0] += 16

        n_loaded = 16 * 8

        @block.scalar
        def _(act):
            act.wait_ge(loaded, n_loaded)
            act.activation(c_exp[:], c_t[:].rearrange("p l k b -> p (l k b)"), ACT.Exp, scale=-1.0).then_inc(c_e, 1)

        @block.tensor
        def _(pe):
            pe.wait_ge(loaded, n_loaded)
            pe.wait_ge(c_r, 1)
            for layer in range(2):
                for ct in range(12):
                    for k in range(KT):
                        mm = pe.matmul(psum[0][:, layer * 24 + ct * 2:layer * 24 + ct * 2 + 2],
                                       wmod[:, layer, k, ct * P:(ct + 1) * P], c_silu[:, layer, k, :],
                                       start=(k == 0), stop=(k == KT - 1))
            mm.then_inc(mods, 1)
            for layer in range(2):
                for g, part in enumerate((2, 5)):
                    for b in range(B):
                        for k in range(KT):
                            mm = pe.matmul(psum[1 + layer * 2 + g][:, b * DIM:(b + 1) * DIM], c_rep[:, layer, k, b, :],
                                           wmod[:, layer, k, part * DIM:(part + 1) * DIM],
                                           start=(k == 0), stop=(k == KT - 1))
            mm.then_inc(gates_ps, 1)

        @block.vector
        def _(dve):
            dve.wait_ge(c_e, 1)
            flat = c_t[:].rearrange("p l k b -> p (l k b)")
            dve.tensor_scalar(c_exp[:], c_exp[:], 1.0, None, ALU.add).then_inc(c_s, 1)
            dve.wait_ge(c_s, 1)
            dve.reciprocal(c_exp[:], c_exp[:]).then_inc(c_s, 1)
            dve.wait_ge(c_s, 2)
            dve.tensor_tensor(c_silu[:].rearrange("p l k b -> p (l k b)"), flat, c_exp[:], ALU.mult).then_inc(c_s, 1)
            dve.wait_ge(c_s, 3)
            for layer in range(2):
                for k in range(KT):
                    rep = dve.tensor_copy(c_rep[:, layer, k], c_silu[:, layer, k, :].unsqueeze(2).to_broadcast([P, B, P]))
            rep.then_inc(c_r, 1)
            dve.wait_ge(mods, 1)
            dve.tensor_copy(sh.mod[:], psum[0][:, 0:48].rearrange("p (l s k b) -> p l s k b", l=2, s=6, k=KT)).then_inc(done, 1)
            dve.wait_ge(done, 1)
            for layer in range(2):
                for s in (1, 4):
                    dve.tensor_scalar(sh.mod[:, layer, s], sh.mod[:, layer, s], 1.0, None, ALU.add).then_inc(done, 1)
            dve.wait_ge(gates_ps, 1)
            for n in range(4):
                part = slice(n * 512, (n + 1) * 512)
                dve.tensor_scalar(sign[:, part], psum[1 + n][:], 0.0, 2.0, ALU.is_ge, ALU.mult).then_inc(sgn, 1)
                dve.tensor_copy(mag[:, part], psum[1 + n][:]).then_inc(sgn, 1)
                dve.wait_ge(sgn, 4 * n + 2)
                dve.scalar_tensor_tensor(mag[:, part], mag[:, part], -1.0, mag[:, part], ALU.mult, ALU.max).then_inc(sgn, 1)
                dve.wait_ge(sgn, 4 * n + 3)
                dve.tensor_scalar(mag[:, part], mag[:, part], 0.25, None, ALU.max).then_inc(sgn, 1)
                dve.wait_ge(sgn, 4 * n + 4)
                dve.scalar_tensor_tensor(sh.gate[:].rearrange("p l g b d -> p (l g b d)")[:, part], sign[:, part], -1.0,
                                         mag[:, part], ALU.add, ALU.mult).then_inc(done, 1)
            dve.memset(sh.pw[:, 0:1], -0.5).then_inc(done, 1)
            dve.memset(sh.pw[:, 1:2], LN_EPS).then_inc(done, 1)
            dve.memset(sh.pw[:, 2:3], 4 * EPS).then_inc(done, 1)
            dve.memset(sh.pw[:, 3:4], 4 * EPS * P).then_inc(done, 1)
            dve.wait_ge(done, 13)
            dve.drain()


def ln_phase(nc, A, sh, sem):
    with ExitStack() as ctx:
        def sb(name, shape, dt=F32):
            return ctx.enter_context(nc.sbuf_tensor(name, shape, dt))

        w_ba = sb("w_ba", [P, KT, 4 * HK])
        ba = sb("ba", [P, HK, CH, B, 2, RATIO])
        alog = sb("a_log_sb", [P, HK, RATIO])
        dtb = sb("dt_bias_sb", [P, HK, RATIO])
        stats = [sb(f"ln_stats{b}", [P, 6]) for b in range(B)]
        mean_var = [sb(f"ln_mv{b}", [P, 2]) for b in range(B)]
        rstd = [sb(f"ln_rstd{b}", [P, 1]) for b in range(B)]
        normed = [sb(f"ln_normed{b}", [P, DIM]) for b in range(B)]
        h_tile = [sb(f"ln_htile{b}", [P, KT, P]) for b in range(B)]
        NG = STEPS * M
        work = [sb(f"gate_work{k}", [P, NG]) for k in range(4)]
        g_flat = sb("g_flat", [P, NG])
        tr_ps = [ctx.enter_context(nc.psum_tensor(f"ln_tr{b}", [P, 512], F32)) for b in range(B)]
        ba_ps = [ctx.enter_context(nc.psum_tensor(f"ln_ba{b}", [P, 512], F32)) for b in range(B)]
        cum_ps = [ctx.enter_context(nc.psum_tensor(f"cum_ps{k}", [P, 512], F32)) for k in range(3)]
        (loaded, st, mv, veps, rs, nm, tr, ht, ba_mm, ba_sb, neg, vec, cum, ex) = (
            sem(n) for n in ("ln_loaded", "ln_st", "ln_mvs", "ln_veps", "ln_rs", "ln_nm", "ln_trs", "ln_ht",
                             "ln_bamm", "ln_basb", "gt_neg", "gt_vec", "gt_cum", "gt_exp"))
        h_out = [sem(f"ln_hout{b}") for b in range(B)]
        ident = sh.masks[:, 0:P]
        block = ctx.enter_context(nc.Block())

        @block.sync
        def _(sp):
            sp.dma_start(w_ba[:], A["L0_attn_W_ba"].rearrange("(k p) n -> p k n", p=P)).then_inc(loaded, 16)
            sp.dma_start(alog[:].rearrange("p a b -> p (a b)"), A["alog"].to_broadcast([P, 2 * HK])).then_inc(loaded, 16)
            sp.dma_start(dtb[:].rearrange("p a b -> p (a b)"), A["dtb"].to_broadcast([P, 2 * HK])).then_inc(loaded, 16)
            with sp.Fori(0, CH) as c:
                for b in range(B):
                    sp.wait_ge(ht, c * 4 + 2 * b + 2)
                    sp.dma_start(sh.h[:, :, bass.ds((c * B + b) * P, P)], h_tile[b][:]).then_inc(h_out[b], 16)
            for b in range(B):
                sp.wait_ge(h_out[b], 16 * CH)

        @block.vector
        def _(dve):
            with dve.Fori(0, CH) as c:
                for b in range(B):
                    n = c * B + b
                    xt = sh.x[:, bass.ds(c, 1), b, :]
                    dve.bn_stats(stats[b][:], xt).then_inc(st, 1)
                    wait_apart(dve, sh, st, n + 1)
                    dve.bn_aggr(mean_var[b][:], stats[b][:]).then_inc(mv, 1)
                for b in range(B):
                    n = c * B + b
                    xt = sh.x[:, bass.ds(c, 1), b, :]
                    dve.wait_ge(rs, n + 1)
                    dve.tensor_scalar(normed[b][:], xt, mean_var[b][:, 0:1], rstd[b][:],
                                      ALU.subtract, ALU.mult).then_inc(nm, 1)
                for b in range(B):
                    n = c * B + b
                    dve.wait_ge(tr, n + 1)
                    dve.wait_ge(h_out[b], c * 16)
                    dve.wait_ge(ba_mm, n - b)
                    for k in range(KT):
                        dve.tensor_scalar(h_tile[b][:, k, :], tr_ps[b][:, k * P:(k + 1) * P], sh.mod[:, 0, 1, k, b:b + 1],
                                          sh.mod[:, 0, 0, k, b:b + 1], ALU.mult, ALU.add).then_inc(ht, 1)
            dve.wait_ge(ba_sb, CH * B)
            dve.wait_ge(loaded, 48)
            bv = ba[:, :, :, :, 0, :].rearrange("p h c b r -> p (h c b) r")
            G = sh.gates[:].rearrange("p s q m -> p s (q m)")
            k = [0]

            def link(ins):
                k[0] += 1
                ins.then_inc(vec, 1)
                dve.wait_ge(vec, k[0])

            w0, w1, w2, w3 = (w[:] for w in work)
            hbr = lambda w: w.rearrange("p (h q r) -> p h q r", h=HK, r=RATIO)
            dve.wait_ge(neg, 1)
            link(dve.tensor_scalar(w0, w0, 1.0, None, ALU.add))
            link(dve.reciprocal(w0, w0))
            link(dve.tensor_scalar(G[:, :, 0:4], w0.rearrange("p (s m) -> p s m", m=M), 0.5, None, ALU.mult))
            for kh in range(HK):
                ins = dve.tensor_tensor(hbr(w1)[:, kh], ba[:, kh, :, :, 1, :].rearrange("p c b r -> p (c b) r"),
                                        dtb[:, kh:kh + 1, :].to_broadcast([P, CH * B, RATIO]), ALU.add)
            link(ins)
            link(dve.scalar_tensor_tensor(w2, w1, -1.0, w1, ALU.mult, ALU.min))
            dve.wait_ge(neg, 2)
            link(dve.tensor_scalar(w3, w2, 2.0, None, ALU.add))
            link(dve.reciprocal(w3, w3))
            link(dve.tensor_tensor(w3, w3, w2, ALU.mult))
            link(dve.tensor_tensor(w2, w3, w3, ALU.mult))
            link(dve.tensor_scalar(w0, w2, 1.0 / 19, 1.0 / 17, ALU.mult, ALU.add))
            for d in (15, 13, 11, 9, 7, 5, 3, 1):
                link(dve.tensor_tensor(w0, w0, w2, ALU.mult))
                link(dve.tensor_scalar(w0, w0, 1.0 / d, None, ALU.add))
            link(dve.tensor_tensor(w0, w0, w3, ALU.mult))
            link(dve.tensor_scalar(w1, w1, 0.0, None, ALU.max))
            link(dve.scalar_tensor_tensor(w0, w0, 2.0, w1, ALU.mult, ALU.add))
            for kh in range(HK):
                ins = dve.scalar_tensor_tensor(hbr(g_flat[:])[:, kh], hbr(w0)[:, kh], -1.0,
                                               alog[:, kh:kh + 1, :].to_broadcast([P, CH * B, RATIO]), ALU.mult, ALU.mult)
            link(ins)
            link(dve.tensor_copy(G[:, :, 4:8], g_flat[:].rearrange("p (s m) -> p s m", m=M)))
            dve.wait_ge(ex, 3)
            e = lambda w: w.rearrange("p (s m) -> p s m", m=M)
            link(dve.tensor_scalar(G[:, :, 8:12], e(w1), -2.0, None, ALU.mult))
            link(dve.tensor_scalar(G[:, :, 12:16], e(w1), float(P) ** -0.5, None, ALU.mult))
            link(dve.tensor_copy(G[:, :, 16:20], e(w2)))
            link(dve.tensor_copy(G[:, :, 20:24], e(w3)))
            link(dve.memset(sh.gates[:].rearrange("p (h c) q m -> p h c (q m)", c=CH)[:, :, CH - 1, 16:24], 0.0))

        @block.gpsimd
        def _(pool):
            with pool.Fori(0, CH) as c:
                for b in range(B):
                    n = c * B + b
                    pool.wait_ge(mv, n + 1)
                    pool.tensor_tensor(rstd[b][:], mean_var[b][:, 1:2], sh.pw[:, 1:2], ALU.add).then_inc(veps, 1)
                    pool.wait_ge(veps, n + 1)
                    pool.tensor_tensor(rstd[b][:], rstd[b][:], sh.pw[:, 0:1], ALU.pow).then_inc(rs, 1)

        @block.tensor
        def _(pe):
            pe.wait_ge(loaded, 48)
            with pe.Fori(0, CH) as c:
                for b in range(B):
                    n = c * B + b
                    pe.wait_ge(nm, n + 1)
                    pe.wait_ge(ht, c * 4)
                    for k in range(KT):
                        mm = pe.transpose(tr_ps[b][:, k * P:(k + 1) * P], normed[b][:, k * P:(k + 1) * P], ident)
                    mm.then_inc(tr, 1)
                for b in range(B):
                    n = c * B + b
                    pe.wait_ge(ht, c * 4 + 2 * b + 2)
                    pe.wait_ge(ba_sb, n - b)
                    for k in range(KT):
                        mm = pe.matmul(ba_ps[b][:, 0:4 * HK], h_tile[b][:, k, :], w_ba[:, k, :],
                                       start=(k == 0), stop=(k == KT - 1))
                    mm.then_inc(ba_mm, 1)
            pe.wait_ge(vec, 30)
            for k, lhs in enumerate((sh.masks[:, 3 * P:4 * P], sh.masks[:, 4 * P:5 * P], sh.masks[:, 5 * P:6 * P])):
                pe.matmul(cum_ps[k][:], lhs, g_flat[:], start=True, stop=True).then_inc(cum, 1)

        @block.scalar
        def _(act):
            with act.Fori(0, CH) as c:
                for b in range(B):
                    act.wait_ge(ba_mm, c * B + b + 1)
                    act.activation(ba[:].rearrange("p h c b q r -> p h c b (q r)")[:, :, bass.ds(c, 1), b, :],
                                   ba_ps[b][:, 0:4 * HK].rearrange("p (h q) -> p h q", h=HK).unsqueeze(2),
                                   ACT.Copy).then_inc(ba_sb, 1)
            act.wait_ge(ba_sb, CH * B)
            act.activation(work[0][:].rearrange("p (s r) -> p s r", r=RATIO),
                           ba[:, :, :, :, 0, :].rearrange("p h c b r -> p (h c b) r"), ACT.Exp, scale=-1.0).then_inc(neg, 1)
            act.wait_ge(loaded, 48)
            act.wait_ge(vec, 5)
            act.activation(work[2][:], work[2][:], ACT.Exp)
            act.activation(alog[:], alog[:], ACT.Exp).then_inc(neg, 1)
            act.wait_ge(vec, 30)
            for k in range(3):
                act.wait_ge(cum, k + 1)
                act.activation(work[1 + k][:], cum_ps[k][:], ACT.Exp).then_inc(ex, 1)


def delta_phase(nc, A, sh, sem):
    with ExitStack() as ctx:
        def sb(name, shape, dt=F32):
            return ctx.enter_context(nc.sbuf_tensor(name, shape, dt))

        raw = sb("raw", [P, 4, B, T + 3])
        w_qkv = sb("w_qkv", [P, KT, QKV])
        w_z = sb("w_z", [P, KT, RATIO * P])
        w_out = sb("w_out", [P, 2, RATIO * DIM])
        norm_w = sb("norm_w_sb", [P, 1])
        h_in = [sb(f"h_in{p}", [P, KT, B, P]) for p in range(2)]
        gate = [sb(f"gate_in{p}", [P, 6, B, RATIO]) for p in range(2)]
        taps = [sb(f"taps{p}", [P, 4, 4]) for p in range(2)]
        conv = sb("conv", [P, 4, B, P])
        conv_tanh_sb = sb("conv_tanh_sb", [P, 4, B, P])
        qkv = [sb(f"qkv{p}", [P, 4, B, P]) for p in range(2)]
        squares = sb("squares", [P, 2, B, P])
        rnorm = [sb(f"rnorm{p}", [P, 2, B]) for p in range(2)]
        beta_r = [sb(f"beta_r{p}", [P, B, RATIO]) for p in range(2)]
        beta_r2 = [sb(f"beta_r2{p}", [P, B, RATIO]) for p in range(2)]
        ks_scale = [sb(f"ks_scale{p}", [P, B, RATIO]) for p in range(2)]
        qs_scale = [sb(f"qs_scale{p}", [P, B, RATIO]) for p in range(2)]
        g_below = sb("g_below", [P, M, P])
        decay = sb("decay", [P, M, P])
        kkq = sb("kkq", [P, 2, B, P])
        m_neg = sb("m_neg", [P, M, P])
        a_t = [sb(f"a_t{p}", [P, B, RATIO, P]) for p in range(2)]
        z_neg = [sb(f"z_neg{l}", [P, M * P]) for l in range(LEVELS)]
        r_inv = sb("r_inv", [P, M * P])
        t_inv = sb("t_inv", [P, M * P])
        k_norms = sb("k_norms", [P, B * P + 2 * B])
        k_tok = k_norms[:, 0:B * P].rearrange("p (b d) -> p b d", b=B)
        norms = k_norms[:, B * P:]
        k_dec = [sb(f"k_dec{p}", [P, B, RATIO, P]) for p in range(2)]
        v_beta = sb("v_beta", [P, M, P])
        rhs = sb("rhs", [P, M, P])
        u = sb("u", [P, M, P])
        qs = sb("qs", [P, M, P])
        state = sb("state", [P, B, RATIO, P])
        o = sb("o", [P, M, P])
        z_tanh = sb("z_tanh", [P, M * P])
        z_silu = [sb(f"z_silu{p}", [P, M * P]) for p in range(2)]
        gated = sb("gated", [P, M * P])
        gated_sq = sb("gated_sq", [P, M, P])
        o_norm = sb("o_norm", [P, M])
        o_rnorm = sb("o_rnorm", [P, M])
        scaled = sb("scaled", [P, M, P])
        o_t = sb("o_t", [P, M, P])
        bank = [ctx.enter_context(nc.psum_tensor(f"bank{k}", [P, 512], F32)) for k in range(8)]
        y = sh.y

        ident = sh.masks[:, 0:P]
        below = sh.masks[:, 3 * P + P:5 * P]
        upto = sh.masks[:, 3 * P:4 * P]
        kkq_mask = sh.masks[:, P:3 * P].rearrange("p (a n) -> p a n", a=2)
        ones = sh.masks[:, 5 * P:5 * P + 1]

        ld_const, ld_wqkv, ld_wz, ld_wout = (sem(n) for n in ("ld_const", "ld_wqkv", "ld_wz", "ld_wout"))
        ld_h, ld_taps, ld_gate = ([sem(f"{n}{p}") for p in range(2)] for n in ("ld_h", "ld_taps", "ld_gate"))
        (pe_proj, pe_z, pe_kkq, pe_dd, pe_v, pe_k, pe_dt, pe_lev, pe_inv, pe_ks, pe_qs, pe_u, pe_s, pe_o, pe_xt,
         pe_y) = (sem(n) for n in ("pe_proj", "pe_z", "pe_kkq", "pe_dd", "pe_v", "pe_k", "pe_dt", "pe_lev", "pe_inv",
                                   "pe_ks", "pe_qs", "pe_u", "pe_s", "pe_o", "pe_xt", "pe_y"))
        (act_raw, act_conv, act_dec, act_k, act_inv, act_r, act_u, act_z, act_xt) = (
            sem(n) for n in ("act_raw", "act_conv", "act_dec", "act_k", "act_inv", "act_r", "act_u", "act_z", "act_xt"))
        (dve_conv, dve_qkv, dve_kkq, dve_m, dve_v, dve_a, dve_z, dve_rhs, dve_qs, dve_s, dve_o, dve_zs,
         dve_red, dve_y, dve_init) = (
            sem(n) for n in ("dve_conv", "dve_qkv", "dve_kkq", "dve_m", "dve_v", "dve_a", "dve_z", "dve_rhs",
                             "dve_qs", "dve_s", "dve_o", "dve_zs", "dve_red", "dve_y", "dve_init"))
        (pl_sq, pl_rn, pl_sc, pl_g, pl_r, pl_kd, pl_gt, pl_gsq, pl_on, pl_x) = (
            sem(n) for n in ("pl_sq", "pl_rn", "pl_sc", "pl_g", "pl_r", "pl_kd", "pl_gt", "pl_gsq", "pl_on", "pl_x"))
        block = ctx.enter_context(nc.Block())

        def turns(eng, body):
            body(0, 0, True, True, False)
            with eng.Fori(0, (STEPS - 2) // 2) as j:
                body(j * 2 + 1, 1, True, True, True)
                body(j * 2 + 2, 0, True, True, True)
            body(STEPS - 1, 1, False, True, True)
            body(STEPS, 0, False, False, True)

        @block.sync
        def _(sp):
            sp.dma_start(norm_w[:], A["norm_w"]).then_inc(ld_const, 16)

            def chunk(step, kh, c, p, first):
                if not first:
                    sp.wait_ge(pe_z, step - 1)
                sp.dma_start(h_in[p][:], sh.h[:, :, bass.ds(c * (B * P), B * P)].rearrange("p k (b t) -> p k b t", b=B)).then_inc(ld_h[p], 16)
                if not first:
                    sp.wait_ge(dve_conv, (step - 1) * 16)
                sp.dma_start(taps[p][:].rearrange("p a b -> p (a b)"), A["conv_w"][:, bass.ds(kh * 16, 16)]).then_inc(ld_taps[p], 16)
                if not first:
                    sp.wait_ge(dve_s, step - 1)
                    sp.wait_ge(pl_kd, step - 1)
                sp.dma_start(gate[p][:].rearrange("p q b r -> p (q b r)"),
                             sh.gates[:, bass.ds(step, 1)].rearrange("p s q m -> p (s q m)")).then_inc(ld_gate[p], 16)

            def weights(kh, first):
                src = A["L0_attn_W_qkvz"].rearrange("(k p) n -> p k n", p=P)
                if not first:
                    sp.wait_ge(pe_proj, 4 * CH * kh)
                sp.dma_start(w_qkv[:], src[:, :, bass.ds(kh * WCOL, QKV)]).then_inc(ld_wqkv, 16)

            def weights_z(kh, first):
                src = A["L0_attn_W_qkvz"].rearrange("(k p) n -> p k n", p=P)
                if not first:
                    sp.wait_ge(pe_z, CH * kh)
                sp.dma_start(w_z[:], src[:, :, bass.ds(kh * WCOL + QKV, RATIO * P)]).then_inc(ld_wz, 16)

            def weights_out(kh, first):
                src = A["L0_attn_W_out"].rearrange("(h r e) n -> e h r n", e=P, r=RATIO)
                if not first:
                    sp.wait_ge(pe_y, CH * (kh - 1))
                sp.dma_start(w_out[:, bass.ds(kh % 2, 1)].rearrange("p a (r n) -> p (a r) n", r=RATIO),
                             src[:, bass.ds(kh, 1)].rearrange("p a r n -> p (a r) n")).then_inc(ld_wout, 16)

            weights(0, True)
            weights_z(0, True)
            weights_out(0, True)
            for c in range(CH):
                chunk(c, 0, c, c % 2, c < 2)
            with sp.Fori(1, HK) as kh:
                weights(kh, False)
                chunk(kh * CH, kh, 0, 0, False)
                weights_z(kh, False)
                weights_out(kh, False)
                with sp.Fori(0, CH // 2 - 1) as cc:
                    chunk(kh * CH + cc * 2 + 1, kh, cc * 2 + 1, 1, False)
                    chunk(kh * CH + cc * 2 + 2, kh, cc * 2 + 2, 0, False)
                chunk(kh * CH + CH - 1, kh, CH - 1, 1, False)

        @block.tensor
        def _(pe):
            def project(i, p, ct, reader):
                j = ct // 2
                if ct == 0:
                    pe.wait_ge(ld_h[p], 16 * (i // 2 + 1))
                    pe.wait_ge(ld_wqkv, wq_count(i))
                if ct % 2 == 0:
                    reader()
                out = bank[j][:, (ct % 2) * B * P:(ct % 2 + 1) * B * P]
                for k in range(KT):
                    mm = pe.matmul(out, w_qkv[:, k, ct * P:(ct + 1) * P], h_in[p][:, k].rearrange("p b t -> p (b t)"),
                                   start=(k == 0), stop=(k == KT - 1))
                mm.then_inc(pe_proj, 1)

            def wq_count(i):
                return 16 * (i // CH + 1)

            def body(i, p, nxt, cur, prev):
                q = 1 - p
                zq = z_neg

                def level(l):
                    pe.wait_ge(act_r, 6 * i + l - 1) if l > 1 else None
                    if l == 2:
                        pe.wait_ge(pl_r, i + 1)
                    src = z_neg[0] if l == 1 else r_inv
                    pe.wait_ge(dve_z, LEVELS * i + l)
                    for m in range(M):
                        mm = pe.matmul(bank[6][:, m * 64:(m + 1) * 64], m_neg[:, m, :],
                                       half(src[:, m * P:(m + 1) * P], l, True), start=True, stop=True)
                    mm.then_inc(pe_lev, 1)

                def grow(l):
                    pe.wait_ge(act_inv, 6 * i + l)
                    pe.wait_ge(dve_z, LEVELS * i + l + 1)
                    for m in range(M):
                        mm = pe.matmul(bank[7][:, m * 64:(m + 1) * 64], t_inv[:, m * P:(m + 1) * P],
                                       half(z_neg[l][:, m * P:(m + 1) * P], l, True), start=True, stop=True)
                    if l < LEVELS - 1:
                        for m in range(M):
                            mm = pe.matmul(bank[7][:, 256 + m * 64:256 + (m + 1) * 64], z_neg[l][:, m * P:(m + 1) * P],
                                           half(t_inv[:, m * P:(m + 1) * P], l, False), start=True, stop=True)
                    mm.then_inc(pe_inv, 1)

                kt = lambda pp, b: qkv[pp][:, 1, b, :]
                qt = lambda pp, b: qkv[pp][:, 0, b, :]
                if not prev:
                    pe.wait_ge(ld_const, 16)
                    for ct in range(4):
                        project(0, 0, ct, lambda: None)
                if cur:
                    pe.wait_ge(dve_qkv, 2 * i + 1)
                    if prev:
                        pe.wait_ge(dve_o, i - 1)
                    for b in range(B):
                        pe.matmul(bank[5][:, b * P:(b + 1) * P], kt(p, b), kt(p, b), start=True, stop=True)
                    for b in range(B):
                        mm = pe.matmul(bank[5][:, (B + b) * P:(B + b + 1) * P], kt(p, b), qt(p, b), start=True, stop=True)
                    mm.then_inc(pe_kkq, 1)
                    pe.wait_ge(pl_g, i + 1)
                    pe.wait_ge(act_r, 6 * i) if prev else None
                    pe.matmul(bank[7][:], upto, g_below[:].rearrange("p m s -> p (m s)"), start=True, stop=True).then_inc(pe_dd, 1)
                    if prev:
                        pe.wait_ge(dve_s, i - 1)
                    for b in range(B):
                        pe.transpose(bank[4][:, b * P:(b + 1) * P], kt(p, b), ident)
                    pe.wait_ge(pl_sq, i + 1)
                    for a in range(2):
                        for b in range(B):
                            mm = pe.matmul(bank[4][:, 256 + a * B + b:257 + a * B + b], squares[:, a, b, :], ones,
                                           start=True, stop=True)
                    mm.then_inc(pe_k, 1)
                if prev:
                    pe.wait_ge(dve_s, i - 1)
                    if cur:
                        pe.wait_ge(act_raw, 2 * i + 1)
                    for b in range(B):
                        mm = pe.matmul(bank[0][:, b * 256:(b + 1) * 256], kt(q, b), state[:, b].rearrange("p r e -> p (r e)"),
                                       start=True, stop=True)
                    mm.then_inc(pe_ks, 1)
                    if cur:
                        pe.wait_ge(act_raw, 2 * i + 2)
                    for b in range(B):
                        mm = pe.matmul(bank[1][:, b * 256:(b + 1) * 256], qt(q, b), state[:, b].rearrange("p r e -> p (r e)"),
                                       start=True, stop=True)
                    mm.then_inc(pe_qs, 1)
                if cur:
                    pe.wait_ge(act_dec, i + 1)
                    pe.wait_ge(dve_kkq, i + 1)
                    for m in range(M):
                        mm = pe.transpose(bank[5][:, m * P:(m + 1) * P], decay[:, m, :], ident)
                    mm.then_inc(pe_dt, 1)
                    pe.wait_ge(dve_m, i + 1)
                    for m in range(M):
                        mm = pe.transpose(bank[6][:, m * P:(m + 1) * P], m_neg[:, m, :], ident)
                    mm.then_inc(pe_lev, 1)
                    pe.wait_ge(dve_qkv, 2 * i + 2)
                    if prev:
                        pe.wait_ge(dve_y, i - 1)
                    for m in range(M):
                        mm = pe.transpose(bank[3][:, m * P:(m + 1) * P], qkv[p][:, 2 + m % RATIO, m // RATIO, :], ident)
                    mm.then_inc(pe_v, 1)
                if cur:
                    pe.wait_ge(dve_z, LEVELS * i + 1)
                    for m in range(M):
                        mm = pe.transpose(bank[7][:, m * P:(m + 1) * P], z_neg[0][:, m * P:(m + 1) * P], ident)
                    mm.then_inc(pe_inv, 1)
                if prev:
                    pe.wait_ge(dve_rhs, i)
                    if cur:
                        pe.wait_ge(dve_v, i + 1)
                    else:
                        pe.wait_ge(act_r, 6 * i)
                    for m in range(M):
                        mm = pe.matmul(bank[3][:, m * P:(m + 1) * P], r_inv[:, m * P:(m + 1) * P],
                                       rhs[:, m, :], start=True, stop=True)
                    mm.then_inc(pe_u, 1)
                if cur:
                    level(1)
                    pe.wait_ge(ld_wz, wq_count(i))
                    if prev:
                        pe.wait_ge(act_xt, i - 1)
                    for b in range(B):
                        for k in range(KT):
                            mm = pe.matmul(bank[2][:, b * 256:(b + 1) * 256], h_in[p][:, k, b, :], w_z[:, k, :],
                                           start=(k == 0), stop=(k == KT - 1))
                    mm.then_inc(pe_z, 1)
                    grow(1)
                if nxt:
                    project(i + 1, q, 0, (lambda: pe.wait_ge(dve_rhs, i)) if prev else (lambda: None))
                if cur:
                    level(2)
                if prev:
                    pe.wait_ge(act_u, i)
                    pe.wait_ge(pl_kd, i)
                    if cur:
                        pe.wait_ge(act_k, i + 1)
                    for m in range(M):
                        mm = pe.matmul(bank[4][:, m * P:(m + 1) * P], k_dec[q][:, m // RATIO, m % RATIO, :], u[:, m, :],
                                       start=True, stop=True)
                    mm.then_inc(pe_s, 1)
                if cur:
                    grow(2)
                if nxt:
                    project(i + 1, q, 1, lambda: None)
                if cur:
                    level(3)
                if prev:
                    if cur:
                        pe.wait_ge(dve_a, i + 1)
                    for m in range(M):
                        mm = pe.matmul(bank[5][:, m * P:(m + 1) * P], a_t[q][:, m // RATIO, m % RATIO, :], u[:, m, :],
                                       start=True, stop=True)
                    mm.then_inc(pe_o, 1)
                if cur:
                    grow(3)
                if nxt:
                    project(i + 1, q, 2, (lambda: pe.wait_ge(dve_qs, i)) if prev else (lambda: None))
                if cur:
                    level(4)
                    grow(4)
                if nxt:
                    project(i + 1, q, 3, lambda: None)
                if cur:
                    level(5)
                    grow(5)
                if prev:
                    pe.wait_ge(pl_x, i)
                    if cur:
                        pe.wait_ge(dve_zs, i + 1)
                    for m in range(M):
                        mm = pe.transpose(bank[2][:, m * P:(m + 1) * P], scaled[:, m, :], ident)
                    mm.then_inc(pe_xt, 1)
                if cur:
                    level(6)
                    grow(6)
                if prev:
                    pe.wait_ge(act_xt, i)
                    kh = (i - 1) // CH
                    pe.wait_ge(ld_wout, 16 * (kh + 1))
                    for b in range(B):
                        for r in range(RATIO):
                            mm = pe.matmul(bank[3][:, b * 256:(b + 1) * 256], o_t[:, b * RATIO + r, :],
                                           w_out[:, bass.ds(kh % 2, 1), r * DIM:(r + 1) * DIM].rearrange("p a n -> p (a n)"),
                                           start=(r == 0), stop=(r == RATIO - 1))
                    mm.then_inc(pe_y, 1)

            turns(pe, body)

        @block.scalar
        def _(act):
            def raw_copy(i, j):
                act.wait_ge(pe_proj, 4 * i + 2 * j + 2)
                c = i % CH
                for a in range(2):
                    mm = act.activation(raw[:, 2 * j + a, :, bass.ds(c * P + 3, P)],
                                        bank[j][:, a * 256:(a + 1) * 256].rearrange("p (b t) -> p b t", b=B), ACT.Copy)
                mm.then_inc(act_raw, 1)

            def conv_tanh(i, j):
                act.wait_ge(dve_conv, 16 * i + 8 * j + 8)
                act.activation(conv_tanh_sb[:, 2 * j:2 * j + 2].rearrange("p a b t -> p (a b t)"),
                               conv[:, 2 * j:2 * j + 2].rearrange("p a b t -> p (a b t)"), ACT.Tanh, scale=0.5).then_inc(act_conv, 1)

            def body(i, p, nxt, cur, prev):
                q = 1 - p
                if not prev:
                    act.wait_ge(ld_const, 16)
                    act.wait_ge(dve_init, 1)
                    for j in range(2):
                        raw_copy(0, j)
                    for j in range(2):
                        conv_tanh(0, j)
                if cur:
                    act.wait_ge(pe_dd, i + 1)
                    act.activation(decay[:].rearrange("p m s -> p (m s)"), bank[7][:], ACT.Exp).then_inc(act_dec, 1)
                    act.wait_ge(pe_k, i + 1)
                    if prev:
                        act.wait_ge(pl_kd, i)
                    act.activation(k_norms[:], bank[4][:, 0:B * P + 2 * B], ACT.Copy).then_inc(act_k, 1)
                    act.wait_ge(pe_inv, 6 * i + i + 1)
                    act.activation(t_inv[:], bank[7][:], ACT.Copy).then_inc(act_inv, 1)
                if prev:
                    act.wait_ge(pe_u, i)
                    act.activation(u[:].rearrange("p m e -> p (m e)"), bank[3][:], ACT.Copy).then_inc(act_u, 1)

                def inverse(l):
                    act.wait_ge(pe_inv, LEVELS * i + l + 1)
                    act.activation(half(r_inv[:], l, True), bank[7][:, 0:256].rearrange("p (q s) -> p q s", s=1 << l),
                                   ACT.Copy).then_inc(act_r, 1)
                    if l < LEVELS - 1:
                        act.activation(half(t_inv[:], l, False), bank[7][:, 256:512].rearrange("p (q s) -> p q s", s=1 << l),
                                       ACT.Copy).then_inc(act_inv, 1)

                if cur:
                    act.wait_ge(pe_z, i + 1)
                    act.activation(z_tanh[:], bank[2][:], ACT.Tanh, scale=0.5).then_inc(act_z, 1)
                    inverse(1)
                    inverse(2)
                if nxt:
                    raw_copy(i + 1, 0)
                if cur:
                    inverse(3)
                    inverse(4)
                if nxt:
                    raw_copy(i + 1, 1)
                    conv_tanh(i + 1, 0)
                if cur:
                    inverse(5)
                if prev:
                    act.wait_ge(pe_xt, i)
                    act.activation(o_t[:].rearrange("p m t -> p (m t)"), bank[2][:], ACT.Copy, scale=norm_w[:]).then_inc(act_xt, 1)
                if cur:
                    inverse(6)
                if nxt:
                    conv_tanh(i + 1, 1)

            turns(act, body)

        @block.vector
        def _(dve):
            def convolve(i, j):
                c = i % CH
                p = par[0]
                dve.wait_ge(act_raw, 2 * i + j + 1)
                if j == 0:
                    dve.wait_ge(ld_taps[p], 16 * (i // 2 + 1))
                for tap in range(4):
                    for a in range(2):
                        n = 8 * j + 2 * tap + a
                        src = raw[:, 2 * j + a, :, bass.ds(c * P + tap, P)]
                        dst = conv[:, 2 * j + a]
                        w = taps[p][:, 2 * j + a, tap:tap + 1]
                        if tap == 0:
                            dve.tensor_scalar(dst, src, w, None, ALU.mult).then_inc(dve_conv, 1)
                        else:
                            dve.wait_ge(dve_conv, 16 * i + n - 1)
                            dve.scalar_tensor_tensor(dst, src, w, dst, ALU.mult, ALU.add).then_inc(dve_conv, 1)

            def conv_silu(i, j):
                p = par[0]
                dve.wait_ge(act_conv, 2 * i + j + 1)
                f = lambda t: t[:, 2 * j:2 * j + 2].rearrange("p a b t -> p (a b t)")
                dve.scalar_tensor_tensor(f(qkv[p]), f(conv_tanh_sb), 1.0, f(conv), ALU.add, ALU.mult).then_inc(dve_qkv, 1)

            par = [0]

            def body(i, p, nxt, cur, prev):
                q = 1 - p
                if not prev:
                    dve.memset(raw[:, :, :, 0:3], 0.0)
                    dve.memset(state[:], 0.0)
                    for l in range(LEVELS):
                        dve.tensor_copy(z_neg[l][:].rearrange("p (m n) -> p m n", m=M), ident.unsqueeze(1).to_broadcast([P, M, P]))
                    dve.wait_ge(ld_const, 16)
                    dve.tensor_scalar(norm_w[:], norm_w[:], float(P) ** 0.5, None, ALU.mult)
                    dve.memset(y[:], 0.0).then_inc(dve_init, 1)
                    dve.wait_ge(dve_init, 1)
                    par[0] = 0
                    convolve(0, 0)
                    convolve(0, 1)
                    conv_silu(0, 0)
                    conv_silu(0, 1)

                def join(l):
                    wait_apart(dve, sh, pe_lev, LEVELS * i + l + 1)
                    src = half(bank[6][:], 0, True) if l == 0 else bank[6][:, 0:256].rearrange("p (q s) -> p q s", s=1 << l)
                    dve.copy_predicated(half(z_neg[l][:], l, True), sh.level_masks[:, l].rearrange("p (q s) -> p q s", s=1 << l),
                                        src).then_inc(dve_z, 1)

                if cur:
                    dve.wait_ge(pe_kkq, i + 1)
                    dve.tensor_tensor(kkq[:], bank[5][:].rearrange("p (a b s) -> p a b s", a=2, b=B),
                                      kkq_mask.unsqueeze(2).to_broadcast([P, 2, B, P]), ALU.mult).then_inc(dve_kkq, 1)
                if prev:
                    dve.wait_ge(pe_ks, i)
                    dve.wait_ge(dve_v, i)
                    for m in range(M):
                        mm = dve.scalar_tensor_tensor(rhs[:, m, :], bank[0][:, m * P:(m + 1) * P],
                                                      ks_scale[q][:, m // RATIO, m % RATIO:m % RATIO + 1], v_beta[:, m, :],
                                                      ALU.mult, ALU.add)
                    mm.then_inc(dve_rhs, 1)
                if cur:
                    dve.wait_ge(act_dec, i + 1)
                    dve.wait_ge(dve_kkq, i + 1)
                    dve.wait_ge(pl_sc, 4 * i + 2)
                    for m in range(M):
                        mm = dve.scalar_tensor_tensor(m_neg[:, m, :], decay[:, m, :], beta_r2[p][:, m // RATIO, m % RATIO:m % RATIO + 1],
                                                      kkq[:, 0, m // RATIO, :], ALU.mult, ALU.mult)
                    mm.then_inc(dve_m, 1)
                    dve.wait_ge(pe_dt, i + 1)
                    dve.tensor_tensor(a_t[p][:], bank[5][:].rearrange("p (b r t) -> p b r t", b=B, r=RATIO),
                                      kkq[:, 1].unsqueeze(2).to_broadcast([P, B, RATIO, P]), ALU.mult).then_inc(dve_a, 1)
                    join(0)
                    dve.wait_ge(pe_v, i + 1)
                    dve.tensor_tensor(v_beta[:], bank[3][:].rearrange("p (m e) -> p m e", m=M),
                                      beta_r[p][:].rearrange("p b r -> p (b r)").unsqueeze(2).to_broadcast([P, M, P]),
                                      ALU.mult).then_inc(dve_v, 1)
                if prev:
                    dve.wait_ge(pe_qs, i)
                    dve.tensor_tensor(qs[:], bank[1][:].rearrange("p (m e) -> p m e", m=M),
                                      qs_scale[q][:].rearrange("p b r -> p (b r)").unsqueeze(2).to_broadcast([P, M, P]),
                                      ALU.mult).then_inc(dve_qs, 1)
                if cur:
                    join(1)
                    dve.wait_ge(act_z, i + 1)
                    dve.scalar_tensor_tensor(z_silu[p][:], z_tanh[:], 1.0, bank[2][:], ALU.add, ALU.mult).then_inc(dve_zs, 1)
                    join(2)
                if prev:
                    dve.wait_ge(pe_s, i)
                    for m in range(M):
                        b, r = m // RATIO, m % RATIO
                        mm = dve.scalar_tensor_tensor(state[:, b, r, :], state[:, b, r, :], gate[q][:, 5, b, r:r + 1],
                                                      bank[4][:, m * P:(m + 1) * P], ALU.mult, ALU.add)
                    mm.then_inc(dve_s, 1)
                if cur:
                    join(3)
                if prev:
                    dve.wait_ge(pe_o, i)
                    dve.wait_ge(dve_qs, i)
                    for b in range(B):
                        mm = dve.scalar_tensor_tensor(o[:, b * RATIO:(b + 1) * RATIO, :], bank[5][:, b * 256:(b + 1) * 256].rearrange("p (r e) -> p r e", r=RATIO),
                                                      rnorm[q][:, 0, b:b + 1], qs[:, b * RATIO:(b + 1) * RATIO, :], ALU.mult, ALU.add)
                    mm.then_inc(dve_o, 1)
                par[0] = q
                if nxt:
                    convolve(i + 1, 0)
                if cur:
                    join(4)
                if prev:
                    dve.wait_ge(pl_gsq, i)
                    dve.tensor_reduce(o_norm[:], gated_sq[:], AX.X, ALU.add).then_inc(dve_red, 1)
                if cur:
                    join(5)
                if nxt:
                    conv_silu(i + 1, 0)
                    convolve(i + 1, 1)
                if cur:
                    join(6)
                if nxt:
                    conv_silu(i + 1, 1)
                if prev:
                    dve.wait_ge(pe_y, i)
                    c = (i - 1) % CH
                    yt = y[:, bass.ds(c, 1)].rearrange("p c b d -> p (c b d)")
                    dve.tensor_tensor(yt, bank[3][:], yt, ALU.add).then_inc(dve_y, 1)

            turns(dve, body)
            dve.wait_ge(dve_y, STEPS)

        @block.gpsimd
        def _(pool):
            def body(i, p, nxt, cur, prev):
                q = 1 - p

                def early(i, p, first):
                    pool.wait_ge(dve_qkv, 2 * i + 1)
                    if not first:
                        pool.wait_ge(pe_k, i)
                    pool.tensor_tensor(squares[:].rearrange("p a b t -> p (a b t)"), qkv[p][:, 0:2].rearrange("p a b t -> p (a b t)"),
                                       qkv[p][:, 0:2].rearrange("p a b t -> p (a b t)"), ALU.mult).then_inc(pl_sq, 1)
                    pool.wait_ge(ld_gate[p], 16 * (i // 2 + 1))
                    if not first:
                        pool.wait_ge(pe_dd, i)
                    pool.tensor_tensor(g_below[:], below.unsqueeze(1).to_broadcast([P, M, P]),
                                       gate[p][:, 1].rearrange("p b r -> p (b r)").unsqueeze(2).to_broadcast([P, M, P]),
                                       ALU.mult).then_inc(pl_g, 1)

                if cur:
                    early(i, p, not prev)
                    pool.wait_ge(act_k, i + 1)
                    if prev:
                        pool.wait_ge(dve_o, i - 1)
                    pool.tensor_tensor(rnorm[p][:].rearrange("p a b -> p (a b)"), norms,
                                       sh.pw[:, 2:3].to_broadcast([P, 4]), ALU.add).then_inc(pl_rn, 1)
                    pool.wait_ge(pl_rn, 2 * i + 1)
                    pool.tensor_tensor(rnorm[p][:].rearrange("p a b -> p (a b)"), rnorm[p][:].rearrange("p a b -> p (a b)"),
                                       sh.pw[:, 0:1].to_broadcast([P, 4]), ALU.pow).then_inc(pl_rn, 1)
                    pool.wait_ge(pl_rn, 2 * i + 2)
                    rk = rnorm[p][:, 1].unsqueeze(2).to_broadcast([P, B, RATIO])
                    rq = rnorm[p][:, 0].unsqueeze(2).to_broadcast([P, B, RATIO])
                    pool.tensor_tensor(beta_r[p][:], gate[p][:, 0], rk, ALU.mult).then_inc(pl_sc, 1)
                    pool.wait_ge(pl_sc, 4 * i + 1)
                    pool.tensor_tensor(beta_r2[p][:], beta_r[p][:], rk, ALU.mult).then_inc(pl_sc, 1)
                    pool.tensor_tensor(qs_scale[p][:], gate[p][:, 3], rq, ALU.mult).then_inc(pl_sc, 1)
                    pool.wait_ge(pl_sc, 4 * i + 3)
                    pool.tensor_tensor(ks_scale[p][:], gate[p][:, 2], beta_r2[p][:], ALU.mult).then_inc(pl_sc, 1)
                    pool.tensor_tensor(k_dec[p][:], k_tok.unsqueeze(2).to_broadcast([P, B, RATIO, P]),
                                       gate[p][:, 4].unsqueeze(3).to_broadcast([P, B, RATIO, P]), ALU.mult).then_inc(pl_kd, 1)
                    pool.wait_ge(pe_inv, LEVELS * i + 1)
                    if prev:
                        pool.wait_ge(pe_u, i)
                    z0 = half(z_neg[0][:], 1, False)
                    pool.tensor_tensor(half(r_inv[:], 1, False), z0, sh.masks[:, 5 * P:6 * P].unsqueeze(2).to_broadcast([P, P, 2]), ALU.mult).then_inc(pl_r, 1)
                if prev:
                    pool.wait_ge(dve_o, i)
                    pool.wait_ge(dve_zs, i)
                    pool.wait_ge(pl_x, i - 1)
                    pool.tensor_tensor(gated[:], o[:].rearrange("p m e -> p (m e)"), z_silu[q][:], ALU.mult).then_inc(pl_gt, 1)
                    pool.wait_ge(pl_gt, i)
                    pool.tensor_tensor(gated_sq[:].rearrange("p m e -> p (m e)"), gated[:], gated[:], ALU.mult).then_inc(pl_gsq, 1)
                    pool.wait_ge(dve_red, i)
                    pool.tensor_tensor(o_rnorm[:], o_norm[:], sh.pw[:, 3:4].to_broadcast([P, M]), ALU.add).then_inc(pl_on, 1)
                    pool.wait_ge(pl_on, 2 * i - 1)
                    pool.tensor_tensor(o_rnorm[:], o_rnorm[:], sh.pw[:, 0:1].to_broadcast([P, M]), ALU.pow).then_inc(pl_on, 1)
                    pool.wait_ge(pl_on, 2 * i)
                    pool.wait_ge(pe_xt, i - 1)
                    pool.tensor_tensor(scaled[:], gated[:].rearrange("p (m e) -> p m e", m=M),
                                       o_rnorm[:].unsqueeze(2).to_broadcast([P, M, P]), ALU.mult).then_inc(pl_x, 1)

            turns(pool, body)


def ln_vector(dve, sh, w, n, src, S):
    dve.bn_stats(sh.stats[w][:], src).then_inc(S.stats, 1)
    wait_apart(dve, sh, S.stats, n + 1)
    dve.bn_aggr(sh.mean_var[w][:], sh.stats[w][:]).then_inc(S.mean, 1)


def ln_pool(pool, sh, w, n, S):
    pool.wait_ge(S.mean, n + 1)
    pool.tensor_tensor(sh.rstd[w][:], sh.mean_var[w][:, 1:2], sh.pw[:, 1:2], ALU.add).then_inc(S.var, 1)
    pool.wait_ge(S.var, n + 1)
    pool.tensor_tensor(sh.rstd[w][:], sh.rstd[w][:], sh.pw[:, 0:1], ALU.pow).then_inc(S.rstd, 1)


def ln_norm(dve, sh, w, n, src, S):
    dve.wait_ge(S.rstd, n + 1)
    dve.tensor_scalar(sh.normed[w][:], src, sh.mean_var[w][:, 0:1], sh.rstd[w][:], ALU.subtract, ALU.mult).then_inc(S.norm, 1)


def ln_turn(pe, sh, w, n, bank, S):
    pe.wait_ge(S.norm, n + 1)
    for k in range(KT):
        mm = pe.transpose(bank[:, k * P:(k + 1) * P], sh.normed[w][:, k * P:(k + 1) * P], sh.masks[:, 0:P])
    mm.then_inc(S.turn, 1)


def ln_modulate(dve, sh, w, n, bank, dst, layer, half_of_layer, b, S):
    dve.wait_ge(S.turn, n + 1)
    for k in range(KT):
        ins = dve.tensor_scalar(dst[:, k, :], bank[:, k * P:(k + 1) * P], sh.mod[:, layer, 3 * half_of_layer + 1, k, b:b + 1],
                                sh.mod[:, layer, 3 * half_of_layer, k, b:b + 1], ALU.mult, ALU.add)
    ins.then_inc(S.h, 1)


class LnSems:
    def __init__(self, sem, name):
        self.stats, self.mean, self.var, self.rstd, self.norm, self.turn, self.h = (
            sem(f"{name}_{n}") for n in ("stats", "mean", "var", "rstd", "norm", "turn", "h"))


W = 4
NT = CH * B
NH = 32
NG = 8
HD = 8
PARTS = 3


def ffn0_phase(nc, A, sh, sem):
    with ExitStack() as ctx:
        def sb(name, shape, dt=F32):
            return ctx.enter_context(nc.sbuf_tensor(name, shape, dt))

        w_up = sb("f0_up", [P, KT, DIM])
        w_down = sb("f0_down", [P, KT, DIM])
        w_exp = sb("f0_exp", [P, KT, DIM])
        w_gate = sb("f0_gate", [P, KT, 8])
        w_q = sb("a_wq", [P, KT, DIM])
        w_k = sb("a_wk", [P, KT, 64])
        w_v = sb("a_wv", [P, KT, 64])
        b_q = sb("a_bq", [P, KT])
        b_k = sb("a_bk", [64, 1])
        b_v = sb("a_bv", [P, 64])
        parts = sb("qk_parts", [P, PARTS, 3, T * B], BF16)
        h_a = [sb(f"f0_ha{w}", [P, KT, P]) for w in range(W)]
        h_b = [sb(f"f0_hb{w}", [P, KT, P]) for w in range(W)]
        up = [sb(f"f0_relu{w}", [P, KT, P]) for w in range(W)]
        shared = [sb(f"f0_shared{w}", [P, DIM]) for w in range(W)]
        tmp = [sb(f"f0_tmp{w}", [P, DIM]) for w in range(W)]
        logits = sb("f0_logits", [P, W, 8])
        top = sb("f0_top", [P, W, 8])
        gap = sb("f0_gap", [P, W])
        r1_in = sb("f0_neg", [P, W])
        r1 = sb("f0_r1", [P, W])
        route = sb("f0_route", [P, W])
        qk = [sb(f"qk{w}", [P, 3, P]) for w in range(W)]
        qk_hi = [[sb(f"qk_part{k}_{w}", [P, 3, P], BF16) for w in range(W)] for k in range(PARTS)]
        bank = [[ctx.enter_context(nc.psum_tensor(f"f0_{n}{w}", [P, 512], F32)) for w in range(W)] for n in "ab"]
        neg, loaded, yg, x1, mm_up, relu, mm_down, lg, tops, ex, rt, sh_sb, moe, x2, mm_qkv, qk_sb, v_sb, split, stored, init = (
            sem("f0_" + n) for n in ("neg", "loaded", "yg", "x1", "mm_up", "relu", "mm_down", "lg", "tops", "ex", "rt", "shsb", "moe",
                                     "x2", "mm_qkv", "qk_sb", "v_sb", "split", "stored", "init"))
        SA, SB = LnSems(sem, "f0a"), LnSems(sem, "f0b")
        block = ctx.enter_context(nc.Block())
        tiles = [(w, w // B, w % B) for w in range(W)]

        def xt(c, b, t):
            return t[:, bass.ds(c, 1), b, :].rearrange("p a d -> p (a d)")

        @block.sync
        def _(sp):
            n = 0
            for dst, src in ((w_up[:], A["f0_up"]), (w_down[:], A["f0_down"]), (w_exp[:], A["f0_exp"]), (w_gate[:], A["f0_gate"]),
                             (w_q[:], A["a_wq"]), (w_k[:], A["a_wk"]), (w_v[:], A["a_wv"]), (b_q[:], A["a_bq"]),
                             (b_k[:], A["a_bk"]), (b_v[:], A["a_bv"].to_broadcast([P, 64]))):
                sp.dma_start(dst, src).then_inc(loaded, 16)
            sp.wait_ge(v_sb, 2 * NT)
            for i in range(PARTS):
                for ct in range(3):
                    rows = P if ct < 2 else 64
                    sp.dma_start(sh.scratch[i, ct * P:ct * P + rows, :], parts[0:rows, i, ct, :]).then_inc(stored, 16)
            sp.wait_ge(stored, 16 * 9)

        @block.vector
        def _(dve):
            for w in range(W):
                dve.memset(qk[w][:, 2, :], 0.0)
            dve.memset(sh.v_aug[:], 0.0).then_inc(init, 1)
            dve.wait_ge(init, 1)
            dve.memset(sh.v_aug[:, :, :, HD:HD + 1], 1.0).then_inc(init, 1)
            dve.wait_ge(init, 2)
            dve.wait_ge(loaded, 160)
            with dve.Fori(0, NT // W) as it:
                for w, dc, b in tiles:
                    c = it * (W // B) + dc
                    dve.tensor_tensor(tmp[w][:], xt(c, b, sh.y), sh.gate[:, 0, 0, b, :], ALU.mult).then_inc(yg, 1)
                for w, dc, b in tiles:
                    c, n = it * (W // B) + dc, it * W + w
                    dve.wait_ge(yg, n + 1)
                    dve.tensor_tensor(xt(c, b, sh.x), xt(c, b, sh.x), tmp[w][:], ALU.add).then_inc(x1, 1)
                for w, dc, b in tiles:
                    c, n = it * (W // B) + dc, it * W + w
                    wait_apart(dve, sh, x1, n + 1)
                    ln_vector(dve, sh, w, n, xt(c, b, sh.x), SA)
                for w, dc, b in tiles:
                    c, n = it * (W // B) + dc, it * W + w
                    ln_norm(dve, sh, w, n, xt(c, b, sh.x), SA)
                for w, dc, b in tiles:
                    ln_modulate(dve, sh, w, it * W + w, bank[0][w], h_a[w], 0, 1, b, SA)
                for w, dc, b in tiles:
                    wait_apart(dve, sh, lg, it * W + w + 1)
                    dve.max(top[:, w, :], logits[:, w, :]).then_inc(tops, 1)
                dve.wait_ge(ex, it + 1)
                dve.tensor_scalar(r1[:], gap[:], 1.0, None, ALU.add).then_inc(rt, 1)
                wait_apart(dve, sh, rt, it * 4 + 1)
                dve.reciprocal(r1[:], r1[:]).then_inc(rt, 1)
                dve.wait_ge(rt, it * 4 + 2)
                dve.tensor_tensor(route[:], gap[:], r1[:], ALU.mult).then_inc(rt, 1)
                dve.wait_ge(rt, it * 4 + 3)
                dve.tensor_tensor(route[:], route[:], r1[:], ALU.add).then_inc(rt, 1)
                dve.wait_ge(rt, it * 4 + 4)
                for w, dc, b in tiles:
                    dve.wait_ge(sh_sb, it * W + w + 1)
                    dve.scalar_tensor_tensor(tmp[w][:], bank[0][w][:, 256:512], route[:, w:w + 1], shared[w][:],
                                             ALU.mult, ALU.add).then_inc(moe, 1)
                for w, dc, b in tiles:
                    n = it * W + w
                    dve.wait_ge(moe, it * 2 * W + w + 1)
                    dve.tensor_tensor(tmp[w][:], tmp[w][:], sh.gate[:, 0, 1, b, :], ALU.mult).then_inc(moe, 1)
                for w, dc, b in tiles:
                    c, n = it * (W // B) + dc, it * W + w
                    dve.wait_ge(moe, it * 2 * W + W + w + 1)
                    dve.tensor_tensor(xt(c, b, sh.x), xt(c, b, sh.x), tmp[w][:], ALU.add).then_inc(x2, 1)
                for w, dc, b in tiles:
                    c, n = it * (W // B) + dc, it * W + w
                    wait_apart(dve, sh, x2, n + 1)
                    ln_vector(dve, sh, w, n, xt(c, b, sh.x), SB)
                for w, dc, b in tiles:
                    c, n = it * (W // B) + dc, it * W + w
                    ln_norm(dve, sh, w, n, xt(c, b, sh.x), SB)
                for w, dc, b in tiles:
                    ln_modulate(dve, sh, w, it * W + w, bank[0][w], h_b[w], 1, 0, b, SB)
                for w, dc, b in tiles:
                    n = it * W + w
                    dve.wait_ge(qk_sb, n + 1)
                    tile = bass.ds((it * (W // B) + dc) + b * CH, 1)
                    dve.tensor_tensor(sh.v_aug[:, tile, :, 0:HD], bank[1][w][:, 384:448].rearrange("p (a g d) -> p a g d", a=1, g=NG),
                                      b_v[:].rearrange("p (a g d) -> p a g d", a=1, g=NG), ALU.add).then_inc(v_sb, 1)
                    dve.tensor_copy(qk_hi[0][w][:], qk[w][:]).then_inc(split, 1)
                for k in range(1, PARTS):
                    for w, dc, b in tiles:
                        dve.wait_ge(split, it * 5 * W + (2 * k - 2) * W + w + 1)
                        dve.tensor_tensor(qk[w][:], qk[w][:], qk_hi[k - 1][w][:], ALU.subtract).then_inc(split, 1)
                    for w, dc, b in tiles:
                        dve.wait_ge(split, it * 5 * W + (2 * k - 1) * W + w + 1)
                        dve.tensor_copy(qk_hi[k][w][:], qk[w][:]).then_inc(split, 1)
                for w, dc, b in tiles:
                    col = bass.ds((it * (W // B) + dc) * P + b * T, P)
                    for k in range(PARTS):
                        if k == 2:
                            dve.wait_ge(split, it * 5 * W + 4 * W + w + 1)
                        ins = dve.tensor_copy(parts[:, k, :, col], qk_hi[k][w][:])
                    ins.then_inc(v_sb, 1)
            dve.wait_ge(v_sb, 2 * NT)
            dve.wait_ge(x2, NT)

        @block.gpsimd
        def _(pool):
            with pool.Fori(0, NT // W) as it:
                for w in range(W):
                    ln_pool(pool, sh, w, it * W + w, SA)
                for w in range(W):
                    ln_pool(pool, sh, w, it * W + w, SB)

        @block.scalar
        def _(act):
            act.wait_ge(loaded, 160)
            with act.Fori(0, NT // W) as it:
                for w in range(W):
                    n = it * W + w
                    act.wait_ge(mm_up, n + 1)
                    act.activation(logits[:, w, :], bank[1][w][:, 256:264], ACT.Copy).then_inc(lg, 1)
                    act.activation(up[w][:].rearrange("p k t -> p (k t)"), bank[1][w][:, 0:256], ACT.Relu).then_inc(relu, 1)
                for w in range(W):
                    n = it * W + w
                    act.wait_ge(tops, n + 1)
                    act.activation(r1_in[:, w:w + 1], top[:, w, 0:1], ACT.Copy, scale=-1.0).then_inc(neg, 1)
                for w in range(W):
                    act.wait_ge(neg, it * W + w + 1)
                    e = act.activation(gap[:, w:w + 1], top[:, w, 1:2], ACT.Exp, bias=r1_in[:, w:w + 1])
                e.then_inc(ex, 1)
                for w in range(W):
                    n = it * W + w
                    act.wait_ge(mm_down, n + 1)
                    act.activation(shared[w][:], bank[0][w][:, 0:256], ACT.Copy).then_inc(sh_sb, 1)
                for w in range(W):
                    n = it * W + w
                    act.wait_ge(mm_qkv, n + 1)
                    for ct in range(KT):
                        act.activation(qk[w][:, ct, :], bank[1][w][:, ct * P:(ct + 1) * P], ACT.Identity, bias=b_q[:, ct:ct + 1])
                    act.activation(qk[w][0:64, 2, :], bank[1][w][0:64, 256:384], ACT.Identity, bias=b_k[:]).then_inc(qk_sb, 1)

        @block.tensor
        def _(pe):
            pe.wait_ge(loaded, 160)
            with pe.Fori(0, NT // W) as it:
                for w in range(W):
                    ln_turn(pe, sh, w, it * W + w, bank[0][w], SA)
                for w in range(W):
                    n = it * W + w
                    pe.wait_ge(SA.h, n + 1)
                    pe.wait_ge(v_sb, it * 2 * W)
                    for ft in range(2):
                        for k in range(KT):
                            pe.matmul(bank[1][w][:, ft * P:(ft + 1) * P], w_up[:, k, ft * P:(ft + 1) * P], h_a[w][:, k, :],
                                      start=(k == 0), stop=(k == KT - 1))
                    for k in range(KT):
                        mm = pe.matmul(bank[1][w][:, 256:264], h_a[w][:, k, :], w_gate[:, k, :], start=(k == 0), stop=(k == KT - 1))
                    mm.then_inc(mm_up, 1)
                for w in range(W):
                    n = it * W + w
                    pe.wait_ge(relu, n + 1)
                    for k in range(KT):
                        pe.matmul(bank[0][w][:, 0:256], up[w][:, k, :], w_down[:, k, :], start=(k == 0), stop=(k == KT - 1))
                    for k in range(KT):
                        mm = pe.matmul(bank[0][w][:, 256:512], h_a[w][:, k, :], w_exp[:, k, :], start=(k == 0), stop=(k == KT - 1))
                    mm.then_inc(mm_down, 1)
                for w in range(W):
                    ln_turn(pe, sh, w, it * W + w, bank[0][w], SB)
                for w in range(W):
                    n = it * W + w
                    pe.wait_ge(SB.h, n + 1)
                    for ct in range(2):
                        for k in range(KT):
                            pe.matmul(bank[1][w][:, ct * P:(ct + 1) * P], w_q[:, k, ct * P:(ct + 1) * P], h_b[w][:, k, :],
                                      start=(k == 0), stop=(k == KT - 1))
                    for k in range(KT):
                        pe.matmul(bank[1][w][0:64, 256:384], w_k[:, k, :], h_b[w][:, k, :], start=(k == 0), stop=(k == KT - 1))
                    for k in range(KT):
                        mm = pe.matmul(bank[1][w][:, 384:448], h_b[w][:, k, :], w_v[:, k, :], start=(k == 0), stop=(k == KT - 1))
                    mm.then_inc(mm_qkv, 1)


QH = T // 512
KC = T // P
ROWS = 96
UNITS = B * NG


def attention_phase(nc, A, sh, sem):
    with ExitStack() as ctx:
        def sb(name, shape, dt=F32):
            return ctx.enter_context(nc.sbuf_tensor(name, shape, dt))

        q_rows = [sb(f"q_rows{p}", [ROWS, 4, T], BF16) for p in range(2)]
        k_rows = [sb(f"k_rows{p}", [ROWS, T], BF16) for p in range(2)]
        v_unit = [sb(f"v_unit{p}", [P, KC, 32]) for p in range(2)]
        ones_row = sb("ones_row", [PARTS, T], BF16)
        half_max = sb("half_max", [P, 32, 2])
        row_max = sb("row_max", [P, 32])
        neg_max = sb("neg_max", [32, P])
        max_part = [[sb(f"max_part{k}_{p}", [32, P], BF16) for p in range(2)] for k in range(PARTS)]
        probs = [sb(f"probs{p}", [P, 4, 512]) for p in range(2)]
        out_t = [sb(f"out_t{p}", [P, 512]) for p in range(2)]
        rden = sb("rden", [P, 16])
        s_ps = [ctx.enter_context(nc.psum_tensor(f"s_ps{k}", [P, 1024], F32)) for k in range(2)]
        m_ps = [ctx.enter_context(nc.psum_tensor(f"m_ps{k}", [P, 512], F32)) for k in range(2)]
        pv_ps = ctx.enter_context(nc.psum_tensor("pv_ps", [P, 512], F32))
        t_ps = ctx.enter_context(nc.psum_tensor("t_ps", [P, 512], F32))
        ld_q, ld_k, ld_m = ([sem(f"at_{n}{p}") for p in range(2)] for n in ("ldq", "ldk", "ldm"))
        init, mm_m, red, rmax, mx_t, nmax, mm_s, exp, mm_pv, o_sb, o_tr, den, att, vcp, ld_one = (
            sem("at_" + n) for n in ("init", "mm_m", "red", "rmax", "mx_t", "nmax", "mm_s", "exp", "mm_pv", "o_sb", "o_tr",
                                     "den", "att", "vcp", "ld_one"))
        block = ctx.enter_context(nc.Block())
        ident = sh.masks[:, 0:P]
        SLOTS = QH * KC

        def turns(eng, body):
            body(0, 0, True, False)
            body(1, 1, True, True)
            with eng.Fori(0, (UNITS - 2) // 2) as j:
                body(j * 2 + 2, 0, True, True)
                body(j * 2 + 3, 1, True, True)
            body(UNITS, 0, False, True)

        @block.sync
        def _(sp):
            sp.wait_ge(init, 1)
            for p in range(2):
                sp.dma_start(k_rows[p][72:75, :], ones_row[:]).then_inc(ld_one, 16)

            def body(u, p, cur, prev):
                if cur:
                    b, g = u // NG, u % NG
                    if not isinstance(u, int) or u >= 2:
                        sp.wait_ge(mm_pv, (u - 1) * SLOTS)
                    src = sh.scratch
                    for j in range(PARTS):
                        for i in range(PARTS):
                            r = (j * PARTS + i) * HD
                            sp.dma_start(q_rows[p][r:r + HD, :, :],
                                         src[i:i + 1, bass.ds(g * 4 * HD, 4 * HD), bass.ds(b * T, T)]
                                         .rearrange("a (h d) t -> d (a h) t", h=4)).then_inc(ld_q[p], 16)
                            sp.dma_start(k_rows[p][r:r + HD, :],
                                         src[j:j + 1, bass.ds(2 * P + g * HD, HD), bass.ds(b * T, T)]
                                         .rearrange("a d t -> (a d) t")).then_inc(ld_k[p], 16)
                    sp.wait_ge(nmax, 6 * (u + 1))
                    for k in range(PARTS):
                        sp.dma_start(q_rows[p][72 + k:73 + k, :, :].rearrange("a h (q t) -> a (h q) t", t=P),
                                     max_part[k][p][:]).then_inc(ld_m[p], 16)

            turns(sp, body)

        @block.gpsimd
        def _(pool):
            def body(u, p, cur, prev):
                if cur:
                    b, g = u // NG, u % NG
                    if not isinstance(u, int) or u >= 2:
                        pool.wait_ge(mm_pv, (u - 1) * SLOTS)
                    pool.tensor_tensor(v_unit[p][:], sh.v_aug[:, bass.ds(b * CH, CH), bass.ds(g, 1), :].rearrange("p c a d -> p (c a) d"),
                                       sh.masks[:, 5 * P:5 * P + 32].unsqueeze(1).to_broadcast([P, KC, 32]), ALU.mult).then_inc(vcp, 1)

            turns(pool, body)

        @block.tensor
        def _(pe):
            def body(u, p, cur, prev):
                q = 1 - p
                if cur:
                    pe.wait_ge(ld_q[p], 144 * (u // 2 + 1))
                    pe.wait_ge(ld_k[p], 144 * (u // 2 + 1))
                if not prev:
                    pe.wait_ge(ld_one, 32)
                if prev:
                    pe.wait_ge(ld_m[q], 48 * ((u - 1) // 2 + 1))
                    pe.wait_ge(vcp, u)

                def maxima(slot):
                    for t in (2 * slot, 2 * slot + 1):
                        for hf in range(2):
                            n = 2 * t + hf
                            if n >= 2:
                                pe.wait_ge(red, 64 * u + n - 1)
                            elif prev:
                                pe.wait_ge(red, 64 * u + n - 1)
                            pe.matmul(m_ps[n % 2][:], q_rows[p][0:72, t // 8, (t % 8) * P:(t % 8 + 1) * P],
                                      k_rows[p][0:72, hf * 512:(hf + 1) * 512], start=True, stop=True).then_inc(mm_m, 1)

                def scores(slot):
                    qh, kc = slot // KC, slot % KC
                    for pair in range(2):
                        if not isinstance(u, int) or u > 1 or slot > 0:
                            pe.wait_ge(exp, 2 * SLOTS * (u - 1) + 2 * slot + pair - 1)
                        for hh in range(2):
                            mm = pe.matmul(s_ps[pair][:, hh * 512:(hh + 1) * 512], k_rows[q][:, kc * P:(kc + 1) * P],
                                           q_rows[q][:, 2 * pair + hh, qh * 512:(qh + 1) * 512], start=True, stop=True)
                        mm.then_inc(mm_s, 1)

                def attend(slot):
                    qh, kc = slot // KC, slot % KC
                    pe.wait_ge(exp, 2 * SLOTS * (u - 1) + 2 * slot + 2)
                    if kc == 0:
                        pe.wait_ge(o_sb, QH * (u - 1) + qh)
                    for h in range(4):
                        mm = pe.matmul(pv_ps[32 * h:32 * h + 32, :], v_unit[q][:, kc, :], probs[slot % 2][:, h, :],
                                       start=(kc == 0), stop=(kc == KC - 1))
                    mm.then_inc(mm_pv, 1)

                def turn_out(qh):
                    n = QH * (u - 1) + qh
                    pe.wait_ge(o_sb, n + 1)
                    if cur or qh > 0:
                        pe.wait_ge(att, n)
                    if qh == 0:
                        pe.wait_ge(nmax, 6 * u)
                    for t in range(4):
                        mm = pe.transpose(t_ps[:, t * P:(t + 1) * P], out_t[qh][:, t * P:(t + 1) * P], ident)
                    mm.then_inc(o_tr, 1)

                for slot in range(SLOTS):
                    if prev:
                        scores(slot)
                    if cur:
                        maxima(slot)
                    if prev and slot > 0:
                        attend(slot - 1)
                    if prev and slot == KC + 2:
                        turn_out(0)
                if prev:
                    attend(SLOTS - 1)
                    turn_out(1)
                if cur:
                    pe.wait_ge(rmax, u + 1)
                    if prev:
                        pe.wait_ge(att, QH * u)
                    pe.transpose(t_ps[0:32, 0:P], row_max[:], ident).then_inc(mx_t, 1)

            turns(pe, body)

        @block.scalar
        def _(act):
            def body(u, p, cur, prev):
                if not prev:
                    return
                for slot in range(SLOTS):
                    n = SLOTS * (u - 1) + slot
                    if slot >= 2 or not isinstance(u, int) or u > 1:
                        act.wait_ge(mm_pv, n - 1)
                    for pair in range(2):
                        act.wait_ge(mm_s, 2 * n + pair + 1)
                        act.activation(probs[slot % 2][:, 2 * pair:2 * pair + 2, :].rearrange("p h q -> p (h q)"), s_ps[pair][:],
                                       ACT.Exp, scale=float(HD) ** -0.5).then_inc(exp, 1)
                    if slot % KC == KC - 1:
                        qh = slot // KC
                        act.wait_ge(mm_pv, n + 1)
                        if not isinstance(u, int) or u > 1:
                            act.wait_ge(o_tr, QH * (u - 2) + qh + 1)
                        act.activation(out_t[qh][:], pv_ps[:], ACT.Copy).then_inc(o_sb, 1)

            turns(act, body)

        @block.vector
        def _(dve):
            for p in range(2):
                dve.memset(k_rows[p][64:ROWS, :], 0.0)
                dve.memset(q_rows[p][64:ROWS, :, :], 0.0)
            dve.memset(ones_row[:], 1.0)
            dve.drain().then_inc(init, 1)

            def body(u, p, cur, prev):
                def output(qh):
                    n = QH * (u - 1) + qh
                    b, g = (u - 1) // NG, (u - 1) % NG
                    src = t_ps[:].rearrange("p (t d) -> p t d", d=32)
                    wait_apart(dve, sh, o_tr, n + 1)
                    dve.reciprocal(rden[:], src[:, :, HD:HD + 1].rearrange("p t a -> p (t a)")).then_inc(den, 1)
                    dve.wait_ge(den, n + 1)
                    for t in range(4):
                        ins = dve.tensor_tensor(sh.att[:, bass.ds(b * CH + 4 * qh + t, 1), bass.ds(g * 32, 32)].rearrange("p a (h d) -> p (a h) d", h=4),
                                                src[:, 4 * t:4 * t + 4, 0:HD], rden[:, 4 * t:4 * t + 4].unsqueeze(2).to_broadcast([P, 4, HD]),
                                                ALU.mult)
                    ins.then_inc(att, 1)

                for slot in range(SLOTS):
                    if cur:
                        for n in range(4 * slot, 4 * slot + 4):
                            dve.wait_ge(mm_m, 64 * u + n + 1)
                            dve.tensor_reduce(half_max[:, n // 2, n % 2:n % 2 + 1], m_ps[n % 2][:], AX.X, ALU.max).then_inc(red, 1)
                    if prev and slot == KC + 2:
                        output(0)
                if cur:
                    if prev:
                        dve.wait_ge(mx_t, u)
                    dve.wait_ge(red, 64 * (u + 1))
                    dve.tensor_tensor(row_max[:], half_max[:, :, 0], half_max[:, :, 1], ALU.max).then_inc(rmax, 1)
                if prev:
                    output(1)
                if cur:
                    dve.wait_ge(mx_t, u + 1)
                    if not isinstance(u, int) or u >= 2:
                        dve.wait_ge(ld_m[p], 48 * (u // 2))
                    dve.tensor_scalar(neg_max[:], t_ps[0:32, 0:P], -1.0, None, ALU.mult).then_inc(nmax, 1)
                    dve.wait_ge(nmax, 6 * u + 1)
                    dve.tensor_copy(max_part[0][p][:], neg_max[:]).then_inc(nmax, 1)
                    for k in range(1, PARTS):
                        dve.wait_ge(nmax, 6 * u + 2 * k)
                        dve.tensor_tensor(neg_max[:], neg_max[:], max_part[k - 1][p][:], ALU.subtract).then_inc(nmax, 1)
                        dve.wait_ge(nmax, 6 * u + 2 * k + 1)
                        dve.tensor_copy(max_part[k][p][:], neg_max[:]).then_inc(nmax, 1)

            turns(dve, body)
            dve.wait_ge(att, QH * UNITS)


E8 = 8
FF = 176
FT = E8 * FF // P


def ffn1_phase(nc, A, sh, sem, out):
    with ExitStack() as ctx:
        def sb(name, shape, dt=F32):
            return ctx.enter_context(nc.sbuf_tensor(name, shape, dt))

        w_o = sb("f1_wo", [P, KT, DIM])
        b_o = sb("f1_bo", [P, DIM])
        w_r = sb("f1_router", [P, KT, E8])
        w_g = sb("f1_wg", [P, KT, FT * P])
        w_u = sb("f1_wu", [P, KT, FT * P])
        w_d = sb("f1_wd", [P, FT, DIM])
        expand = sb("f1_expand", [E8, FT * P])
        iota = sb("f1_iota", [P, E8])
        att_t = [sb(f"f1_att{w}", [P, KT, P]) for w in range(W)]
        tmp = [sb(f"f1_tmp{w}", [P, DIM]) for w in range(W)]
        h_all = sb("f1_h", [P, KT, W * P])
        logits = sb("f1_logits", [P, W, E8])
        top = sb("f1_top", [P, W, 8])
        idx = sb("f1_idx", [P, W, 8], U32)
        idx_f = sb("f1_idxf", [P, W, 8])
        neg = sb("f1_neg", [P, W])
        wt = sb("f1_wt", [P, 3, W])
        comb = sb("f1_comb", [P, 2, W, E8])
        comb_t = sb("f1_combt", [E8, W * P])
        g_tanh = [sb(f"f1_gt{p}", [P, W * P]) for p in range(2)]
        silu = [sb(f"f1_silu{p}", [P, W * P]) for p in range(2)]
        act_c = [sb(f"f1_c{p}", [P, W * P]) for p in range(2)]
        hid = sb("f1_hid", [P, FT, W * P])
        bank = [ctx.enter_context(nc.psum_tensor(f"f1_b{k}", [P, 512], F32)) for k in range(8)]
        loaded, tr, at_sb, mm_o, ob, og, x3, mm_r, lg, tops, idxs, ng, ex, rt, cb, ct_ps, ct_sb = (
            sem("f1_" + n) for n in ("loaded", "tr", "at_sb", "mm_o", "ob", "og", "x3", "mm_r", "lg", "tops", "idxs", "ng", "ex",
                                     "rt", "cb", "ct_ps", "ct_sb"))
        mm_g, mm_u, mm_c, tanh, sl, ccp, prod, hd, mm_y, yg, x4, stored = (
            sem("f1_" + n) for n in ("mm_g", "mm_u", "mm_c", "tanh", "sl", "ccp", "prod", "hd", "mm_y", "yg", "x4", "stored"))
        S = LnSems(sem, "f1")
        block = ctx.enter_context(nc.Block())
        tiles = [(w, w // B, w % B) for w in range(W)]
        ITS = NT // W

        def xt(c, b, t):
            return t[:, bass.ds(c, 1), b, :].rearrange("p a d -> p (a d)")

        @block.sync
        def _(sp):
            for dst, src in ((w_o[:], A["a_wo"]), (b_o[:], A["a_bo"].to_broadcast([P, DIM])), (w_r[:], A["f1_router"]),
                             (w_g[:], A["f1_wg"]), (w_u[:], A["f1_wu"]), (w_d[:], A["f1_wd"]), (expand[:], A["f1_expand"]),
                             (iota[:], A["f1_iota"])):
                sp.dma_start(dst, src).then_inc(loaded, 16)
            with sp.Fori(0, ITS) as it:
                for w, dc, b in tiles:
                    c = it * (W // B) + dc
                    sp.wait_ge(x4, it * W + w + 1)
                    sp.dma_start(out[b].rearrange("(c p) d -> p c d", p=P)[:, bass.ds(c, 1), :], sh.x[:, bass.ds(c, 1), b, :]).then_inc(stored, 16)
            sp.wait_ge(stored, 16 * NT)

        @block.tensor
        def _(pe):
            pe.wait_ge(loaded, 128)
            ident = sh.masks[:, 0:P]
            with pe.Fori(0, ITS) as it:
                for w, dc, b in tiles:
                    c = it * (W // B) + dc
                    pe.wait_ge(yg, it * 2 * W + w + 1)
                    for k in range(KT):
                        mm = pe.transpose(bank[w][:, k * P:(k + 1) * P], tmp[w][:, k * P:(k + 1) * P], ident)
                    mm.then_inc(tr, 1)
                for w, dc, b in tiles:
                    pe.wait_ge(at_sb, it * W + w + 1)
                    for k in range(KT):
                        mm = pe.matmul(bank[w][:, 256:512], att_t[w][:, k, :], w_o[:, k, :], start=(k == 0), stop=(k == KT - 1))
                    mm.then_inc(mm_o, 1)
                for w in range(W):
                    pe.wait_ge(ob, it * W + w + 1)
                    ln_turn(pe, sh, w, it * W + w, bank[w], S)
                for w in range(W):
                    pe.wait_ge(S.h, it * W + w + 1)
                    for k in range(KT):
                        mm = pe.matmul(bank[w][:, 256:264], h_all[:, k, w * P:(w + 1) * P], w_r[:, k, :], start=(k == 0), stop=(k == KT - 1))
                    mm.then_inc(mm_r, 1)

                def gate_up(f):
                    n = it * FT + f
                    pe.wait_ge(hd, n - 1 if f >= 2 else it * FT)
                    for bk, wts, s in ((4 + f % 2, w_g, mm_g), (6 + f % 2, w_u, mm_u)):
                        for k in range(KT):
                            mm = pe.matmul(bank[bk][:], wts[:, k, f * P:(f + 1) * P], h_all[:, k, :], start=(k == 0), stop=(k == KT - 1))
                        mm.then_inc(s, 1)

                def spread(f):
                    n = it * FT + f
                    pe.wait_ge(ccp, n - 1 if f >= 2 else it * FT)
                    pe.matmul(bank[f % 2][:], expand[:, f * P:(f + 1) * P], comb_t[:], start=True, stop=True).then_inc(mm_c, 1)

                gate_up(0)
                gate_up(1)
                pe.wait_ge(cb, (it + 1) * 2)
                for w in range(W):
                    mm = pe.transpose(bank[0][0:E8, w * P:(w + 1) * P], comb[:, 0, w, :], ident)
                mm.then_inc(ct_ps, 1)
                pe.wait_ge(ct_sb, it + 1)
                for f in range(FT):
                    spread(f)
                    if f >= 2:
                        gate_up(f)
                pe.wait_ge(hd, (it + 1) * FT)
                pe.wait_ge(ccp, (it + 1) * FT)
                for w in range(W):
                    for f in range(FT):
                        mm = pe.matmul(bank[w][:, 0:256], hid[:, f, w * P:(w + 1) * P], w_d[:, f, :], start=(f == 0), stop=(f == FT - 1))
                    mm.then_inc(mm_y, 1)

        @block.scalar
        def _(act):
            act.wait_ge(loaded, 128)
            with act.Fori(0, ITS) as it:
                for w, dc, b in tiles:
                    act.wait_ge(tr, it * W + w + 1)
                    act.activation(att_t[w][:].rearrange("p k t -> p (k t)"), bank[w][:, 0:256], ACT.Copy).then_inc(at_sb, 1)
                for w in range(W):
                    act.wait_ge(mm_r, it * W + w + 1)
                    act.activation(logits[:, w, :], bank[w][:, 256:264], ACT.Copy).then_inc(lg, 1)
                for w in range(W):
                    act.wait_ge(tops, it * W + w + 1)
                    act.activation(neg[:, w:w + 1], top[:, w, 0:1], ACT.Copy, scale=-1.0).then_inc(ng, 1)
                for w in range(W):
                    act.wait_ge(ng, it * W + w + 1)
                    e = act.activation(wt[:, 0, w:w + 1], top[:, w, 1:2], ACT.Exp, bias=neg[:, w:w + 1])
                e.then_inc(ex, 1)

                def tanh_of(f):
                    n = it * FT + f
                    act.wait_ge(mm_g, n + 1)
                    act.activation(g_tanh[f % 2][:], bank[4 + f % 2][:], ACT.Tanh, scale=0.5).then_inc(tanh, 1)

                def spread_copy(f):
                    n = it * FT + f
                    act.wait_ge(mm_c, n + 1)
                    act.wait_ge(hd, n - 1 if f >= 2 else it * FT)
                    act.activation(act_c[f % 2][:], bank[f % 2][:], ACT.Copy, scale=0.5).then_inc(ccp, 1)

                tanh_of(0)
                tanh_of(1)
                act.wait_ge(ct_ps, it + 1)
                act.activation(comb_t[:], bank[0][0:E8, :], ACT.Copy).then_inc(ct_sb, 1)
                for f in range(FT):
                    spread_copy(f)
                    if f >= 2:
                        tanh_of(f)

        @block.gpsimd
        def _(pool):
            with pool.Fori(0, ITS) as it:
                for w in range(W):
                    ln_pool(pool, sh, w, it * W + w, S)
                for f in range(FT):
                    n = it * FT + f
                    pool.wait_ge(sl, n + 1)
                    pool.wait_ge(ccp, n + 1)
                    pool.tensor_tensor(silu[f % 2][:], silu[f % 2][:], act_c[f % 2][:], ALU.mult).then_inc(prod, 1)

        @block.vector
        def _(dve):
            dve.wait_ge(loaded, 128)
            with dve.Fori(0, ITS) as it:
                for w, dc, b in tiles:
                    c = it * (W // B) + dc
                    dve.wait_ge(x4, it * W)
                    dve.tensor_copy(tmp[w][:], sh.att[:, bass.ds(b * CH + c, 1), :].rearrange("p a d -> p (a d)")).then_inc(yg, 1)
                for w, dc, b in tiles:
                    dve.wait_ge(mm_o, it * W + w + 1)
                    dve.tensor_tensor(tmp[w][:], bank[w][:, 256:512], b_o[:], ALU.add).then_inc(ob, 1)
                for w, dc, b in tiles:
                    dve.wait_ge(ob, it * W + w + 1)
                    dve.tensor_tensor(tmp[w][:], tmp[w][:], sh.gate[:, 1, 0, b, :], ALU.mult).then_inc(og, 1)
                for w, dc, b in tiles:
                    c, n = it * (W // B) + dc, it * W + w
                    dve.wait_ge(og, n + 1)
                    dve.tensor_tensor(xt(c, b, sh.x), xt(c, b, sh.x), tmp[w][:], ALU.add).then_inc(x3, 1)
                for w, dc, b in tiles:
                    c, n = it * (W // B) + dc, it * W + w
                    wait_apart(dve, sh, x3, n + 1)
                    ln_vector(dve, sh, w, n, xt(c, b, sh.x), S)
                for w, dc, b in tiles:
                    c, n = it * (W // B) + dc, it * W + w
                    ln_norm(dve, sh, w, n, xt(c, b, sh.x), S)
                for w, dc, b in tiles:
                    ln_modulate(dve, sh, w, it * W + w, bank[w], h_all[:, :, w * P:(w + 1) * P], 1, 1, b, S)
                for w in range(W):
                    wait_apart(dve, sh, lg, it * W + w + 1)
                    dve.max(top[:, w, :], logits[:, w, :]).then_inc(tops, 1)
                for w in range(W):
                    wait_apart(dve, sh, tops, it * W + w + 1)
                    dve.max_index(idx[:, w, :], top[:, w, :], logits[:, w, :]).then_inc(idxs, 1)
                dve.wait_ge(idxs, (it + 1) * W)
                dve.tensor_copy(idx_f[:], idx[:]).then_inc(rt, 1)
                dve.wait_ge(ex, it + 1)
                dve.tensor_scalar(wt[:, 1, :], wt[:, 0, :], 1.0, None, ALU.add).then_inc(rt, 1)
                wait_apart(dve, sh, rt, it * 4 + 2)
                dve.reciprocal(wt[:, 1, :], wt[:, 1, :]).then_inc(rt, 1)
                dve.wait_ge(rt, it * 4 + 3)
                dve.tensor_tensor(wt[:, 2, :], wt[:, 0, :], wt[:, 1, :], ALU.mult).then_inc(rt, 1)
                dve.wait_ge(rt, it * 4 + 4)
                for w in range(W):
                    for j in range(2):
                        ins = dve.tensor_scalar(comb[:, j, w, :], iota[:], idx_f[:, w, j:j + 1], wt[:, 1 + j, w:w + 1],
                                                ALU.is_equal, ALU.mult)
                ins.then_inc(cb, 1)
                dve.wait_ge(cb, it * 2 + 1)
                dve.tensor_tensor(comb[:, 0], comb[:, 0], comb[:, 1], ALU.add).then_inc(cb, 1)
                for f in range(FT + 1):
                    if f < FT:
                        n = it * FT + f
                        dve.wait_ge(tanh, n + 1)
                        dve.wait_ge(hd, n - 1 if f >= 2 else it * FT)
                        dve.scalar_tensor_tensor(silu[f % 2][:], g_tanh[f % 2][:], 1.0, bank[4 + f % 2][:], ALU.add, ALU.mult).then_inc(sl, 1)
                    if f > 0:
                        n = it * FT + f - 1
                        dve.wait_ge(prod, n + 1)
                        dve.wait_ge(mm_u, n + 1)
                        if f == 1:
                            dve.wait_ge(mm_y, it * W)
                        dve.tensor_tensor(hid[:, f - 1, :], bank[6 + (f - 1) % 2][:], silu[(f - 1) % 2][:], ALU.mult).then_inc(hd, 1)
                for w, dc, b in tiles:
                    dve.wait_ge(mm_y, it * W + w + 1)
                    dve.tensor_tensor(tmp[w][:], bank[w][:, 0:256], sh.gate[:, 1, 1, b, :], ALU.mult).then_inc(yg, 1)
                for w, dc, b in tiles:
                    c = it * (W // B) + dc
                    dve.wait_ge(yg, it * 2 * W + W + w + 1)
                    dve.tensor_tensor(xt(c, b, sh.x), xt(c, b, sh.x), tmp[w][:], ALU.add).then_inc(x4, 1)


def build(nc, A, out):
    held = []

    def sem(name):
        held.append(nc.alloc_semaphore(name=name))
        return held[-1]

    def phase_end():
        nc.all_engine_barrier()
        nc.clear_and_free_semaphores(held)
        held.clear()
        nc.all_engine_barrier()

    with ExitStack() as top:
        sh = Shared()

        def sb(name, shape, dt=F32):
            return top.enter_context(nc.sbuf_tensor(name, shape, dt))

        sh.apart = top.enter_context(nc.semaphore("apart"))
        sh.masks = sb("masks_sb", [P, 6 * P])
        sh.mod = sb("mod", [P, 2, 6, KT, B])
        sh.gate = sb("mod_gate", [P, 2, 2, B, DIM])
        sh.pw = sb("pw", [P, 4])
        sh.x = sb("x_res", [P, CH, B, DIM])
        sh.scratch = nc.dram_tensor("qk_rows", (PARTS, 2 * P + 64, B * T), BF16, kind="Internal").ap()
        sh.y = sb("y_res", [P, CH, B, DIM])
        with ExitStack() as first:
            sh.level_masks = first.enter_context(nc.sbuf_tensor("level_masks_sb", [P, LEVELS, 256], I32))
            setup_phase(nc, A, sh, sem)
            sh.h = first.enter_context(nc.sbuf_tensor("h_res", [P, KT, CH * B * P], F32))
            sh.gates = first.enter_context(nc.sbuf_tensor("gates_sb", [P, STEPS, 6, M], F32))
            ln_phase(nc, A, sh, sem)
            phase_end()
            delta_phase(nc, A, sh, sem)
            phase_end()
        sh.stats = [sb(f"stats{w}", [P, 6]) for w in range(W)]
        sh.mean_var = [sb(f"mean_var{w}", [P, 2]) for w in range(W)]
        sh.rstd = [sb(f"rstd{w}", [P, 1]) for w in range(W)]
        sh.normed = [sb(f"normed{w}", [P, DIM]) for w in range(W)]
        sh.v_aug = sb("v_aug", [P, NT, NG, 32])
        ffn0_phase(nc, A, sh, sem)
        sh.att = sb("attended", [P, NT, DIM])
        attention_phase(nc, A, sh, sem)
        ffn1_phase(nc, A, sh, sem, out)


def layouts(inp):
    a = {k: np.ascontiguousarray(v) for k, v in inp.items()}
    d = {k: a[k] for k in ("L0_attn_hidden_states", "L0_attn_W_qkvz", "L0_attn_W_ba", "L0_attn_W_out", "L0_wmod", "L1_wmod")}
    d["c0"] = a["L0_c"].reshape(B, KT, P).transpose(2, 1, 0)
    d["c1"] = a["L1_c"].reshape(B, KT, P).transpose(2, 1, 0)
    d["alog"] = a["L0_attn_A_log"].reshape(1, 2 * HK)
    d["dtb"] = a["L0_attn_dt_bias"].reshape(1, 2 * HK)
    d["norm_w"] = a["L0_attn_norm_weight"].reshape(P, 1)
    w = a["L0_attn_conv_w"]
    q, k, v = w[:2048].reshape(HK, 1, P, 4), w[2048:4096].reshape(HK, 1, P, 4), w[4096:].reshape(HK, RATIO, P, 4)
    d["conv_w"] = np.concatenate([q, k, v], 1).transpose(2, 0, 1, 3).reshape(P, HK * 16)
    rows = lambda m: m.reshape(KT, P, -1).transpose(1, 0, 2)
    d["f0_up"], d["f0_down"] = rows(a["L0_ffn_W_up"].T), rows(a["L0_ffn_W_down"].T)
    d["f0_exp"], d["f0_gate"] = rows(a["L0_ffn_W_expert"]), rows(a["L0_ffn_W_gate"].T)
    d["a_wq"], d["a_wk"], d["a_wv"], d["a_wo"] = (rows(a["L1_attn_W" + n]) for n in "qkvo")
    d["a_bq"] = a["L1_attn_bq"].reshape(KT, P).T
    d["a_bk"] = a["L1_attn_bk"].reshape(64, 1)
    d["a_bv"], d["a_bo"] = a["L1_attn_bv"].reshape(1, 64), a["L1_attn_bo"].reshape(1, DIM)
    d["f1_router"] = rows(a["L1_ffn_gate_w"])
    d["f1_wg"], d["f1_wu"] = (rows(a["L1_ffn_w_" + n].transpose(1, 0, 2).reshape(DIM, E8 * FF)) for n in ("gate", "up"))
    d["f1_wd"] = a["L1_ffn_w_down"].reshape(FT, P, DIM).transpose(1, 0, 2)
    d["f1_expand"] = np.repeat(np.eye(E8, dtype=np.float32), FF, axis=1)
    d["f1_iota"] = np.tile(np.arange(E8, dtype=np.float32), (P, 1))
    i = np.arange(P)
    le = (i[:, None] <= i[None, :]).astype(np.float32)
    sl = (i[:, None] > i[None, :]).astype(np.float32)
    d["masks"] = np.concatenate([np.eye(P, dtype=np.float32), -2 * sl, le * np.float32(P ** -0.5), le, sl,
                                 np.ones((P, P), np.float32)], 1)
    lm = np.zeros((P, LEVELS, M, 64), np.int32)
    for l in range(LEVELS):
        s = 1 << l
        cols = np.array([c for c in range(P) if (c // s) % 2])
        lm[:, l] = ((i[:, None] // (2 * s) == cols[None, :] // (2 * s)) & ((i[:, None] // s) % 2 == 0))[:, None, :]
    d["level_masks"] = lm.reshape(P, LEVELS, 256)
    return {k: np.ascontiguousarray(v) for k, v in d.items()}


def kernel(**inputs):
    import concourse.bacc as bacc
    from concourse.bass_utils import run_bass_kernel_spmd

    nc = bacc.Bacc("TRN2", target_bir_lowering=False, num_devices=1)
    arrays = {"in_" + name: a for name, a in layouts(inputs).items()}
    A = {name[3:]: nc.dram_tensor(name, a.shape, mybir.dt.from_np(a.dtype), kind="ExternalInput").ap() for name, a in arrays.items()}
    out = nc.dram_tensor("out", (B, T, DIM), F32, kind="ExternalOutput").ap()
    build(nc, A, out)
    return run_bass_kernel_spmd(nc, [arrays], core_ids=[0]).results[0]["out"]
```

```python
from contextlib import ExitStack

import numpy as np
import concourse.bass as bass
from concourse import mybir

F32 = mybir.dt.float32
BF16 = mybir.dt.bfloat16
I32 = mybir.dt.int32
U32 = mybir.dt.uint32
ALU = mybir.AluOpType
ACT = mybir.ActivationFunctionType
AX = mybir.AxisListType

P = 128
DIM = 256
KT = DIM // P
B = 2
T = 1024
CH = T // P
HK = 16
RATIO = 2
STEPS = HK * CH
M = B * RATIO
LEVELS = 7
WCOL = 768
QKV = 512
LN_EPS = 1e-5
EPS = 1e-6


def half(x, level, second):
    s = 1 << level
    return x.rearrange("p (q two s) -> p q two s", two=2, s=s)[:, :, int(second), :]


class Shared:
    pass


def wait_apart(eng, sh, s, value):
    eng.wait_ge(s, value)
    eng.sem_inc(sh.apart, 1)


def setup_phase(nc, A, sh, sem):
    with ExitStack() as ctx:
        def sb(name, shape, dt=F32):
            return ctx.enter_context(nc.sbuf_tensor(name, shape, dt))

        wmod = sb("wmod", [P, 2, KT, 6 * DIM])
        c_t = sb("c_t", [P, 2, KT, B])
        c_exp = sb("c_exp", [P, 2 * KT * B])
        c_silu = sb("c_silu", [P, 2, KT, B])
        c_rep = sb("c_rep", [P, 2, KT, B, P])
        sign = sb("sign", [P, 2 * 2 * B * DIM])
        mag = sb("mag", [P, 2 * 2 * B * DIM])
        psum = [ctx.enter_context(nc.psum_tensor(f"mod_ps{k}", [P, 512], F32)) for k in range(5)]
        loaded, c_e, c_s, c_r, mods, gates_ps, gates_sb, done, sgn = (
            sem(n) for n in ("set_loaded", "set_cexp", "set_csilu", "set_crep", "set_mods", "set_gps",
                             "set_gsb", "set_done", "set_sign"))
        block = ctx.enter_context(nc.Block())
        count = [0]

        @block.sync
        def _(sp):
            loads = [
                (c_t[:, 0], A["c0"]), (c_t[:, 1], A["c1"]),
                (wmod[:, 0], A["L0_wmod"].rearrange("(k p) n -> p k n", p=P)),
                (wmod[:, 1], A["L1_wmod"].rearrange("(k p) n -> p k n", p=P)),
                (sh.masks[:], A["masks"]), (sh.level_masks[:], A["level_masks"]),
            ] + [(sh.x[:, :, b], A["L0_attn_hidden_states"][b].rearrange("(c p) d -> p c d", p=P)) for b in range(B)]
            for dst, src in loads:
                sp.dma_start(dst, src).then_inc(loaded, 16)
                count[0] += 16

        n_loaded = 16 * 8

        @block.scalar
        def _(act):
            act.wait_ge(loaded, n_loaded)
            act.activation(c_exp[:], c_t[:].rearrange("p l k b -> p (l k b)"), ACT.Exp, scale=-1.0).then_inc(c_e, 1)

        @block.tensor
        def _(pe):
            pe.wait_ge(loaded, n_loaded)
            pe.wait_ge(c_r, 1)
            for layer in range(2):
                for ct in range(12):
                    for k in range(KT):
                        mm = pe.matmul(psum[0][:, layer * 24 + ct * 2:layer * 24 + ct * 2 + 2],
                                       wmod[:, layer, k, ct * P:(ct + 1) * P], c_silu[:, layer, k, :],
                                       start=(k == 0), stop=(k == KT - 1))
            mm.then_inc(mods, 1)
            for layer in range(2):
                for g, part in enumerate((2, 5)):
                    for b in range(B):
                        for k in range(KT):
                            mm = pe.matmul(psum[1 + layer * 2 + g][:, b * DIM:(b + 1) * DIM], c_rep[:, layer, k, b, :],
                                           wmod[:, layer, k, part * DIM:(part + 1) * DIM],
                                           start=(k == 0), stop=(k == KT - 1))
            mm.then_inc(gates_ps, 1)

        @block.vector
        def _(dve):
            dve.wait_ge(c_e, 1)
            flat = c_t[:].rearrange("p l k b -> p (l k b)")
            dve.tensor_scalar(c_exp[:], c_exp[:], 1.0, None, ALU.add).then_inc(c_s, 1)
            dve.wait_ge(c_s, 1)
            dve.reciprocal(c_exp[:], c_exp[:]).then_inc(c_s, 1)
            dve.wait_ge(c_s, 2)
            dve.tensor_tensor(c_silu[:].rearrange("p l k b -> p (l k b)"), flat, c_exp[:], ALU.mult).then_inc(c_s, 1)
            dve.wait_ge(c_s, 3)
            for layer in range(2):
                for k in range(KT):
                    rep = dve.tensor_copy(c_rep[:, layer, k], c_silu[:, layer, k, :].unsqueeze(2).to_broadcast([P, B, P]))
            rep.then_inc(c_r, 1)
            dve.wait_ge(mods, 1)
            dve.tensor_copy(sh.mod[:], psum[0][:, 0:48].rearrange("p (l s k b) -> p l s k b", l=2, s=6, k=KT)).then_inc(done, 1)
            dve.wait_ge(done, 1)
            for layer in range(2):
                for s in (1, 4):
                    dve.tensor_scalar(sh.mod[:, layer, s], sh.mod[:, layer, s], 1.0, None, ALU.add).then_inc(done, 1)
            dve.wait_ge(gates_ps, 1)
            for n in range(4):
                part = slice(n * 512, (n + 1) * 512)
                dve.tensor_scalar(sign[:, part], psum[1 + n][:], 0.0, 2.0, ALU.is_ge, ALU.mult).then_inc(sgn, 1)
                dve.tensor_copy(mag[:, part], psum[1 + n][:]).then_inc(sgn, 1)
                dve.wait_ge(sgn, 4 * n + 2)
                dve.scalar_tensor_tensor(mag[:, part], mag[:, part], -1.0, mag[:, part], ALU.mult, ALU.max).then_inc(sgn, 1)
                dve.wait_ge(sgn, 4 * n + 3)
                dve.tensor_scalar(mag[:, part], mag[:, part], 0.25, None, ALU.max).then_inc(sgn, 1)
                dve.wait_ge(sgn, 4 * n + 4)
                dve.scalar_tensor_tensor(sh.gate[:].rearrange("p l g b d -> p (l g b d)")[:, part], sign[:, part], -1.0,
                                         mag[:, part], ALU.add, ALU.mult).then_inc(done, 1)
            dve.memset(sh.pw[:, 0:1], -0.5).then_inc(done, 1)
            dve.memset(sh.pw[:, 1:2], LN_EPS).then_inc(done, 1)
            dve.memset(sh.pw[:, 2:3], 4 * EPS).then_inc(done, 1)
            dve.memset(sh.pw[:, 3:4], 4 * EPS * P).then_inc(done, 1)
            dve.wait_ge(done, 13)
            dve.drain()


def ln_phase(nc, A, sh, sem):
    with ExitStack() as ctx:
        def sb(name, shape, dt=F32):
            return ctx.enter_context(nc.sbuf_tensor(name, shape, dt))

        w_ba = sb("w_ba", [P, KT, 4 * HK])
        ba = sb("ba", [P, HK, CH, B, 2, RATIO])
        alog = sb("a_log_sb", [P, HK, RATIO])
        dtb = sb("dt_bias_sb", [P, HK, RATIO])
        stats = [sb(f"ln_stats{b}", [P, 6]) for b in range(B)]
        mean_var = [sb(f"ln_mv{b}", [P, 2]) for b in range(B)]
        rstd = [sb(f"ln_rstd{b}", [P, 1]) for b in range(B)]
        normed = [sb(f"ln_normed{b}", [P, DIM]) for b in range(B)]
        h_tile = [sb(f"ln_htile{b}", [P, KT, P]) for b in range(B)]
        NG = STEPS * M
        work = [sb(f"gate_work{k}", [P, NG]) for k in range(4)]
        g_flat = sb("g_flat", [P, NG])
        tr_ps = [ctx.enter_context(nc.psum_tensor(f"ln_tr{b}", [P, 512], F32)) for b in range(B)]
        ba_ps = [ctx.enter_context(nc.psum_tensor(f"ln_ba{b}", [P, 512], F32)) for b in range(B)]
        cum_ps = [ctx.enter_context(nc.psum_tensor(f"cum_ps{k}", [P, 512], F32)) for k in range(3)]
        (loaded, st, mv, veps, rs, nm, tr, ht, ba_mm, ba_sb, neg, vec, cum, ex) = (
            sem(n) for n in ("ln_loaded", "ln_st", "ln_mvs", "ln_veps", "ln_rs", "ln_nm", "ln_trs", "ln_ht",
                             "ln_bamm", "ln_basb", "gt_neg", "gt_vec", "gt_cum", "gt_exp"))
        h_out = [sem(f"ln_hout{b}") for b in range(B)]
        ident = sh.masks[:, 0:P]
        block = ctx.enter_context(nc.Block())

        @block.sync
        def _(sp):
            sp.dma_start(w_ba[:], A["L0_attn_W_ba"].rearrange("(k p) n -> p k n", p=P)).then_inc(loaded, 16)
            sp.dma_start(alog[:].rearrange("p a b -> p (a b)"), A["alog"].to_broadcast([P, 2 * HK])).then_inc(loaded, 16)
            sp.dma_start(dtb[:].rearrange("p a b -> p (a b)"), A["dtb"].to_broadcast([P, 2 * HK])).then_inc(loaded, 16)
            with sp.Fori(0, CH) as c:
                for b in range(B):
                    sp.wait_ge(ht, c * 4 + 2 * b + 2)
                    sp.dma_start(sh.h[:, :, bass.ds((c * B + b) * P, P)], h_tile[b][:]).then_inc(h_out[b], 16)
            for b in range(B):
                sp.wait_ge(h_out[b], 16 * CH)

        @block.vector
        def _(dve):
            with dve.Fori(0, CH) as c:
                for b in range(B):
                    n = c * B + b
                    xt = sh.x[:, bass.ds(c, 1), b, :]
                    dve.bn_stats(stats[b][:], xt).then_inc(st, 1)
                    wait_apart(dve, sh, st, n + 1)
                    dve.bn_aggr(mean_var[b][:], stats[b][:]).then_inc(mv, 1)
                for b in range(B):
                    n = c * B + b
                    xt = sh.x[:, bass.ds(c, 1), b, :]
                    dve.wait_ge(rs, n + 1)
                    dve.tensor_scalar(normed[b][:], xt, mean_var[b][:, 0:1], rstd[b][:],
                                      ALU.subtract, ALU.mult).then_inc(nm, 1)
                for b in range(B):
                    n = c * B + b
                    dve.wait_ge(tr, n + 1)
                    dve.wait_ge(h_out[b], c * 16)
                    dve.wait_ge(ba_mm, n - b)
                    for k in range(KT):
                        dve.tensor_scalar(h_tile[b][:, k, :], tr_ps[b][:, k * P:(k + 1) * P], sh.mod[:, 0, 1, k, b:b + 1],
                                          sh.mod[:, 0, 0, k, b:b + 1], ALU.mult, ALU.add).then_inc(ht, 1)
            dve.wait_ge(ba_sb, CH * B)
            dve.wait_ge(loaded, 48)
            bv = ba[:, :, :, :, 0, :].rearrange("p h c b r -> p (h c b) r")
            G = sh.gates[:].rearrange("p s q m -> p s (q m)")
            k = [0]

            def link(ins):
                k[0] += 1
                ins.then_inc(vec, 1)
                dve.wait_ge(vec, k[0])

            w0, w1, w2, w3 = (w[:] for w in work)
            hbr = lambda w: w.rearrange("p (h q r) -> p h q r", h=HK, r=RATIO)
            dve.wait_ge(neg, 1)
            link(dve.tensor_scalar(w0, w0, 1.0, None, ALU.add))
            link(dve.reciprocal(w0, w0))
            link(dve.tensor_scalar(G[:, :, 0:4], w0.rearrange("p (s m) -> p s m", m=M), 0.5, None, ALU.mult))
            for kh in range(HK):
                ins = dve.tensor_tensor(hbr(w1)[:, kh], ba[:, kh, :, :, 1, :].rearrange("p c b r -> p (c b) r"),
                                        dtb[:, kh:kh + 1, :].to_broadcast([P, CH * B, RATIO]), ALU.add)
            link(ins)
            link(dve.scalar_tensor_tensor(w2, w1, -1.0, w1, ALU.mult, ALU.min))
            dve.wait_ge(neg, 2)
            link(dve.tensor_scalar(w3, w2, 2.0, None, ALU.add))
            link(dve.reciprocal(w3, w3))
            link(dve.tensor_tensor(w3, w3, w2, ALU.mult))
            link(dve.tensor_tensor(w2, w3, w3, ALU.mult))
            link(dve.tensor_scalar(w0, w2, 1.0 / 19, 1.0 / 17, ALU.mult, ALU.add))
            for d in (15, 13, 11, 9, 7, 5, 3, 1):
                link(dve.tensor_tensor(w0, w0, w2, ALU.mult))
                link(dve.tensor_scalar(w0, w0, 1.0 / d, None, ALU.add))
            link(dve.tensor_tensor(w0, w0, w3, ALU.mult))
            link(dve.tensor_scalar(w1, w1, 0.0, None, ALU.max))
            link(dve.scalar_tensor_tensor(w0, w0, 2.0, w1, ALU.mult, ALU.add))
            for kh in range(HK):
                ins = dve.scalar_tensor_tensor(hbr(g_flat[:])[:, kh], hbr(w0)[:, kh], -1.0,
                                               alog[:, kh:kh + 1, :].to_broadcast([P, CH * B, RATIO]), ALU.mult, ALU.mult)
            link(ins)
            link(dve.tensor_copy(G[:, :, 4:8], g_flat[:].rearrange("p (s m) -> p s m", m=M)))
            dve.wait_ge(ex, 3)
            e = lambda w: w.rearrange("p (s m) -> p s m", m=M)
            link(dve.tensor_scalar(G[:, :, 8:12], e(w1), -2.0, None, ALU.mult))
            link(dve.tensor_scalar(G[:, :, 12:16], e(w1), float(P) ** -0.5, None, ALU.mult))
            link(dve.tensor_copy(G[:, :, 16:20], e(w2)))
            link(dve.tensor_copy(G[:, :, 20:24], e(w3)))
            link(dve.memset(sh.gates[:].rearrange("p (h c) q m -> p h c (q m)", c=CH)[:, :, CH - 1, 16:24], 0.0))

        @block.gpsimd
        def _(pool):
            with pool.Fori(0, CH) as c:
                for b in range(B):
                    n = c * B + b
                    pool.wait_ge(mv, n + 1)
                    pool.tensor_tensor(rstd[b][:], mean_var[b][:, 1:2], sh.pw[:, 1:2], ALU.add).then_inc(veps, 1)
                    pool.wait_ge(veps, n + 1)
                    pool.tensor_tensor(rstd[b][:], rstd[b][:], sh.pw[:, 0:1], ALU.pow).then_inc(rs, 1)

        @block.tensor
        def _(pe):
            pe.wait_ge(loaded, 48)
            with pe.Fori(0, CH) as c:
                for b in range(B):
                    n = c * B + b
                    pe.wait_ge(nm, n + 1)
                    pe.wait_ge(ht, c * 4)
                    for k in range(KT):
                        mm = pe.transpose(tr_ps[b][:, k * P:(k + 1) * P], normed[b][:, k * P:(k + 1) * P], ident)
                    mm.then_inc(tr, 1)
                for b in range(B):
                    n = c * B + b
                    pe.wait_ge(ht, c * 4 + 2 * b + 2)
                    pe.wait_ge(ba_sb, n - b)
                    for k in range(KT):
                        mm = pe.matmul(ba_ps[b][:, 0:4 * HK], h_tile[b][:, k, :], w_ba[:, k, :],
                                       start=(k == 0), stop=(k == KT - 1))
                    mm.then_inc(ba_mm, 1)
            pe.wait_ge(vec, 30)
            for k, lhs in enumerate((sh.masks[:, 3 * P:4 * P], sh.masks[:, 4 * P:5 * P], sh.masks[:, 5 * P:6 * P])):
                pe.matmul(cum_ps[k][:], lhs, g_flat[:], start=True, stop=True).then_inc(cum, 1)

        @block.scalar
        def _(act):
            with act.Fori(0, CH) as c:
                for b in range(B):
                    act.wait_ge(ba_mm, c * B + b + 1)
                    act.activation(ba[:].rearrange("p h c b q r -> p h c b (q r)")[:, :, bass.ds(c, 1), b, :],
                                   ba_ps[b][:, 0:4 * HK].rearrange("p (h q) -> p h q", h=HK).unsqueeze(2),
                                   ACT.Copy).then_inc(ba_sb, 1)
            act.wait_ge(ba_sb, CH * B)
            act.activation(work[0][:].rearrange("p (s r) -> p s r", r=RATIO),
                           ba[:, :, :, :, 0, :].rearrange("p h c b r -> p (h c b) r"), ACT.Exp, scale=-1.0).then_inc(neg, 1)
            act.wait_ge(loaded, 48)
            act.wait_ge(vec, 5)
            act.activation(work[2][:], work[2][:], ACT.Exp)
            act.activation(alog[:], alog[:], ACT.Exp).then_inc(neg, 1)
            act.wait_ge(vec, 30)
            for k in range(3):
                act.wait_ge(cum, k + 1)
                act.activation(work[1 + k][:], cum_ps[k][:], ACT.Exp).then_inc(ex, 1)


def delta_phase(nc, A, sh, sem):
    with ExitStack() as ctx:
        def sb(name, shape, dt=F32):
            return ctx.enter_context(nc.sbuf_tensor(name, shape, dt))

        raw = sb("raw", [P, 4, B, T + 3])
        w_qkv = sb("w_qkv", [P, KT, QKV])
        w_z = sb("w_z", [P, KT, RATIO * P])
        w_out = sb("w_out", [P, 2, RATIO * DIM])
        norm_w = sb("norm_w_sb", [P, 1])
        h_in = [sb(f"h_in{p}", [P, KT, B, P]) for p in range(2)]
        gate = [sb(f"gate_in{p}", [P, 6, B, RATIO]) for p in range(2)]
        taps = [sb(f"taps{p}", [P, 4, 4]) for p in range(2)]
        conv = sb("conv", [P, 4, B, P])
        qkv = [sb(f"qkv{p}", [P, 4, B, P]) for p in range(2)]
        squares = sb("squares", [P, 2, B, P])
        rnorm = [sb(f"rnorm{p}", [P, 2, B]) for p in range(2)]
        beta_r = [sb(f"beta_r{p}", [P, B, RATIO]) for p in range(2)]
        beta_r2 = [sb(f"beta_r2{p}", [P, B, RATIO]) for p in range(2)]
        ks_scale = [sb(f"ks_scale{p}", [P, B, RATIO]) for p in range(2)]
        qs_scale = [sb(f"qs_scale{p}", [P, B, RATIO]) for p in range(2)]
        g_below = sb("g_below", [P, M, P])
        decay = sb("decay", [P, M, P])
        kkq = sb("kkq", [P, 2, B, P])
        m_neg = [sb(f"m_neg{p}", [P, M, P]) for p in range(2)]
        a_t = [sb(f"a_t{p}", [P, B, RATIO, P]) for p in range(2)]
        z_neg = [sb(f"z_neg{l}", [P, M * P]) for l in range(LEVELS)]
        r_inv = [sb(f"r_inv{p}", [P, M * P]) for p in range(2)]
        t_inv = [sb(f"t_inv{p}", [P, M * P]) for p in range(2)]
        k_norms = sb("k_norms", [P, B * P + 2 * B])
        k_tok = k_norms[:, 0:B * P].rearrange("p (b d) -> p b d", b=B)
        norms = k_norms[:, B * P:]
        k_dec = [sb(f"k_dec{p}", [P, B, RATIO, P]) for p in range(2)]
        v_beta = sb("v_beta", [P, M, P])
        rhs = sb("rhs", [P, M, P])
        u = sb("u", [P, M, P])
        qs = sb("qs", [P, M, P])
        state = sb("state", [P, B, RATIO, P])
        o = sb("o", [P, M, P])
        z_tanh = sb("z_tanh", [P, M * P])
        z_silu = [sb(f"z_silu{p}", [P, M * P]) for p in range(2)]
        gated = sb("gated", [P, M * P])
        gated_sq = sb("gated_sq", [P, M, P])
        o_norm = sb("o_norm", [P, M])
        o_rnorm = sb("o_rnorm", [P, M])
        scaled = sb("scaled", [P, M, P])
        o_t = sb("o_t", [P, M, P])
        bank = [ctx.enter_context(nc.psum_tensor(f"bank{k}", [P, 512], F32)) for k in range(8)]
        y = sh.y

        ident = sh.masks[:, 0:P]
        below = sh.masks[:, 3 * P + P:5 * P]
        upto = sh.masks[:, 3 * P:4 * P]
        kkq_mask = sh.masks[:, P:3 * P].rearrange("p (a n) -> p a n", a=2)
        ones = sh.masks[:, 5 * P:5 * P + 1]

        ld_const, ld_wqkv, ld_wz, ld_wout = (sem(n) for n in ("ld_const", "ld_wqkv", "ld_wz", "ld_wout"))
        ld_h, ld_taps, ld_gate = ([sem(f"{n}{p}") for p in range(2)] for n in ("ld_h", "ld_taps", "ld_gate"))
        (pe_proj, pe_z, pe_kkq, pe_dd, pe_v, pe_k, pe_dt, pe_lev_e, pe_lev_l, pe_inv_e, pe_inv_l, pe_ks, pe_qs, pe_u,
         pe_s, pe_o, pe_xt, pe_y) = (
            sem("pe_" + n) for n in ("proj", "z", "kkq", "dd", "v", "k", "dt", "lev_e", "lev_l", "inv_e", "inv_l", "ks",
                                     "qs", "u", "s", "o", "xt", "y"))
        act_raw, act_conv, act_dec, act_k, act_t_e, act_t_l, act_r_e, act_r_l, act_u, act_z, act_xt = (
            sem("act_" + n) for n in ("raw", "conv", "dec", "k", "t_e", "t_l", "r_e", "r_l", "u", "z", "xt"))
        (dve_conv, dve_qkv, dve_kkq, dve_m, dve_v, dve_a, dve_z_e, dve_z_l, dve_rhs, dve_qs, dve_s, dve_o, dve_zs,
         dve_red, dve_y, dve_init) = (
            sem("dve_" + n) for n in ("conv", "qkv", "kkq", "m", "v", "a", "z_e", "z_l", "rhs", "qs", "s", "o", "zs",
                                      "red", "y", "init"))
        (pl_sq, pl_rn, pl_sc, pl_g, pl_r, pl_kd, pl_gt, pl_gsq, pl_on, pl_x) = (
            sem(n) for n in ("pl_sq", "pl_rn", "pl_sc", "pl_g", "pl_r", "pl_kd", "pl_gt", "pl_gsq", "pl_on", "pl_x"))
        block = ctx.enter_context(nc.Block())

        def turns(eng, body):
            body(0, 0, True, True, False, False)
            body(1, 1, True, True, True, False)
            with eng.Fori(0, (STEPS - 4) // 2) as j:
                body(j * 2 + 2, 0, True, True, True, True)
                body(j * 2 + 3, 1, True, True, True, True)
            body(STEPS - 2, 0, True, True, True, True)
            body(STEPS - 1, 1, False, True, True, True)
            body(STEPS, 0, False, False, True, True)
            body(STEPS + 1, 1, False, False, False, True)

        @block.sync
        def _(sp):
            sp.dma_start(norm_w[:], A["norm_w"]).then_inc(ld_const, 16)

            def chunk(step, kh, c, p, first):
                if not first:
                    sp.wait_ge(pe_z, step - 1)
                sp.dma_start(h_in[p][:], sh.h[:, :, bass.ds(c * (B * P), B * P)].rearrange("p k (b t) -> p k b t", b=B)).then_inc(ld_h[p], 16)
                if not first:
                    sp.wait_ge(dve_conv, (step - 1) * 16)
                sp.dma_start(taps[p][:].rearrange("p a b -> p (a b)"), A["conv_w"][:, bass.ds(kh * 16, 16)]).then_inc(ld_taps[p], 16)
                if not first:
                    sp.wait_ge(dve_s, step - 1)
                    sp.wait_ge(pl_kd, step - 1)
                sp.dma_start(gate[p][:].rearrange("p q b r -> p (q b r)"),
                             sh.gates[:, bass.ds(step, 1)].rearrange("p s q m -> p (s q m)")).then_inc(ld_gate[p], 16)

            def weights(kh, first):
                src = A["L0_attn_W_qkvz"].rearrange("(k p) n -> p k n", p=P)
                if not first:
                    sp.wait_ge(pe_proj, 4 * CH * kh)
                sp.dma_start(w_qkv[:], src[:, :, bass.ds(kh * WCOL, QKV)]).then_inc(ld_wqkv, 16)

            def weights_z(kh, first):
                src = A["L0_attn_W_qkvz"].rearrange("(k p) n -> p k n", p=P)
                if not first:
                    sp.wait_ge(pe_z, CH * kh)
                sp.dma_start(w_z[:], src[:, :, bass.ds(kh * WCOL + QKV, RATIO * P)]).then_inc(ld_wz, 16)

            def weights_out(kh, first):
                src = A["L0_attn_W_out"].rearrange("(h r e) n -> e h r n", e=P, r=RATIO)
                if not first:
                    sp.wait_ge(pe_y, CH * (kh - 1))
                sp.dma_start(w_out[:, bass.ds(kh % 2, 1)].rearrange("p a (r n) -> p (a r) n", r=RATIO),
                             src[:, bass.ds(kh, 1)].rearrange("p a r n -> p (a r) n")).then_inc(ld_wout, 16)

            weights(0, True)
            weights_z(0, True)
            weights_out(0, True)
            for c in range(CH):
                chunk(c, 0, c, c % 2, c < 2)
            with sp.Fori(1, HK) as kh:
                weights(kh, False)
                chunk(kh * CH, kh, 0, 0, False)
                weights_z(kh, False)
                weights_out(kh, False)
                with sp.Fori(0, CH // 2 - 1) as cc:
                    chunk(kh * CH + cc * 2 + 1, kh, cc * 2 + 1, 1, False)
                    chunk(kh * CH + cc * 2 + 2, kh, cc * 2 + 2, 0, False)
                chunk(kh * CH + CH - 1, kh, CH - 1, 1, False)

        EARLY, LATE = 4, LEVELS - 4
        cols = lambda m: slice(m * P, (m + 1) * P)

        @block.tensor
        def _(pe):
            def project(i, p, ct):
                j = ct // 2
                if ct == 0:
                    pe.wait_ge(ld_h[p], 16 * (i // 2 + 1))
                    pe.wait_ge(ld_wqkv, weights_count(i))
                out = bank[j][:, (ct % 2) * B * P:(ct % 2 + 1) * B * P]
                for k in range(KT):
                    mm = pe.matmul(out, w_qkv[:, k, ct * P:(ct + 1) * P], h_in[p][:, k].rearrange("p b t -> p (b t)"),
                                   start=(k == 0), stop=(k == KT - 1))
                mm.then_inc(pe_proj, 1)

            def weights_count(i):
                return 16 * (i // CH + 1)

            def body(i, p, nxt, cur, prev, prev2):
                q = 1 - p

                def level(l, n, done):
                    src = z_neg[0] if l == 1 else r_inv[n]
                    for m in range(M):
                        mm = pe.matmul(bank[6][:, m * 64:(m + 1) * 64], m_neg[n][:, m, :],
                                       half(src[:, cols(m)], l, True), start=True, stop=True)
                    mm.then_inc(done, 1)

                def grow(l, n, done):
                    for m in range(M):
                        mm = pe.matmul(bank[7][:, m * 64:(m + 1) * 64], t_inv[n][:, cols(m)],
                                       half(z_neg[l][:, cols(m)], l, True), start=True, stop=True)
                    if l < LEVELS - 1:
                        for m in range(M):
                            mm = pe.matmul(bank[7][:, 256 + m * 64:256 + (m + 1) * 64], z_neg[l][:, cols(m)],
                                           half(t_inv[n][:, cols(m)], l, False), start=True, stop=True)
                    mm.then_inc(done, 1)

                def level_early(l):
                    pe.wait_ge(dve_z_e, EARLY * i + l)
                    if l > 1:
                        pe.wait_ge(act_r_e, (EARLY - 1) * i + l - 1)
                    if l == 2:
                        pe.wait_ge(pl_r, i + 1)
                    if prev and l < EARLY - 1:
                        pe.wait_ge(dve_z_l, LATE * (i - 1) + l + 1)
                    level(l, p, pe_lev_e)

                def grow_early(l):
                    pe.wait_ge(act_t_e, EARLY * i + l)
                    pe.wait_ge(dve_z_e, EARLY * i + l + 1)
                    if prev and l == 1:
                        pe.wait_ge(act_t_l, (LATE - 1) * i)
                    if prev and l == 2:
                        pe.wait_ge(act_r_l, LATE * i)
                    grow(l, p, pe_inv_e)

                def level_late(l):
                    k = l - EARLY
                    if k == 0:
                        pe.wait_ge(act_r_e, (EARLY - 1) * i)
                        pe.wait_ge(dve_z_e, EARLY * i)
                    else:
                        pe.wait_ge(act_r_l, LATE * (i - 1) + k)
                        if cur:
                            pe.wait_ge(dve_z_e, EARLY * i + k)
                    level(l, q, pe_lev_l)

                def grow_late(l):
                    k = l - EARLY
                    pe.wait_ge(dve_z_l, LATE * (i - 1) + k + 1)
                    if k == 0:
                        pe.wait_ge(act_t_e, EARLY * i)
                        if cur:
                            pe.wait_ge(act_dec, i + 1)
                    else:
                        pe.wait_ge(act_t_l, (LATE - 1) * (i - 1) + k)
                        if cur:
                            pe.wait_ge(act_t_e, EARLY * i + k)
                    grow(l, q, pe_inv_l)

                kt = lambda pp, b: qkv[pp][:, 1, b, :]
                qt = lambda pp, b: qkv[pp][:, 0, b, :]
                if not prev and not prev2:
                    pe.wait_ge(ld_const, 16)
                    for ct in range(4):
                        project(0, 0, ct)
                def keys_state():
                    if prev2:
                        pe.wait_ge(dve_s, i - 1)
                    if cur:
                        pe.wait_ge(act_raw, 2 * i + 1)
                    for b in range(B):
                        mm = pe.matmul(bank[0][:, b * 256:(b + 1) * 256], kt(q, b), state[:, b].rearrange("p r e -> p (r e)"),
                                       start=True, stop=True)
                    mm.then_inc(pe_ks, 1)
                    if cur:
                        pe.wait_ge(act_raw, 2 * i + 2)
                    for b in range(B):
                        mm = pe.matmul(bank[1][:, b * 256:(b + 1) * 256], qt(q, b), state[:, b].rearrange("p r e -> p (r e)"),
                                       start=True, stop=True)
                    mm.then_inc(pe_qs, 1)

                def exponents():
                    pe.wait_ge(pl_g, i + 1)
                    if prev:
                        pe.wait_ge(act_t_e, EARLY * i)
                        pe.wait_ge(act_r_e, (EARLY - 1) * i)
                    pe.matmul(bank[7][:], upto, g_below[:].rearrange("p m s -> p (m s)"), start=True, stop=True).then_inc(pe_dd, 1)

                def project_z():
                    pe.wait_ge(ld_wz, weights_count(i))
                    if not prev:
                        pe.wait_ge(ld_h[p], 16)
                    else:
                        pe.wait_ge(dve_zs, i)
                    for b in range(B):
                        for k in range(KT):
                            mm = pe.matmul(bank[2][:, b * 256:(b + 1) * 256], h_in[p][:, k, b, :], w_z[:, k, :],
                                           start=(k == 0), stop=(k == KT - 1))
                    mm.then_inc(pe_z, 1)

                def keys_tokens():
                    pe.wait_ge(dve_qkv, 2 * i + 1)
                    if prev2:
                        pe.wait_ge(dve_s, i - 1)
                    for b in range(B):
                        pe.transpose(bank[4][:, b * P:(b + 1) * P], kt(p, b), ident)
                    pe.wait_ge(pl_sq, i + 1)
                    for a in range(2):
                        for b in range(B):
                            mm = pe.matmul(bank[4][:, 256 + a * B + b:257 + a * B + b], squares[:, a, b, :], ones,
                                           start=True, stop=True)
                    mm.then_inc(pe_k, 1)

                def keys_keys():
                    if prev2:
                        pe.wait_ge(dve_o, i - 1)
                    for b in range(B):
                        pe.matmul(bank[5][:, b * P:(b + 1) * P], kt(p, b), kt(p, b), start=True, stop=True)
                    for b in range(B):
                        mm = pe.matmul(bank[5][:, (B + b) * P:(B + b + 1) * P], kt(p, b), qt(p, b), start=True, stop=True)
                    mm.then_inc(pe_kkq, 1)

                def turn_decay():
                    pe.wait_ge(act_dec, i + 1)
                    pe.wait_ge(dve_kkq, i + 1)
                    for m in range(M):
                        mm = pe.transpose(bank[5][:, cols(m)], decay[:, m, :], ident)
                    mm.then_inc(pe_dt, 1)

                def turn_m():
                    pe.wait_ge(dve_m, i + 1)
                    if prev:
                        pe.wait_ge(dve_z_l, LATE * (i - 1) + 1)
                    for m in range(M):
                        mm = pe.transpose(bank[6][:, cols(m)], m_neg[p][:, m, :], ident)
                    mm.then_inc(pe_lev_e, 1)

                def turn_blocks():
                    pe.wait_ge(dve_z_e, EARLY * i + 1)
                    if prev:
                        pe.wait_ge(act_t_l, (LATE - 1) * (i - 1) + 1)
                    for m in range(M):
                        mm = pe.transpose(bank[7][:, cols(m)], z_neg[0][:, cols(m)], ident)
                    mm.then_inc(pe_inv_e, 1)

                def turn_v():
                    pe.wait_ge(dve_qkv, 2 * i + 2)
                    if prev2:
                        pe.wait_ge(act_u, i - 1)
                        pe.wait_ge(dve_y, i - 1)
                    elif prev:
                        pe.wait_ge(dve_v, i)
                    for m in range(M):
                        mm = pe.transpose(bank[3][:, cols(m)], qkv[p][:, 2 + m % RATIO, m // RATIO, :], ident)
                    mm.then_inc(pe_v, 1)

                def updates():
                    pe.wait_ge(dve_rhs, i)
                    pe.wait_ge(act_r_l, LATE * i)
                    if cur:
                        pe.wait_ge(dve_v, i + 1)
                    else:
                        pe.wait_ge(dve_y, i - 1)
                    for m in range(M):
                        mm = pe.matmul(bank[3][:, cols(m)], r_inv[q][:, cols(m)], rhs[:, m, :], start=True, stop=True)
                    mm.then_inc(pe_u, 1)

                def state_update():
                    pe.wait_ge(act_u, i)
                    pe.wait_ge(pl_kd, i)
                    if cur:
                        pe.wait_ge(act_k, i + 1)
                    for m in range(M):
                        mm = pe.matmul(bank[4][:, cols(m)], k_dec[q][:, m // RATIO, m % RATIO, :], u[:, m, :],
                                       start=True, stop=True)
                    mm.then_inc(pe_s, 1)

                def attend():
                    if cur:
                        pe.wait_ge(dve_a, i + 1)
                    for m in range(M):
                        mm = pe.matmul(bank[5][:, cols(m)], a_t[q][:, m // RATIO, m % RATIO, :], u[:, m, :],
                                       start=True, stop=True)
                    mm.then_inc(pe_o, 1)

                def turn_output():
                    pe.wait_ge(pl_x, i - 1)
                    if cur:
                        pe.wait_ge(dve_zs, i + 1)
                    for m in range(M):
                        mm = pe.transpose(bank[2][:, cols(m)], scaled[:, m, :], ident)
                    mm.then_inc(pe_xt, 1)

                def project_output():
                    pe.wait_ge(act_xt, i - 1)
                    if prev:
                        pe.wait_ge(act_u, i)
                    else:
                        pe.wait_ge(dve_y, i - 1)
                    kh = (i - 2) // CH
                    pe.wait_ge(ld_wout, 16 * (kh + 1))
                    for b in range(B):
                        for r in range(RATIO):
                            mm = pe.matmul(bank[3][:, b * 256:(b + 1) * 256], o_t[:, b * RATIO + r, :],
                                           w_out[:, bass.ds(kh % 2, 1), r * DIM:(r + 1) * DIM].rearrange("p a n -> p (a n)"),
                                           start=(r == 0), stop=(r == RATIO - 1))
                    mm.then_inc(pe_y, 1)

                def project_next(ct):
                    if ct == 0:
                        pe.wait_ge(*((dve_rhs, i) if prev else (act_raw, 1)))
                    if ct == 2:
                        pe.wait_ge(*((dve_qs, i) if prev else (act_raw, 2)))
                    project(i + 1, q, ct)

                if prev:
                    keys_state()
                    level_late(4)
                if cur:
                    keys_tokens()
                    keys_keys()
                    exponents()
                    project_z()
                if prev:
                    grow_late(4)
                if cur:
                    turn_decay()
                    turn_m()
                if nxt:
                    project_next(0)
                if prev:
                    level_late(5)
                if cur:
                    turn_blocks()
                if nxt:
                    project_next(1)
                if prev:
                    grow_late(5)
                if cur:
                    level_early(1)
                if nxt:
                    project_next(2)
                if prev:
                    level_late(6)
                if cur:
                    grow_early(1)
                    turn_v()
                if prev:
                    grow_late(6)
                if cur:
                    level_early(2)
                if nxt:
                    project_next(3)
                if prev:
                    updates()
                if cur:
                    grow_early(2)
                if prev:
                    state_update()
                if prev2:
                    turn_output()
                if cur:
                    level_early(3)
                if prev:
                    attend()
                if prev2:
                    project_output()
                if cur:
                    grow_early(3)

            turns(pe, body)

        @block.scalar
        def _(act):
            def raw_copy(i, j):
                act.wait_ge(pe_proj, 4 * i + 2 * j + 2)
                c = i % CH
                for a in range(2):
                    mm = act.activation(raw[:, 2 * j + a, :, bass.ds(c * P + 3, P)],
                                        bank[j][:, a * 256:(a + 1) * 256].rearrange("p (b t) -> p b t", b=B), ACT.Copy)
                mm.then_inc(act_raw, 1)

            def conv_tanh(i, p, j):
                act.wait_ge(dve_conv, 16 * i + 8 * j + 8)
                act.activation(qkv[p][:, 2 * j:2 * j + 2].rearrange("p a b t -> p (a b t)"),
                               conv[:, 2 * j:2 * j + 2].rearrange("p a b t -> p (a b t)"), ACT.Tanh, scale=0.5).then_inc(act_conv, 1)

            def inverse(l, n, r_done, t_done):
                act.activation(half(r_inv[n][:], l, True), bank[7][:, 0:256].rearrange("p (q s) -> p q s", s=1 << l),
                               ACT.Copy).then_inc(r_done, 1)
                if l < LEVELS - 1:
                    act.activation(half(t_inv[n][:], l, False), bank[7][:, 256:512].rearrange("p (q s) -> p q s", s=1 << l),
                                   ACT.Copy).then_inc(t_done, 1)

            def body(i, p, nxt, cur, prev, prev2):
                q = 1 - p

                def early(l):
                    act.wait_ge(pe_inv_e, EARLY * i + l + 1)
                    inverse(l, p, act_r_e, act_t_e)

                def late(l):
                    act.wait_ge(pe_inv_l, LATE * (i - 1) + l - EARLY + 1)
                    inverse(l, q, act_r_l, act_t_l)

                if not prev and not prev2:
                    act.wait_ge(ld_const, 16)
                    act.wait_ge(dve_init, 1)
                    for j in range(2):
                        raw_copy(0, j)
                    conv_tanh(0, 0, 0)
                    conv_tanh(0, 0, 1)
                if cur:
                    act.wait_ge(pe_k, i + 1)
                    if prev:
                        act.wait_ge(pl_kd, i)
                    act.activation(k_norms[:], bank[4][:, 0:B * P + 2 * B], ACT.Copy).then_inc(act_k, 1)
                    act.wait_ge(pe_dd, i + 1)
                    act.activation(decay[:].rearrange("p m s -> p (m s)"), bank[7][:], ACT.Exp).then_inc(act_dec, 1)
                    act.wait_ge(pe_z, i + 1)
                    act.activation(z_tanh[:], bank[2][:], ACT.Tanh, scale=0.5).then_inc(act_z, 1)
                if prev:
                    late(4)
                if cur:
                    act.wait_ge(pe_inv_e, EARLY * i + 1)
                    act.activation(t_inv[p][:], bank[7][:], ACT.Copy).then_inc(act_t_e, 1)
                if nxt:
                    raw_copy(i + 1, 0)
                if prev:
                    late(5)
                if cur:
                    early(1)
                if prev:
                    late(6)
                if nxt:
                    raw_copy(i + 1, 1)
                if prev:
                    act.wait_ge(pe_u, i)
                    act.activation(u[:].rearrange("p m e -> p (m e)"), bank[3][:], ACT.Copy).then_inc(act_u, 1)
                if cur:
                    early(2)
                if nxt:
                    conv_tanh(i + 1, q, 0)
                if prev2:
                    act.wait_ge(pe_xt, i - 1)
                    act.activation(o_t[:].rearrange("p m t -> p (m t)"), bank[2][:], ACT.Copy, scale=norm_w[:]).then_inc(act_xt, 1)
                if nxt:
                    conv_tanh(i + 1, q, 1)
                if cur:
                    early(3)

            turns(act, body)

        @block.vector
        def _(dve):
            def convolve(i, p, j, taps_now):
                c = i % CH
                if 0 in taps_now:
                    dve.wait_ge(act_raw, 2 * i + j + 1)
                    if j == 0:
                        dve.wait_ge(ld_taps[p], 16 * (i // 2 + 1))
                for tap in taps_now:
                    for a in range(2):
                        n = 8 * j + 2 * tap + a
                        src = raw[:, 2 * j + a, :, bass.ds(c * P + tap, P)]
                        dst = conv[:, 2 * j + a]
                        w = taps[p][:, 2 * j + a, tap:tap + 1]
                        if tap == 0:
                            dve.tensor_scalar(dst, src, w, None, ALU.mult).then_inc(dve_conv, 1)
                        else:
                            dve.wait_ge(dve_conv, 16 * i + n - 1)
                            dve.scalar_tensor_tensor(dst, src, w, dst, ALU.mult, ALU.add).then_inc(dve_conv, 1)

            def conv_silu(i, p, j):
                dve.wait_ge(act_conv, 2 * i + j + 1)
                f = lambda t: t[:, 2 * j:2 * j + 2].rearrange("p a b t -> p (a b t)")
                dve.scalar_tensor_tensor(f(qkv[p]), f(qkv[p]), 1.0, f(conv), ALU.add, ALU.mult).then_inc(dve_qkv, 1)

            def join(l, produced, count, done):
                wait_apart(dve, sh, produced, count)
                src = half(bank[6][:], 0, True) if l == 0 else bank[6][:, 0:256].rearrange("p (q s) -> p q s", s=1 << l)
                dve.copy_predicated(half(z_neg[l][:], l, True), sh.level_masks[:, l].rearrange("p (q s) -> p q s", s=1 << l),
                                    src).then_inc(done, 1)

            def body(i, p, nxt, cur, prev, prev2):
                q = 1 - p

                def join_early(l):
                    join(l, pe_lev_e, EARLY * i + l + 1, dve_z_e)

                def join_late(l):
                    join(l, pe_lev_l, LATE * (i - 1) + l - EARLY + 1, dve_z_l)

                if not prev and not prev2:
                    dve.memset(raw[:, :, :, 0:3], 0.0)
                    dve.memset(state[:], 0.0)
                    for l in range(LEVELS):
                        dve.tensor_copy(z_neg[l][:].rearrange("p (m n) -> p m n", m=M), ident.unsqueeze(1).to_broadcast([P, M, P]))
                    dve.wait_ge(ld_const, 16)
                    dve.tensor_scalar(norm_w[:], norm_w[:], float(P) ** 0.5, None, ALU.mult)
                    dve.memset(y[:], 0.0).then_inc(dve_init, 1)
                    dve.wait_ge(dve_init, 1)
                    dve.sem_inc(dve_y, 1)
                    for j in range(2):
                        convolve(0, 0, j, range(4))
                    for j in range(2):
                        conv_silu(0, 0, j)
                if prev:
                    dve.wait_ge(pe_ks, i)
                    dve.wait_ge(dve_v, i)
                    for m in range(M):
                        mm = dve.scalar_tensor_tensor(rhs[:, m, :], bank[0][:, cols(m)],
                                                      ks_scale[q][:, m // RATIO, m % RATIO:m % RATIO + 1], v_beta[:, m, :],
                                                      ALU.mult, ALU.add)
                    mm.then_inc(dve_rhs, 1)
                    join_late(4)
                    if prev2:
                        dve.wait_ge(dve_o, i - 1)
                    dve.wait_ge(pe_qs, i)
                    dve.tensor_tensor(qs[:], bank[1][:].rearrange("p (m e) -> p m e", m=M),
                                      qs_scale[q][:].rearrange("p b r -> p (b r)").unsqueeze(2).to_broadcast([P, M, P]),
                                      ALU.mult).then_inc(dve_qs, 1)
                if cur:
                    dve.wait_ge(pe_kkq, i + 1)
                    dve.tensor_tensor(kkq[:], bank[5][:].rearrange("p (a b s) -> p a b s", a=2, b=B),
                                      kkq_mask.unsqueeze(2).to_broadcast([P, 2, B, P]), ALU.mult).then_inc(dve_kkq, 1)
                    dve.wait_ge(act_dec, i + 1)
                    dve.wait_ge(dve_kkq, i + 1)
                    dve.wait_ge(pl_sc, 4 * i + 2)
                    for m in range(M):
                        mm = dve.scalar_tensor_tensor(m_neg[p][:, m, :], decay[:, m, :], beta_r2[p][:, m // RATIO, m % RATIO:m % RATIO + 1],
                                                      kkq[:, 0, m // RATIO, :], ALU.mult, ALU.mult)
                    mm.then_inc(dve_m, 1)
                    join_early(0)
                    dve.wait_ge(pe_dt, i + 1)
                    dve.tensor_tensor(a_t[p][:], bank[5][:].rearrange("p (b r t) -> p b r t", b=B, r=RATIO),
                                      kkq[:, 1].unsqueeze(2).to_broadcast([P, B, RATIO, P]), ALU.mult).then_inc(dve_a, 1)
                if prev:
                    join_late(5)
                if cur:
                    if prev2:
                        dve.wait_ge(pl_gt, i - 1)
                    dve.wait_ge(act_z, i + 1)
                    dve.scalar_tensor_tensor(z_silu[p][:], z_tanh[:], 1.0, bank[2][:], ALU.add, ALU.mult).then_inc(dve_zs, 1)
                if nxt:
                    convolve(i + 1, q, 0, range(2))
                if cur:
                    join_early(1)
                if prev2:
                    dve.wait_ge(pl_gsq, i - 1)
                    dve.tensor_reduce(o_norm[:], gated_sq[:], AX.X, ALU.add).then_inc(dve_red, 1)
                if prev:
                    join_late(6)
                if nxt:
                    convolve(i + 1, q, 0, range(2, 4))
                if cur:
                    dve.wait_ge(pe_v, i + 1)
                    dve.tensor_tensor(v_beta[:], bank[3][:].rearrange("p (m e) -> p m e", m=M),
                                      beta_r[p][:].rearrange("p b r -> p (b r)").unsqueeze(2).to_broadcast([P, M, P]),
                                      ALU.mult).then_inc(dve_v, 1)
                    join_early(2)
                if nxt:
                    convolve(i + 1, q, 1, range(2))
                    conv_silu(i + 1, q, 0)
                if prev:
                    dve.wait_ge(pe_s, i)
                    for m in range(M):
                        b, r = m // RATIO, m % RATIO
                        mm = dve.scalar_tensor_tensor(state[:, b, r, :], state[:, b, r, :], gate[q][:, 5, b, r:r + 1],
                                                      bank[4][:, cols(m)], ALU.mult, ALU.add)
                    mm.then_inc(dve_s, 1)
                if cur:
                    join_early(3)
                if nxt:
                    convolve(i + 1, q, 1, range(2, 4))
                if prev:
                    dve.wait_ge(pe_o, i)
                    dve.wait_ge(dve_qs, i)
                    for b in range(B):
                        mm = dve.scalar_tensor_tensor(o[:, b * RATIO:(b + 1) * RATIO, :], bank[5][:, b * 256:(b + 1) * 256].rearrange("p (r e) -> p r e", r=RATIO),
                                                      rnorm[q][:, 0, b:b + 1], qs[:, b * RATIO:(b + 1) * RATIO, :], ALU.mult, ALU.add)
                    mm.then_inc(dve_o, 1)
                if prev2:
                    dve.wait_ge(pe_y, i - 1)
                    yt = y[:, bass.ds((i - 2) % CH, 1)].rearrange("p c b d -> p (c b d)")
                    dve.tensor_tensor(yt, bank[3][:], yt, ALU.add).then_inc(dve_y, 1)
                if nxt:
                    conv_silu(i + 1, q, 1)

            turns(dve, body)
            dve.wait_ge(dve_y, STEPS + 1)

        @block.gpsimd
        def _(pool):
            def body(i, p, nxt, cur, prev, prev2):
                q = 1 - p
                def below_sums(n, r, first):
                    pool.wait_ge(ld_gate[r], 16 * (n // 2 + 1))
                    if not first:
                        pool.wait_ge(pe_dd, n)
                    pool.tensor_tensor(g_below[:], below.unsqueeze(1).to_broadcast([P, M, P]),
                                       gate[r][:, 1].rearrange("p b r -> p (b r)").unsqueeze(2).to_broadcast([P, M, P]),
                                       ALU.mult).then_inc(pl_g, 1)

                if cur:
                    pool.wait_ge(dve_qkv, 2 * i + 1)
                    if prev:
                        pool.wait_ge(pe_k, i)
                    pool.tensor_tensor(squares[:].rearrange("p a b t -> p (a b t)"), qkv[p][:, 0:2].rearrange("p a b t -> p (a b t)"),
                                       qkv[p][:, 0:2].rearrange("p a b t -> p (a b t)"), ALU.mult).then_inc(pl_sq, 1)
                    below_sums(i, p, not prev)
                    pool.wait_ge(act_k, i + 1)
                    if prev2:
                        pool.wait_ge(dve_o, i - 1)
                    pool.tensor_tensor(rnorm[p][:].rearrange("p a b -> p (a b)"), norms,
                                       sh.pw[:, 2:3].to_broadcast([P, 4]), ALU.add).then_inc(pl_rn, 1)
                    pool.wait_ge(pl_rn, 2 * i + 1)
                    pool.tensor_tensor(rnorm[p][:].rearrange("p a b -> p (a b)"), rnorm[p][:].rearrange("p a b -> p (a b)"),
                                       sh.pw[:, 0:1].to_broadcast([P, 4]), ALU.pow).then_inc(pl_rn, 1)
                    pool.wait_ge(pl_rn, 2 * i + 2)
                    rk = rnorm[p][:, 1].unsqueeze(2).to_broadcast([P, B, RATIO])
                    rq = rnorm[p][:, 0].unsqueeze(2).to_broadcast([P, B, RATIO])
                    pool.tensor_tensor(beta_r[p][:], gate[p][:, 0], rk, ALU.mult).then_inc(pl_sc, 1)
                    pool.wait_ge(pl_sc, 4 * i + 1)
                    pool.tensor_tensor(beta_r2[p][:], beta_r[p][:], rk, ALU.mult).then_inc(pl_sc, 1)
                    pool.tensor_tensor(qs_scale[p][:], gate[p][:, 3], rq, ALU.mult).then_inc(pl_sc, 1)
                    pool.wait_ge(pl_sc, 4 * i + 3)
                    pool.tensor_tensor(ks_scale[p][:], gate[p][:, 2], beta_r2[p][:], ALU.mult).then_inc(pl_sc, 1)
                if prev2:
                    pool.wait_ge(dve_o, i - 1)
                    pool.wait_ge(dve_zs, i - 1)
                    if not isinstance(i, int) or i > 2:
                        pool.wait_ge(pl_x, i - 2)
                    pool.tensor_tensor(gated[:], o[:].rearrange("p m e -> p (m e)"), z_silu[p][:], ALU.mult).then_inc(pl_gt, 1)
                    pool.wait_ge(pl_gt, i - 1)
                    pool.tensor_tensor(gated_sq[:].rearrange("p m e -> p (m e)"), gated[:], gated[:], ALU.mult).then_inc(pl_gsq, 1)
                if cur:
                    pool.wait_ge(dve_z_e, EARLY * i + 1)
                    if prev2:
                        pool.wait_ge(pe_u, i - 1)
                    z0 = half(z_neg[0][:], 1, False)
                    pool.tensor_tensor(half(r_inv[p][:], 1, False), z0, sh.masks[:, 5 * P:6 * P].unsqueeze(2).to_broadcast([P, P, 2]), ALU.mult).then_inc(pl_r, 1)
                if prev2:
                    pool.wait_ge(dve_red, i - 1)
                    pool.tensor_tensor(o_rnorm[:], o_norm[:], sh.pw[:, 3:4].to_broadcast([P, M]), ALU.add).then_inc(pl_on, 1)
                    pool.wait_ge(pl_on, 2 * i - 3)
                    pool.tensor_tensor(o_rnorm[:], o_rnorm[:], sh.pw[:, 0:1].to_broadcast([P, M]), ALU.pow).then_inc(pl_on, 1)
                    pool.wait_ge(pl_on, 2 * i - 2)
                    pool.tensor_tensor(scaled[:], gated[:].rearrange("p (m e) -> p m e", m=M),
                                       o_rnorm[:].unsqueeze(2).to_broadcast([P, M, P]), ALU.mult).then_inc(pl_x, 1)
                if cur:
                    if prev2:
                        pool.wait_ge(pe_s, i - 1)
                    pool.tensor_tensor(k_dec[p][:], k_tok.unsqueeze(2).to_broadcast([P, B, RATIO, P]),
                                       gate[p][:, 4].unsqueeze(3).to_broadcast([P, B, RATIO, P]), ALU.mult).then_inc(pl_kd, 1)

            turns(pool, body)


def ln_vector(dve, sh, w, n, src, S):
    dve.bn_stats(sh.stats[w][:], src).then_inc(S.stats, 1)
    wait_apart(dve, sh, S.stats, n + 1)
    dve.bn_aggr(sh.mean_var[w][:], sh.stats[w][:]).then_inc(S.mean, 1)


def ln_pool(pool, sh, w, n, S):
    pool.wait_ge(S.mean, n + 1)
    pool.tensor_tensor(sh.rstd[w][:], sh.mean_var[w][:, 1:2], sh.pw[:, 1:2], ALU.add).then_inc(S.var, 1)
    pool.wait_ge(S.var, n + 1)
    pool.tensor_tensor(sh.rstd[w][:], sh.rstd[w][:], sh.pw[:, 0:1], ALU.pow).then_inc(S.rstd, 1)


def ln_norm(dve, sh, w, n, src, S):
    dve.wait_ge(S.rstd, n + 1)
    dve.tensor_scalar(sh.normed[w][:], src, sh.mean_var[w][:, 0:1], sh.rstd[w][:], ALU.subtract, ALU.mult).then_inc(S.norm, 1)


def ln_turn(pe, sh, w, n, bank, S):
    pe.wait_ge(S.norm, n + 1)
    for k in range(KT):
        mm = pe.transpose(bank[:, k * P:(k + 1) * P], sh.normed[w][:, k * P:(k + 1) * P], sh.masks[:, 0:P])
    mm.then_inc(S.turn, 1)


def ln_modulate(dve, sh, w, n, bank, dst, layer, half_of_layer, b, S):
    dve.wait_ge(S.turn, n + 1)
    for k in range(KT):
        ins = dve.tensor_scalar(dst[:, k, :], bank[:, k * P:(k + 1) * P], sh.mod[:, layer, 3 * half_of_layer + 1, k, b:b + 1],
                                sh.mod[:, layer, 3 * half_of_layer, k, b:b + 1], ALU.mult, ALU.add)
    ins.then_inc(S.h, 1)


class LnSems:
    def __init__(self, sem, name):
        self.stats, self.mean, self.var, self.rstd, self.norm, self.turn, self.h = (
            sem(f"{name}_{n}") for n in ("stats", "mean", "var", "rstd", "norm", "turn", "h"))


W = 4
NT = CH * B
NH = 32
NG = 8
HD = 8
PARTS = 3


def ffn0_phase(nc, A, sh, sem):
    with ExitStack() as ctx:
        def sb(name, shape, dt=F32):
            return ctx.enter_context(nc.sbuf_tensor(name, shape, dt))

        w_up = sb("f0_up", [P, KT, DIM])
        w_down = sb("f0_down", [P, KT, DIM])
        w_exp = sb("f0_exp", [P, KT, DIM])
        w_gate = sb("f0_gate", [P, KT, 8])
        w_q = sb("a_wq", [P, KT, DIM])
        w_k = sb("a_wk", [P, KT, 64])
        w_v = sb("a_wv", [P, KT, 64])
        b_q = sb("a_bq", [P, KT])
        b_k = sb("a_bk", [64, 1])
        b_v = sb("a_bv", [P, 64])
        parts = sb("qk_parts", [P, PARTS, 3, T * B], BF16)
        h_a = [sb(f"f0_ha{w}", [P, KT, P]) for w in range(W)]
        h_b = [sb(f"f0_hb{w}", [P, KT, P]) for w in range(W)]
        up = [sb(f"f0_relu{w}", [P, KT, P]) for w in range(W)]
        shared = [sb(f"f0_shared{w}", [P, DIM]) for w in range(W)]
        tmp = [sb(f"f0_tmp{w}", [P, DIM]) for w in range(W)]
        logits = sb("f0_logits", [P, W, 8])
        top = sb("f0_top", [P, W, 8])
        gap = sb("f0_gap", [P, W])
        r1_in = sb("f0_neg", [P, W])
        r1 = sb("f0_r1", [P, W])
        route = sb("f0_route", [P, W])
        qk = [sb(f"qk{w}", [P, 3, P]) for w in range(W)]
        qk_hi = [[sb(f"qk_part{k}_{w}", [P, 3, P], BF16) for w in range(W)] for k in range(PARTS)]
        bank = [[ctx.enter_context(nc.psum_tensor(f"f0_{n}{w}", [P, 512], F32)) for w in range(W)] for n in "ab"]
        neg, loaded, yg, x1, mm_up, relu, mm_down, lg, tops, ex, rt, sh_sb, moe, x2, mm_qkv, qk_sb, v_sb, split, stored, init = (
            sem("f0_" + n) for n in ("neg", "loaded", "yg", "x1", "mm_up", "relu", "mm_down", "lg", "tops", "ex", "rt", "shsb", "moe",
                                     "x2", "mm_qkv", "qk_sb", "v_sb", "split", "stored", "init"))
        SA, SB = LnSems(sem, "f0a"), LnSems(sem, "f0b")
        block = ctx.enter_context(nc.Block())
        tiles = [(w, w // B, w % B) for w in range(W)]

        def xt(c, b, t):
            return t[:, bass.ds(c, 1), b, :].rearrange("p a d -> p (a d)")

        @block.sync
        def _(sp):
            n = 0
            for dst, src in ((w_up[:], A["f0_up"]), (w_down[:], A["f0_down"]), (w_exp[:], A["f0_exp"]), (w_gate[:], A["f0_gate"]),
                             (w_q[:], A["a_wq"]), (w_k[:], A["a_wk"]), (w_v[:], A["a_wv"]), (b_q[:], A["a_bq"]),
                             (b_k[:], A["a_bk"]), (b_v[:], A["a_bv"].to_broadcast([P, 64]))):
                sp.dma_start(dst, src).then_inc(loaded, 16)
            sp.wait_ge(v_sb, 2 * NT)
            for i in range(PARTS):
                for ct in range(3):
                    rows = P if ct < 2 else 64
                    sp.dma_start(sh.scratch[i, ct * P:ct * P + rows, :], parts[0:rows, i, ct, :]).then_inc(stored, 16)
            sp.wait_ge(stored, 16 * 9)

        @block.vector
        def _(dve):
            for w in range(W):
                dve.memset(qk[w][:, 2, :], 0.0)
            dve.memset(sh.v_aug[:], 0.0).then_inc(init, 1)
            dve.wait_ge(init, 1)
            dve.memset(sh.v_aug[:, :, :, HD:HD + 1], 1.0).then_inc(init, 1)
            dve.wait_ge(init, 2)
            dve.wait_ge(loaded, 160)
            with dve.Fori(0, NT // W) as it:
                for w, dc, b in tiles:
                    c = it * (W // B) + dc
                    dve.tensor_tensor(tmp[w][:], xt(c, b, sh.y), sh.gate[:, 0, 0, b, :], ALU.mult).then_inc(yg, 1)
                for w, dc, b in tiles:
                    c, n = it * (W // B) + dc, it * W + w
                    dve.wait_ge(yg, n + 1)
                    dve.tensor_tensor(xt(c, b, sh.x), xt(c, b, sh.x), tmp[w][:], ALU.add).then_inc(x1, 1)
                for w, dc, b in tiles:
                    c, n = it * (W // B) + dc, it * W + w
                    wait_apart(dve, sh, x1, n + 1)
                    ln_vector(dve, sh, w, n, xt(c, b, sh.x), SA)
                for w, dc, b in tiles:
                    c, n = it * (W // B) + dc, it * W + w
                    ln_norm(dve, sh, w, n, xt(c, b, sh.x), SA)
                for w, dc, b in tiles:
                    ln_modulate(dve, sh, w, it * W + w, bank[0][w], h_a[w], 0, 1, b, SA)
                for w, dc, b in tiles:
                    wait_apart(dve, sh, lg, it * W + w + 1)
                    dve.max(top[:, w, :], logits[:, w, :]).then_inc(tops, 1)
                dve.wait_ge(ex, it + 1)
                dve.tensor_scalar(r1[:], gap[:], 1.0, None, ALU.add).then_inc(rt, 1)
                wait_apart(dve, sh, rt, it * 4 + 1)
                dve.reciprocal(r1[:], r1[:]).then_inc(rt, 1)
                dve.wait_ge(rt, it * 4 + 2)
                dve.tensor_tensor(route[:], gap[:], r1[:], ALU.mult).then_inc(rt, 1)
                dve.wait_ge(rt, it * 4 + 3)
                dve.tensor_tensor(route[:], route[:], r1[:], ALU.add).then_inc(rt, 1)
                dve.wait_ge(rt, it * 4 + 4)
                for w, dc, b in tiles:
                    dve.wait_ge(sh_sb, it * W + w + 1)
                    dve.scalar_tensor_tensor(tmp[w][:], bank[0][w][:, 256:512], route[:, w:w + 1], shared[w][:],
                                             ALU.mult, ALU.add).then_inc(moe, 1)
                for w, dc, b in tiles:
                    n = it * W + w
                    dve.wait_ge(moe, it * 2 * W + w + 1)
                    dve.tensor_tensor(tmp[w][:], tmp[w][:], sh.gate[:, 0, 1, b, :], ALU.mult).then_inc(moe, 1)
                for w, dc, b in tiles:
                    c, n = it * (W // B) + dc, it * W + w
                    dve.wait_ge(moe, it * 2 * W + W + w + 1)
                    dve.tensor_tensor(xt(c, b, sh.x), xt(c, b, sh.x), tmp[w][:], ALU.add).then_inc(x2, 1)
                for w, dc, b in tiles:
                    c, n = it * (W // B) + dc, it * W + w
                    wait_apart(dve, sh, x2, n + 1)
                    ln_vector(dve, sh, w, n, xt(c, b, sh.x), SB)
                for w, dc, b in tiles:
                    c, n = it * (W // B) + dc, it * W + w
                    ln_norm(dve, sh, w, n, xt(c, b, sh.x), SB)
                for w, dc, b in tiles:
                    ln_modulate(dve, sh, w, it * W + w, bank[0][w], h_b[w], 1, 0, b, SB)
                for w, dc, b in tiles:
                    n = it * W + w
                    dve.wait_ge(qk_sb, n + 1)
                    tile = bass.ds((it * (W // B) + dc) + b * CH, 1)
                    dve.tensor_tensor(sh.v_aug[:, tile, :, 0:HD], bank[1][w][:, 384:448].rearrange("p (a g d) -> p a g d", a=1, g=NG),
                                      b_v[:].rearrange("p (a g d) -> p a g d", a=1, g=NG), ALU.add).then_inc(v_sb, 1)
                    dve.tensor_copy(qk_hi[0][w][:], qk[w][:]).then_inc(split, 1)
                for k in range(1, PARTS):
                    for w, dc, b in tiles:
                        dve.wait_ge(split, it * 5 * W + (2 * k - 2) * W + w + 1)
                        dve.tensor_tensor(qk[w][:], qk[w][:], qk_hi[k - 1][w][:], ALU.subtract).then_inc(split, 1)
                    for w, dc, b in tiles:
                        dve.wait_ge(split, it * 5 * W + (2 * k - 1) * W + w + 1)
                        dve.tensor_copy(qk_hi[k][w][:], qk[w][:]).then_inc(split, 1)
                for w, dc, b in tiles:
                    col = bass.ds((it * (W // B) + dc) * P + b * T, P)
                    for k in range(PARTS):
                        if k == 2:
                            dve.wait_ge(split, it * 5 * W + 4 * W + w + 1)
                        ins = dve.tensor_copy(parts[:, k, :, col], qk_hi[k][w][:])
                    ins.then_inc(v_sb, 1)
            dve.wait_ge(v_sb, 2 * NT)
            dve.wait_ge(x2, NT)

        @block.gpsimd
        def _(pool):
            with pool.Fori(0, NT // W) as it:
                for w in range(W):
                    ln_pool(pool, sh, w, it * W + w, SA)
                for w in range(W):
                    ln_pool(pool, sh, w, it * W + w, SB)

        @block.scalar
        def _(act):
            act.wait_ge(loaded, 160)
            with act.Fori(0, NT // W) as it:
                for w in range(W):
                    n = it * W + w
                    act.wait_ge(mm_up, n + 1)
                    act.activation(logits[:, w, :], bank[1][w][:, 256:264], ACT.Copy).then_inc(lg, 1)
                    act.activation(up[w][:].rearrange("p k t -> p (k t)"), bank[1][w][:, 0:256], ACT.Relu).then_inc(relu, 1)
                for w in range(W):
                    n = it * W + w
                    act.wait_ge(tops, n + 1)
                    act.activation(r1_in[:, w:w + 1], top[:, w, 0:1], ACT.Copy, scale=-1.0).then_inc(neg, 1)
                for w in range(W):
                    act.wait_ge(neg, it * W + w + 1)
                    e = act.activation(gap[:, w:w + 1], top[:, w, 1:2], ACT.Exp, bias=r1_in[:, w:w + 1])
                e.then_inc(ex, 1)
                for w in range(W):
                    n = it * W + w
                    act.wait_ge(mm_down, n + 1)
                    act.activation(shared[w][:], bank[0][w][:, 0:256], ACT.Copy).then_inc(sh_sb, 1)
                for w in range(W):
                    n = it * W + w
                    act.wait_ge(mm_qkv, n + 1)
                    for ct in range(KT):
                        act.activation(qk[w][:, ct, :], bank[1][w][:, ct * P:(ct + 1) * P], ACT.Identity, bias=b_q[:, ct:ct + 1])
                    act.activation(qk[w][0:64, 2, :], bank[1][w][0:64, 256:384], ACT.Identity, bias=b_k[:]).then_inc(qk_sb, 1)

        @block.tensor
        def _(pe):
            pe.wait_ge(loaded, 160)
            with pe.Fori(0, NT // W) as it:
                for w in range(W):
                    ln_turn(pe, sh, w, it * W + w, bank[0][w], SA)
                for w in range(W):
                    n = it * W + w
                    pe.wait_ge(SA.h, n + 1)
                    pe.wait_ge(v_sb, it * 2 * W)
                    for ft in range(2):
                        for k in range(KT):
                            pe.matmul(bank[1][w][:, ft * P:(ft + 1) * P], w_up[:, k, ft * P:(ft + 1) * P], h_a[w][:, k, :],
                                      start=(k == 0), stop=(k == KT - 1))
                    for k in range(KT):
                        mm = pe.matmul(bank[1][w][:, 256:264], h_a[w][:, k, :], w_gate[:, k, :], start=(k == 0), stop=(k == KT - 1))
                    mm.then_inc(mm_up, 1)
                for w in range(W):
                    n = it * W + w
                    pe.wait_ge(relu, n + 1)
                    for k in range(KT):
                        pe.matmul(bank[0][w][:, 0:256], up[w][:, k, :], w_down[:, k, :], start=(k == 0), stop=(k == KT - 1))
                    for k in range(KT):
                        mm = pe.matmul(bank[0][w][:, 256:512], h_a[w][:, k, :], w_exp[:, k, :], start=(k == 0), stop=(k == KT - 1))
                    mm.then_inc(mm_down, 1)
                for w in range(W):
                    ln_turn(pe, sh, w, it * W + w, bank[0][w], SB)
                for w in range(W):
                    n = it * W + w
                    pe.wait_ge(SB.h, n + 1)
                    for ct in range(2):
                        for k in range(KT):
                            pe.matmul(bank[1][w][:, ct * P:(ct + 1) * P], w_q[:, k, ct * P:(ct + 1) * P], h_b[w][:, k, :],
                                      start=(k == 0), stop=(k == KT - 1))
                    for k in range(KT):
                        pe.matmul(bank[1][w][0:64, 256:384], w_k[:, k, :], h_b[w][:, k, :], start=(k == 0), stop=(k == KT - 1))
                    for k in range(KT):
                        mm = pe.matmul(bank[1][w][:, 384:448], h_b[w][:, k, :], w_v[:, k, :], start=(k == 0), stop=(k == KT - 1))
                    mm.then_inc(mm_qkv, 1)


QH = T // 512
KC = T // P
DATA = 96
ROWS = DATA + PARTS
UNITS = B * NG
SLOTS = QH * KC
BUF = 3


def attention_phase(nc, A, sh, sem):
    with ExitStack() as ctx:
        def sb(name, shape, dt=F32):
            return ctx.enter_context(nc.sbuf_tensor(name, shape, dt))

        q_rows = [sb(f"q_rows{p}", [ROWS, QH, 4, 512], BF16) for p in range(BUF)]
        k_rows = [sb(f"k_rows{p}", [ROWS, T], BF16) for p in range(BUF)]
        v_unit = [sb(f"v_unit{p}", [P, KC, 32]) for p in range(BUF)]
        ones_row = sb("ones_row", [PARTS, T], BF16)
        half_max = sb("half_max", [P, QH, 16, 2])
        row_max = [sb(f"row_max{h}", [P, 16]) for h in range(QH)]
        neg_max = [sb(f"neg_max{h}", [16, P]) for h in range(QH)]
        max_part = [[sb(f"max_part{k}_{h}", [16, P], BF16) for h in range(QH)] for k in range(PARTS)]
        probs = [sb(f"probs{p}", [P, 4, 512]) for p in range(2)]
        out_t = [sb(f"out_t{p}", [P, 512]) for p in range(2)]
        rden = sb("rden", [P, 16])
        s_ps = [ctx.enter_context(nc.psum_tensor(f"s_ps{k}", [P, 1024], F32)) for k in range(2)]
        m_ps = [ctx.enter_context(nc.psum_tensor(f"m_ps{k}", [P, 512], F32)) for k in range(2)]
        pv_ps = ctx.enter_context(nc.psum_tensor("pv_ps", [P, 512], F32))
        t_ps = ctx.enter_context(nc.psum_tensor("t_ps", [P, 512], F32))
        ld_q, ld_k = ([sem(f"at_{n}{p}") for p in range(BUF)] for n in ("ldq", "ldk"))
        ld_m = [[sem(f"at_ldm{p}_{h}") for h in range(QH)] for p in range(BUF)]
        init, mm_m, red, rmax, mx_t, nmax, mm_s, exp, mm_pv, o_sb, o_tr, den, att, vcp, ld_one = (
            sem("at_" + n) for n in ("init", "mm_m", "red", "rmax", "mx_t", "nmax", "mm_s", "exp", "mm_pv", "o_sb", "o_tr",
                                     "den", "att", "vcp", "ld_one"))
        block = ctx.enter_context(nc.Block())
        ident = sh.masks[:, 0:P]

        def turns(eng, body):
            for u in range(BUF):
                body(u, u, True, u >= 1, u >= 2)
            with eng.Fori(0, (UNITS - BUF) // BUF) as j:
                for p in range(BUF):
                    body(j * BUF + (BUF + p), p, True, True, True)
            for u in range(UNITS - (UNITS - BUF) % BUF, UNITS + 2):
                body(u, u % BUF, u < UNITS, u <= UNITS, True)

        def cycle(u):
            return u // BUF + 1

        @block.sync
        def _(sp):
            sp.wait_ge(init, 1)
            for p in range(BUF):
                sp.dma_start(k_rows[p][DATA:ROWS, :], ones_row[:]).then_inc(ld_one, 16)

            def load(u, p, first):
                b, g = u // NG, u % NG
                if not first:
                    sp.wait_ge(mm_s, (u - (BUF - 1)) * 2 * SLOTS)
                for j in range(PARTS):
                    for i in range(PARTS):
                        r = (j * PARTS + i) * HD
                        for hq in range(QH):
                            sp.dma_start(q_rows[p][r:r + HD, hq],
                                         sh.scratch[i:i + 1, bass.ds(g * 4 * HD, 4 * HD), bass.ds(b * T + hq * 512, 512)]
                                         .rearrange("a (h d) t -> d (a h) t", h=4)).then_inc(ld_q[p], 16)
                        sp.dma_start(k_rows[p][r:r + HD, :],
                                     sh.scratch[j:j + 1, bass.ds(2 * P + g * HD, HD), bass.ds(b * T, T)]
                                     .rearrange("a d t -> (a d) t")).then_inc(ld_k[p], 16)

            def body(u, p, cur, prev, prev2):
                if isinstance(u, int) and u == 0:
                    load(0, 0, True)
                if cur and not (isinstance(u, int) and u + 1 >= UNITS):
                    load(u + 1, (p + 1) % BUF, isinstance(u, int) and u + 1 < BUF)
                if cur:
                    for h in range(QH):
                        sp.wait_ge(nmax, (2 * u + h + 1) * 6)
                        for k in range(PARTS):
                            sp.dma_start(q_rows[p][DATA + k:DATA + k + 1, h].rearrange("a h (q t) -> a (h q) t", t=P),
                                         max_part[k][h][:]).then_inc(ld_m[p][h], 16)

            turns(sp, body)

        @block.gpsimd
        def _(pool):
            def body(u, p, cur, prev, prev2):
                if cur:
                    b, g = u // NG, u % NG
                    if not isinstance(u, int) or u >= BUF:
                        pool.wait_ge(mm_pv, (u - (BUF - 1)) * SLOTS)
                    pool.tensor_tensor(v_unit[p][:], sh.v_aug[:, bass.ds(b * CH, CH), bass.ds(g, 1), :].rearrange("p c a d -> p (c a) d"),
                                       sh.masks[:, 5 * P:5 * P + 32].unsqueeze(1).to_broadcast([P, KC, 32]), ALU.mult).then_inc(vcp, 1)

            turns(pool, body)

        @block.tensor
        def _(pe):
            def body(u, p, cur, prev, prev2):
                p1, p2 = (p - 1) % BUF, (p - 2) % BUF

                def maximum(n):
                    if not cur:
                        return
                    t, hf = n // 2, n % 2
                    hq, h, qt = t // 16, t // 4 % 4, t % 4
                    if prev or n >= 2:
                        pe.wait_ge(red, 64 * u + n - 1)
                    pe.matmul(m_ps[n % 2][:], q_rows[p][0:DATA, hq, h, qt * P:(qt + 1) * P],
                              k_rows[p][0:DATA, hf * 512:(hf + 1) * 512], start=True, stop=True).then_inc(mm_m, 1)

                def scores(slot, pair):
                    if not prev:
                        return
                    hq, kc = slot // KC, slot % KC
                    if kc == 0 and pair == 0:
                        pe.wait_ge(ld_m[p1][hq], 48 * cycle(u - 1))
                    if prev2 or slot > 0:
                        pe.wait_ge(exp, 2 * SLOTS * (u - 1) + 2 * slot + pair - 1)
                    for hh in range(2):
                        mm = pe.matmul(s_ps[pair][:, hh * 512:(hh + 1) * 512], k_rows[p1][:, kc * P:(kc + 1) * P],
                                       q_rows[p1][:, hq, 2 * pair + hh, :], start=True, stop=True)
                    mm.then_inc(mm_s, 1)

                def attend(slot, pair):
                    v, buf, there = (u - 1, p1, prev) if slot > 0 else (u - 2, p2, prev2)
                    if not there:
                        return
                    slot = (slot - 1) % SLOTS
                    hq, kc = slot // KC, slot % KC
                    if pair == 0:
                        pe.wait_ge(exp, 2 * SLOTS * v + 2 * slot + 2)
                        pe.wait_ge(vcp, v + 1)
                        if kc == 0 and (prev2 or hq > 0):
                            pe.wait_ge(o_sb, QH * v + hq)
                    for h in (2 * pair, 2 * pair + 1):
                        mm = pe.matmul(pv_ps[32 * h:32 * h + 32, :], v_unit[buf][:, kc, :], probs[slot % 2][:, h, :],
                                       start=(kc == 0), stop=(kc == KC - 1))
                    if pair == 1:
                        mm.then_inc(mm_pv, 1)

                def turn_max(v, hq):
                    pe.wait_ge(rmax, QH * v + hq + 1)
                    pe.transpose(t_ps[0:16, 0:P], row_max[hq][:], ident).then_inc(mx_t, 1)

                def turn_out(v, hq):
                    pe.wait_ge(o_sb, QH * v + hq + 1)
                    for t in range(4):
                        mm = pe.transpose(t_ps[:, t * P:(t + 1) * P], out_t[hq][:, t * P:(t + 1) * P], ident)
                    mm.then_inc(o_tr, 1)

                if cur:
                    pe.wait_ge(ld_q[p], 288 * cycle(u))
                    pe.wait_ge(ld_k[p], 144 * cycle(u))
                if not prev2 and not prev:
                    pe.wait_ge(ld_one, 16 * BUF)
                for slot in range(SLOTS):
                    maximum(4 * slot)
                    scores(slot, 0)
                    maximum(4 * slot + 1)
                    scores(slot, 1)
                    maximum(4 * slot + 2)
                    attend(slot, 0)
                    maximum(4 * slot + 3)
                    attend(slot, 1)
                    if slot == 1 and prev:
                        if prev2:
                            pe.wait_ge(att, QH * (u - 2) + 1)
                        turn_max(u - 1, 1)
                    if slot == 3 and prev2:
                        if prev:
                            pe.wait_ge(nmax, 6 * (QH * (u - 1) + 1) + 1)
                        else:
                            pe.wait_ge(att, QH * (u - 2) + 1)
                        turn_out(u - 2, 1)
                    if slot == 9 and cur:
                        if prev2:
                            pe.wait_ge(att, QH * (u - 2) + 2)
                        elif prev:
                            pe.wait_ge(nmax, 6 * (QH * (u - 1) + 1) + 1)
                        turn_max(u, 0)
                    if slot == 11 and prev:
                        if cur:
                            pe.wait_ge(nmax, 6 * QH * u + 1)
                        else:
                            pe.wait_ge(att, QH * (u - 2) + 2)
                        turn_out(u - 1, 0)

            turns(pe, body)

        @block.scalar
        def _(act):
            def body(u, p, cur, prev, prev2):
                for slot in range(SLOTS):
                    n = SLOTS * (u - 1) + slot
                    if prev:
                        if slot >= 2 or prev2:
                            act.wait_ge(mm_pv, n - 1)
                        for pair in range(2):
                            act.wait_ge(mm_s, 2 * n + pair + 1)
                            act.activation(probs[slot % 2][:, 2 * pair:2 * pair + 2, :].rearrange("p h q -> p (h q)"), s_ps[pair][:],
                                           ACT.Exp, scale=float(HD) ** -0.5).then_inc(exp, 1)
                    if slot % KC == 0 and (prev2 if slot == 0 else prev):
                        k = QH * (u - 1) + slot // KC - 1
                        act.wait_ge(mm_pv, n)
                        if not (isinstance(k, int) and k < 2):
                            act.wait_ge(o_tr, k - 1)
                        act.activation(out_t[(slot // KC - 1) % QH][:], pv_ps[:], ACT.Copy).then_inc(o_sb, 1)

            turns(act, body)

        @block.vector
        def _(dve):
            for p in range(BUF):
                dve.memset(k_rows[p][64:DATA, :], 0.0)
                dve.memset(q_rows[p][64:DATA], 0.0)
            dve.memset(ones_row[:], 1.0)
            dve.drain().then_inc(init, 1)

            def body(u, p, cur, prev, prev2):
                def output(v, hq):
                    n = QH * v + hq
                    b, g = v // NG, v % NG
                    src = t_ps[:].rearrange("p (t d) -> p t d", d=32)
                    wait_apart(dve, sh, o_tr, n + 1)
                    dve.reciprocal(rden[:], src[:, :, HD:HD + 1].rearrange("p t a -> p (t a)")).then_inc(den, 1)
                    dve.wait_ge(den, n + 1)
                    for t in range(4):
                        ins = dve.tensor_tensor(sh.att[:, bass.ds(b * CH + 4 * hq + t, 1), bass.ds(g * 32, 32)].rearrange("p a (h d) -> p (a h) d", h=4),
                                                src[:, 4 * t:4 * t + 4, 0:HD], rden[:, 4 * t:4 * t + 4].unsqueeze(2).to_broadcast([P, 4, HD]),
                                                ALU.mult)
                    ins.then_inc(att, 1)

                def join_halves(v, hq):
                    if hq == 0 or prev2 or prev:
                        dve.wait_ge(red, 64 * v + 32 * (hq + 1))
                    n = QH * v + hq
                    if not (isinstance(n, int) and n < 2):
                        dve.wait_ge(mx_t, n - 1)
                    dve.tensor_tensor(row_max[hq][:], half_max[:, hq, :, 0], half_max[:, hq, :, 1], ALU.max).then_inc(rmax, 1)

                def split_max(v, hq, buf):
                    n = QH * v + hq
                    dve.wait_ge(mx_t, n + 1)
                    dve.tensor_scalar(neg_max[hq][:], t_ps[0:16, 0:P], -1.0, None, ALU.mult).then_inc(nmax, 1)
                    if not (isinstance(v, int) and v == 0):
                        dve.wait_ge(ld_m[(buf - 1) % BUF][hq], 48 * cycle(v - 1))
                    dve.wait_ge(nmax, 6 * n + 1)
                    dve.tensor_copy(max_part[0][hq][:], neg_max[hq][:]).then_inc(nmax, 1)
                    for k in range(1, PARTS):
                        dve.wait_ge(nmax, 6 * n + 2 * k)
                        dve.tensor_tensor(neg_max[hq][:], neg_max[hq][:], max_part[k - 1][hq][:], ALU.subtract).then_inc(nmax, 1)
                        dve.wait_ge(nmax, 6 * n + 2 * k + 1)
                        dve.tensor_copy(max_part[k][hq][:], neg_max[hq][:]).then_inc(nmax, 1)

                for slot in range(SLOTS):
                    if cur:
                        for n in range(4 * slot, 4 * slot + 4):
                            dve.wait_ge(mm_m, 64 * u + n + 1)
                            dve.tensor_reduce(half_max[:, n // 32, n // 2 % 16, n % 2:n % 2 + 1], m_ps[n % 2][:], AX.X, ALU.max).then_inc(red, 1)
                    if slot == 0 and prev:
                        join_halves(u - 1, 1)
                    if slot == 2 and prev:
                        split_max(u - 1, 1, (p - 1) % BUF)
                    if slot == 4 and prev2:
                        output(u - 2, 1)
                    if slot == 8 and cur:
                        join_halves(u, 0)
                    if slot == 10 and cur:
                        split_max(u, 0, p)
                    if slot == 12 and prev:
                        output(u - 1, 0)

            turns(dve, body)
            dve.wait_ge(att, QH * UNITS)


E8 = 8
FF = 176
FT = E8 * FF // P


def ffn1_phase(nc, A, sh, sem, out):
    with ExitStack() as ctx:
        def sb(name, shape, dt=F32):
            return ctx.enter_context(nc.sbuf_tensor(name, shape, dt))

        w_o = sb("f1_wo", [P, KT, DIM])
        b_o = sb("f1_bo", [P, DIM])
        w_r = sb("f1_router", [P, KT, E8])
        w_g = sb("f1_wg", [P, KT, FT * P])
        w_u = sb("f1_wu", [P, KT, FT * P])
        w_d = sb("f1_wd", [P, FT, DIM])
        expand = sb("f1_expand", [E8, FT * P])
        iota = sb("f1_iota", [P, E8])
        att_t = [sb(f"f1_att{w}", [P, KT, P]) for w in range(W)]
        tmp = [sb(f"f1_tmp{w}", [P, DIM]) for w in range(W)]
        h_all = sb("f1_h", [P, KT, W * P])
        logits = sb("f1_logits", [P, W, E8])
        top = sb("f1_top", [P, W, 8])
        idx = sb("f1_idx", [P, W, 8], U32)
        idx_f = sb("f1_idxf", [P, W, 8])
        neg = sb("f1_neg", [P, W])
        wt = sb("f1_wt", [P, 3, W])
        comb = sb("f1_comb", [P, 2, W, E8])
        comb_t = sb("f1_combt", [E8, W * P])
        g_tanh = [sb(f"f1_gt{p}", [P, W * P]) for p in range(2)]
        silu = [sb(f"f1_silu{p}", [P, W * P]) for p in range(2)]
        act_c = [sb(f"f1_c{p}", [P, W * P]) for p in range(2)]
        hid = sb("f1_hid", [P, FT, W * P])
        bank = [ctx.enter_context(nc.psum_tensor(f"f1_b{k}", [P, 512], F32)) for k in range(8)]
        loaded, tr, at_sb, mm_o, ob, og, x3, mm_r, lg, tops, idxs, ng, ex, rt, cb, ct_ps, ct_sb = (
            sem("f1_" + n) for n in ("loaded", "tr", "at_sb", "mm_o", "ob", "og", "x3", "mm_r", "lg", "tops", "idxs", "ng", "ex",
                                     "rt", "cb", "ct_ps", "ct_sb"))
        mm_g, mm_u, mm_c, tanh, sl, ccp, prod, hd, mm_y, yg, x4, stored = (
            sem("f1_" + n) for n in ("mm_g", "mm_u", "mm_c", "tanh", "sl", "ccp", "prod", "hd", "mm_y", "yg", "x4", "stored"))
        S = LnSems(sem, "f1")
        block = ctx.enter_context(nc.Block())
        tiles = [(w, w // B, w % B) for w in range(W)]
        ITS = NT // W

        def xt(c, b, t):
            return t[:, bass.ds(c, 1), b, :].rearrange("p a d -> p (a d)")

        @block.sync
        def _(sp):
            for dst, src in ((w_o[:], A["a_wo"]), (b_o[:], A["a_bo"].to_broadcast([P, DIM])), (w_r[:], A["f1_router"]),
                             (w_g[:], A["f1_wg"]), (w_u[:], A["f1_wu"]), (w_d[:], A["f1_wd"]), (expand[:], A["f1_expand"]),
                             (iota[:], A["f1_iota"])):
                sp.dma_start(dst, src).then_inc(loaded, 16)
            with sp.Fori(0, ITS) as it:
                for w, dc, b in tiles:
                    c = it * (W // B) + dc
                    sp.wait_ge(x4, it * W + w + 1)
                    sp.dma_start(out[b].rearrange("(c p) d -> p c d", p=P)[:, bass.ds(c, 1), :], sh.x[:, bass.ds(c, 1), b, :]).then_inc(stored, 16)
            sp.wait_ge(stored, 16 * NT)

        @block.tensor
        def _(pe):
            pe.wait_ge(loaded, 128)
            ident = sh.masks[:, 0:P]
            with pe.Fori(0, ITS) as it:
                for w, dc, b in tiles:
                    c = it * (W // B) + dc
                    pe.wait_ge(yg, it * 2 * W + w + 1)
                    for k in range(KT):
                        mm = pe.transpose(bank[w][:, k * P:(k + 1) * P], tmp[w][:, k * P:(k + 1) * P], ident)
                    mm.then_inc(tr, 1)
                for w, dc, b in tiles:
                    pe.wait_ge(at_sb, it * W + w + 1)
                    for k in range(KT):
                        mm = pe.matmul(bank[w][:, 256:512], att_t[w][:, k, :], w_o[:, k, :], start=(k == 0), stop=(k == KT - 1))
                    mm.then_inc(mm_o, 1)
                for w in range(W):
                    pe.wait_ge(ob, it * W + w + 1)
                    ln_turn(pe, sh, w, it * W + w, bank[w], S)
                for w in range(W):
                    pe.wait_ge(S.h, it * W + w + 1)
                    for k in range(KT):
                        mm = pe.matmul(bank[w][:, 256:264], h_all[:, k, w * P:(w + 1) * P], w_r[:, k, :], start=(k == 0), stop=(k == KT - 1))
                    mm.then_inc(mm_r, 1)

                def gate_up(f):
                    n = it * FT + f
                    pe.wait_ge(hd, n - 1 if f >= 2 else it * FT)
                    for bk, wts, s in ((4 + f % 2, w_g, mm_g), (6 + f % 2, w_u, mm_u)):
                        for k in range(KT):
                            mm = pe.matmul(bank[bk][:], wts[:, k, f * P:(f + 1) * P], h_all[:, k, :], start=(k == 0), stop=(k == KT - 1))
                        mm.then_inc(s, 1)

                def spread(f):
                    n = it * FT + f
                    pe.wait_ge(ccp, n - 1 if f >= 2 else it * FT)
                    pe.matmul(bank[f % 2][:], expand[:, f * P:(f + 1) * P], comb_t[:], start=True, stop=True).then_inc(mm_c, 1)

                gate_up(0)
                gate_up(1)
                pe.wait_ge(cb, (it + 1) * 2)
                for w in range(W):
                    mm = pe.transpose(bank[0][0:E8, w * P:(w + 1) * P], comb[:, 0, w, :], ident)
                mm.then_inc(ct_ps, 1)
                pe.wait_ge(ct_sb, it + 1)
                for f in range(FT):
                    spread(f)
                    if f >= 2:
                        gate_up(f)
                pe.wait_ge(hd, (it + 1) * FT)
                pe.wait_ge(ccp, (it + 1) * FT)
                for w in range(W):
                    for f in range(FT):
                        mm = pe.matmul(bank[w][:, 0:256], hid[:, f, w * P:(w + 1) * P], w_d[:, f, :], start=(f == 0), stop=(f == FT - 1))
                    mm.then_inc(mm_y, 1)

        @block.scalar
        def _(act):
            act.wait_ge(loaded, 128)
            with act.Fori(0, ITS) as it:
                for w, dc, b in tiles:
                    act.wait_ge(tr, it * W + w + 1)
                    act.activation(att_t[w][:].rearrange("p k t -> p (k t)"), bank[w][:, 0:256], ACT.Copy).then_inc(at_sb, 1)
                for w in range(W):
                    act.wait_ge(mm_r, it * W + w + 1)
                    act.activation(logits[:, w, :], bank[w][:, 256:264], ACT.Copy).then_inc(lg, 1)
                for w in range(W):
                    act.wait_ge(tops, it * W + w + 1)
                    act.activation(neg[:, w:w + 1], top[:, w, 0:1], ACT.Copy, scale=-1.0).then_inc(ng, 1)
                for w in range(W):
                    act.wait_ge(ng, it * W + w + 1)
                    e = act.activation(wt[:, 0, w:w + 1], top[:, w, 1:2], ACT.Exp, bias=neg[:, w:w + 1])
                e.then_inc(ex, 1)

                def tanh_of(f):
                    n = it * FT + f
                    act.wait_ge(mm_g, n + 1)
                    act.activation(g_tanh[f % 2][:], bank[4 + f % 2][:], ACT.Tanh, scale=0.5).then_inc(tanh, 1)

                def spread_copy(f):
                    n = it * FT + f
                    act.wait_ge(mm_c, n + 1)
                    act.wait_ge(hd, n - 1 if f >= 2 else it * FT)
                    act.activation(act_c[f % 2][:], bank[f % 2][:], ACT.Copy, scale=0.5).then_inc(ccp, 1)

                tanh_of(0)
                tanh_of(1)
                act.wait_ge(ct_ps, it + 1)
                act.activation(comb_t[:], bank[0][0:E8, :], ACT.Copy).then_inc(ct_sb, 1)
                for f in range(FT):
                    spread_copy(f)
                    if f >= 2:
                        tanh_of(f)

        @block.gpsimd
        def _(pool):
            with pool.Fori(0, ITS) as it:
                for w in range(W):
                    ln_pool(pool, sh, w, it * W + w, S)
                for f in range(FT):
                    n = it * FT + f
                    pool.wait_ge(sl, n + 1)
                    pool.wait_ge(ccp, n + 1)
                    pool.tensor_tensor(silu[f % 2][:], silu[f % 2][:], act_c[f % 2][:], ALU.mult).then_inc(prod, 1)

        @block.vector
        def _(dve):
            dve.wait_ge(loaded, 128)
            with dve.Fori(0, ITS) as it:
                for w, dc, b in tiles:
                    c = it * (W // B) + dc
                    dve.wait_ge(x4, it * W)
                    dve.tensor_copy(tmp[w][:], sh.att[:, bass.ds(b * CH + c, 1), :].rearrange("p a d -> p (a d)")).then_inc(yg, 1)
                for w, dc, b in tiles:
                    dve.wait_ge(mm_o, it * W + w + 1)
                    dve.tensor_tensor(tmp[w][:], bank[w][:, 256:512], b_o[:], ALU.add).then_inc(ob, 1)
                for w, dc, b in tiles:
                    dve.wait_ge(ob, it * W + w + 1)
                    dve.tensor_tensor(tmp[w][:], tmp[w][:], sh.gate[:, 1, 0, b, :], ALU.mult).then_inc(og, 1)
                for w, dc, b in tiles:
                    c, n = it * (W // B) + dc, it * W + w
                    dve.wait_ge(og, n + 1)
                    dve.tensor_tensor(xt(c, b, sh.x), xt(c, b, sh.x), tmp[w][:], ALU.add).then_inc(x3, 1)
                for w, dc, b in tiles:
                    c, n = it * (W // B) + dc, it * W + w
                    wait_apart(dve, sh, x3, n + 1)
                    ln_vector(dve, sh, w, n, xt(c, b, sh.x), S)
                for w, dc, b in tiles:
                    c, n = it * (W // B) + dc, it * W + w
                    ln_norm(dve, sh, w, n, xt(c, b, sh.x), S)
                for w, dc, b in tiles:
                    ln_modulate(dve, sh, w, it * W + w, bank[w], h_all[:, :, w * P:(w + 1) * P], 1, 1, b, S)
                for w in range(W):
                    wait_apart(dve, sh, lg, it * W + w + 1)
                    dve.max(top[:, w, :], logits[:, w, :]).then_inc(tops, 1)
                for w in range(W):
                    wait_apart(dve, sh, tops, it * W + w + 1)
                    dve.max_index(idx[:, w, :], top[:, w, :], logits[:, w, :]).then_inc(idxs, 1)
                dve.wait_ge(idxs, (it + 1) * W)
                dve.tensor_copy(idx_f[:], idx[:]).then_inc(rt, 1)
                dve.wait_ge(ex, it + 1)
                dve.tensor_scalar(wt[:, 1, :], wt[:, 0, :], 1.0, None, ALU.add).then_inc(rt, 1)
                wait_apart(dve, sh, rt, it * 4 + 2)
                dve.reciprocal(wt[:, 1, :], wt[:, 1, :]).then_inc(rt, 1)
                dve.wait_ge(rt, it * 4 + 3)
                dve.tensor_tensor(wt[:, 2, :], wt[:, 0, :], wt[:, 1, :], ALU.mult).then_inc(rt, 1)
                dve.wait_ge(rt, it * 4 + 4)
                for w in range(W):
                    for j in range(2):
                        ins = dve.tensor_scalar(comb[:, j, w, :], iota[:], idx_f[:, w, j:j + 1], wt[:, 1 + j, w:w + 1],
                                                ALU.is_equal, ALU.mult)
                ins.then_inc(cb, 1)
                dve.wait_ge(cb, it * 2 + 1)
                dve.tensor_tensor(comb[:, 0], comb[:, 0], comb[:, 1], ALU.add).then_inc(cb, 1)
                for f in range(FT + 1):
                    if f < FT:
                        n = it * FT + f
                        dve.wait_ge(tanh, n + 1)
                        dve.wait_ge(hd, n - 1 if f >= 2 else it * FT)
                        dve.scalar_tensor_tensor(silu[f % 2][:], g_tanh[f % 2][:], 1.0, bank[4 + f % 2][:], ALU.add, ALU.mult).then_inc(sl, 1)
                    if f > 0:
                        n = it * FT + f - 1
                        dve.wait_ge(prod, n + 1)
                        dve.wait_ge(mm_u, n + 1)
                        if f == 1:
                            dve.wait_ge(mm_y, it * W)
                        dve.tensor_tensor(hid[:, f - 1, :], bank[6 + (f - 1) % 2][:], silu[(f - 1) % 2][:], ALU.mult).then_inc(hd, 1)
                for w, dc, b in tiles:
                    dve.wait_ge(mm_y, it * W + w + 1)
                    dve.tensor_tensor(tmp[w][:], bank[w][:, 0:256], sh.gate[:, 1, 1, b, :], ALU.mult).then_inc(yg, 1)
                for w, dc, b in tiles:
                    c = it * (W // B) + dc
                    dve.wait_ge(yg, it * 2 * W + W + w + 1)
                    dve.tensor_tensor(xt(c, b, sh.x), xt(c, b, sh.x), tmp[w][:], ALU.add).then_inc(x4, 1)


def build(nc, A, out):
    held = []

    def sem(name):
        held.append(nc.alloc_semaphore(name=name))
        return held[-1]

    def phase_end():
        nc.all_engine_barrier()
        nc.clear_and_free_semaphores(held)
        held.clear()
        nc.all_engine_barrier()

    with ExitStack() as top:
        sh = Shared()

        def sb(name, shape, dt=F32):
            return top.enter_context(nc.sbuf_tensor(name, shape, dt))

        sh.apart = top.enter_context(nc.semaphore("apart"))
        sh.masks = sb("masks_sb", [P, 6 * P])
        sh.mod = sb("mod", [P, 2, 6, KT, B])
        sh.gate = sb("mod_gate", [P, 2, 2, B, DIM])
        sh.pw = sb("pw", [P, 4])
        sh.x = sb("x_res", [P, CH, B, DIM])
        sh.scratch = nc.dram_tensor("qk_rows", (PARTS, 2 * P + 64, B * T), BF16, kind="Internal").ap()
        sh.y = sb("y_res", [P, CH, B, DIM])
        with ExitStack() as first:
            sh.level_masks = first.enter_context(nc.sbuf_tensor("level_masks_sb", [P, LEVELS, 256], I32))
            setup_phase(nc, A, sh, sem)
            sh.h = first.enter_context(nc.sbuf_tensor("h_res", [P, KT, CH * B * P], F32))
            sh.gates = first.enter_context(nc.sbuf_tensor("gates_sb", [P, STEPS, 6, M], F32))
            ln_phase(nc, A, sh, sem)
            phase_end()
            delta_phase(nc, A, sh, sem)
            phase_end()
        sh.stats = [sb(f"stats{w}", [P, 6]) for w in range(W)]
        sh.mean_var = [sb(f"mean_var{w}", [P, 2]) for w in range(W)]
        sh.rstd = [sb(f"rstd{w}", [P, 1]) for w in range(W)]
        sh.normed = [sb(f"normed{w}", [P, DIM]) for w in range(W)]
        sh.v_aug = sb("v_aug", [P, NT, NG, 32])
        ffn0_phase(nc, A, sh, sem)
        sh.att = sb("attended", [P, NT, DIM])
        attention_phase(nc, A, sh, sem)
        ffn1_phase(nc, A, sh, sem, out)


def layouts(inp):
    a = {k: np.ascontiguousarray(v) for k, v in inp.items()}
    d = {k: a[k] for k in ("L0_attn_hidden_states", "L0_attn_W_qkvz", "L0_attn_W_ba", "L0_attn_W_out", "L0_wmod", "L1_wmod")}
    d["c0"] = a["L0_c"].reshape(B, KT, P).transpose(2, 1, 0)
    d["c1"] = a["L1_c"].reshape(B, KT, P).transpose(2, 1, 0)
    d["alog"] = a["L0_attn_A_log"].reshape(1, 2 * HK)
    d["dtb"] = a["L0_attn_dt_bias"].reshape(1, 2 * HK)
    d["norm_w"] = a["L0_attn_norm_weight"].reshape(P, 1)
    w = a["L0_attn_conv_w"]
    q, k, v = w[:2048].reshape(HK, 1, P, 4), w[2048:4096].reshape(HK, 1, P, 4), w[4096:].reshape(HK, RATIO, P, 4)
    d["conv_w"] = np.concatenate([q, k, v], 1).transpose(2, 0, 1, 3).reshape(P, HK * 16)
    rows = lambda m: m.reshape(KT, P, -1).transpose(1, 0, 2)
    d["f0_up"], d["f0_down"] = rows(a["L0_ffn_W_up"].T), rows(a["L0_ffn_W_down"].T)
    d["f0_exp"], d["f0_gate"] = rows(a["L0_ffn_W_expert"]), rows(a["L0_ffn_W_gate"].T)
    d["a_wq"], d["a_wk"], d["a_wv"], d["a_wo"] = (rows(a["L1_attn_W" + n]) for n in "qkvo")
    d["a_bq"] = a["L1_attn_bq"].reshape(KT, P).T
    d["a_bk"] = a["L1_attn_bk"].reshape(64, 1)
    d["a_bv"], d["a_bo"] = a["L1_attn_bv"].reshape(1, 64), a["L1_attn_bo"].reshape(1, DIM)
    d["f1_router"] = rows(a["L1_ffn_gate_w"])
    d["f1_wg"], d["f1_wu"] = (rows(a["L1_ffn_w_" + n].transpose(1, 0, 2).reshape(DIM, E8 * FF)) for n in ("gate", "up"))
    d["f1_wd"] = a["L1_ffn_w_down"].reshape(FT, P, DIM).transpose(1, 0, 2)
    d["f1_expand"] = np.repeat(np.eye(E8, dtype=np.float32), FF, axis=1)
    d["f1_iota"] = np.tile(np.arange(E8, dtype=np.float32), (P, 1))
    i = np.arange(P)
    le = (i[:, None] <= i[None, :]).astype(np.float32)
    sl = (i[:, None] > i[None, :]).astype(np.float32)
    d["masks"] = np.concatenate([np.eye(P, dtype=np.float32), -2 * sl, le * np.float32(P ** -0.5), le, sl,
                                 np.ones((P, P), np.float32)], 1)
    lm = np.zeros((P, LEVELS, M, 64), np.int32)
    for l in range(LEVELS):
        s = 1 << l
        cols = np.array([c for c in range(P) if (c // s) % 2])
        lm[:, l] = ((i[:, None] // (2 * s) == cols[None, :] // (2 * s)) & ((i[:, None] // s) % 2 == 0))[:, None, :]
    d["level_masks"] = lm.reshape(P, LEVELS, 256)
    return {k: np.ascontiguousarray(v) for k, v in d.items()}


def kernel(**inputs):
    import concourse.bacc as bacc
    from concourse.bass_utils import run_bass_kernel_spmd

    nc = bacc.Bacc("TRN2", target_bir_lowering=False, num_devices=1)
    arrays = {"in_" + name: a for name, a in layouts(inputs).items()}
    A = {name[3:]: nc.dram_tensor(name, a.shape, mybir.dt.from_np(a.dtype), kind="ExternalInput").ap() for name, a in arrays.items()}
    out = nc.dram_tensor("out", (B, T, DIM), F32, kind="ExternalOutput").ap()
    build(nc, A, out)
    return run_bass_kernel_spmd(nc, [arrays], core_ids=[0]).results[0]["out"]
```

```python
from contextlib import ExitStack

import numpy as np
import concourse.bass as bass
from concourse import mybir

F32 = mybir.dt.float32
BF16 = mybir.dt.bfloat16
I32 = mybir.dt.int32
U32 = mybir.dt.uint32
ALU = mybir.AluOpType
ACT = mybir.ActivationFunctionType
AX = mybir.AxisListType

P = 128
DIM = 256
KT = DIM // P
B = 2
T = 1024
CH = T // P
HK = 16
RATIO = 2
STEPS = HK * CH
M = B * RATIO
LEVELS = 7
SB = 32
NB = P // SB
FULL = (0, 5, 6)
COMPACT = (1, 2, 3, 4)
WCOL = 768
QKV = 512
LN_EPS = 1e-5
EPS = 1e-6


def half(x, level, second):
    s = 1 << level
    return x.rearrange("p (q two s) -> p q two s", two=2, s=s)[:, :, int(second), :]


class Shared:
    pass


def iterations(eng, n, iteration):
    iteration(0)
    with eng.Fori(1, n) as k:
        iteration(k)


def wait_apart(eng, sh, s, value):
    eng.wait_ge(s, value)
    eng.sem_inc(sh.apart, 1)


def setup_phase(nc, A, sh, sem):
    with ExitStack() as ctx:
        def sb(name, shape, dt=F32):
            return ctx.enter_context(nc.sbuf_tensor(name, shape, dt))

        wmod = sb("wmod", [P, 2, KT, 6 * DIM])
        c_t = sb("c_t", [P, 2, KT, B])
        c_exp = sb("c_exp", [P, 2 * KT * B])
        c_silu = sb("c_silu", [P, 2, KT, B])
        c_rep = sb("c_rep", [P, 2, KT, B, P])
        sign = sb("sign", [P, 2 * 2 * B * DIM])
        mag = sb("mag", [P, 2 * 2 * B * DIM])
        psum = [ctx.enter_context(nc.psum_tensor(f"mod_ps{k}", [P, 512], F32)) for k in range(5)]
        ld_c, ld_wmod, ld_rest, c_e, c_s, c_r, mods, gates_ps, done, sgn = (
            sem(n) for n in ("set_ld_c", "set_ld_wmod", "set_ld_rest", "set_cexp", "set_csilu", "set_crep",
                             "set_mods", "set_gps", "set_done", "set_sign"))
        block = ctx.enter_context(nc.Block())

        @block.sync
        def _(sp):
            sp.dma_start(c_t[:, 0], A["c0"]).then_inc(ld_c, 16)
            sp.dma_start(c_t[:, 1], A["c1"]).then_inc(ld_c, 16)
            for layer in range(2):
                sp.dma_start(wmod[:, layer], A[f"L{layer}_wmod"].rearrange("(k p) n -> p k n", p=P)).then_inc(ld_wmod, 16)
            for b in range(B):
                sp.dma_start(sh.x[:, :, b], A["L0_attn_hidden_states"][b].rearrange("(c p) d -> p c d", p=P)).then_inc(ld_rest, 16)
            sp.dma_start(sh.masks[:], A["masks"]).then_inc(ld_rest, 16)
            sp.dma_start(sh.level_masks[:], A["level_masks"]).then_inc(ld_rest, 16)
            sp.dma_start(sh.block_masks[:], A["block_masks"]).then_inc(ld_rest, 16)
            sp.wait_ge(ld_rest, 16 * (B + 3))

        @block.scalar
        def _(act):
            act.wait_ge(ld_c, 32)
            act.activation(c_exp[:], c_t[:].rearrange("p l k b -> p (l k b)"), ACT.Exp, scale=-1.0).then_inc(c_e, 1)

        @block.tensor
        def _(pe):
            pe.wait_ge(ld_wmod, 32)
            pe.wait_ge(c_r, 1)
            for layer in range(2):
                for ct in range(12):
                    for k in range(KT):
                        mm = pe.matmul(psum[0][:, layer * 24 + ct * 2:layer * 24 + ct * 2 + 2],
                                       wmod[:, layer, k, ct * P:(ct + 1) * P], c_silu[:, layer, k, :],
                                       start=(k == 0), stop=(k == KT - 1))
            mm.then_inc(mods, 1)
            for layer in range(2):
                for g, part in enumerate((2, 5)):
                    for b in range(B):
                        for k in range(KT):
                            mm = pe.matmul(psum[1 + layer * 2 + g][:, b * DIM:(b + 1) * DIM], c_rep[:, layer, k, b, :],
                                           wmod[:, layer, k, part * DIM:(part + 1) * DIM],
                                           start=(k == 0), stop=(k == KT - 1))
            mm.then_inc(gates_ps, 1)

        @block.vector
        def _(dve):
            dve.wait_ge(c_e, 1)
            flat = c_t[:].rearrange("p l k b -> p (l k b)")
            dve.tensor_scalar(c_exp[:], c_exp[:], 1.0, None, ALU.add).then_inc(c_s, 1)
            dve.wait_ge(c_s, 1)
            dve.reciprocal(c_exp[:], c_exp[:]).then_inc(c_s, 1)
            dve.wait_ge(c_s, 2)
            dve.tensor_tensor(c_silu[:].rearrange("p l k b -> p (l k b)"), flat, c_exp[:], ALU.mult).then_inc(c_s, 1)
            dve.wait_ge(c_s, 3)
            for layer in range(2):
                for k in range(KT):
                    rep = dve.tensor_copy(c_rep[:, layer, k], c_silu[:, layer, k, :].unsqueeze(2).to_broadcast([P, B, P]))
            rep.then_inc(c_r, 1)
            dve.wait_ge(mods, 1)
            dve.tensor_copy(sh.mod[:], psum[0][:, 0:48].rearrange("p (l s k b) -> p l s k b", l=2, s=6, k=KT)).then_inc(done, 1)
            dve.wait_ge(done, 1)
            for layer in range(2):
                for s in (1, 4):
                    dve.tensor_scalar(sh.mod[:, layer, s], sh.mod[:, layer, s], 1.0, None, ALU.add).then_inc(done, 1)
            dve.wait_ge(gates_ps, 1)
            for n in range(4):
                part = slice(n * 512, (n + 1) * 512)
                dve.tensor_scalar(sign[:, part], psum[1 + n][:], 0.0, 2.0, ALU.is_ge, ALU.mult).then_inc(sgn, 1)
                dve.tensor_copy(mag[:, part], psum[1 + n][:]).then_inc(sgn, 1)
                dve.wait_ge(sgn, 4 * n + 2)
                dve.scalar_tensor_tensor(mag[:, part], mag[:, part], -1.0, mag[:, part], ALU.mult, ALU.max).then_inc(sgn, 1)
                dve.wait_ge(sgn, 4 * n + 3)
                dve.tensor_scalar(mag[:, part], mag[:, part], 0.25, None, ALU.max).then_inc(sgn, 1)
                dve.wait_ge(sgn, 4 * n + 4)
                dve.scalar_tensor_tensor(sh.gate[:].rearrange("p l g b d -> p (l g b d)")[:, part], sign[:, part], -1.0,
                                         mag[:, part], ALU.add, ALU.mult).then_inc(done, 1)
            dve.memset(sh.pw[:, 0:1], -0.5).then_inc(done, 1)
            dve.memset(sh.pw[:, 1:2], LN_EPS).then_inc(done, 1)
            dve.memset(sh.pw[:, 2:3], 4 * EPS).then_inc(done, 1)
            dve.memset(sh.pw[:, 3:4], 4 * EPS * P).then_inc(done, 1)
            dve.wait_ge(done, 13)
            dve.drain()


def ln_phase(nc, A, sh, sem):
    with ExitStack() as ctx:
        def sb(name, shape, dt=F32):
            return ctx.enter_context(nc.sbuf_tensor(name, shape, dt))

        w_ba = sb("w_ba", [P, KT, 4 * HK])
        ba = sb("ba", [P, HK, CH, B, 2, RATIO])
        alog = sb("a_log_sb", [P, HK, RATIO])
        dtb = sb("dt_bias_sb", [P, HK, RATIO])
        stats = [sb(f"ln_stats{b}", [P, 6]) for b in range(B)]
        mean_var = [sb(f"ln_mv{b}", [P, 2]) for b in range(B)]
        rstd = [sb(f"ln_rstd{b}", [P, 1]) for b in range(B)]
        normed = [sb(f"ln_normed{b}", [P, DIM]) for b in range(B)]
        h_tile = [sb(f"ln_htile{b}", [P, KT, P]) for b in range(B)]
        NG = STEPS * M
        work = [sb(f"gate_work{k}", [P, NG]) for k in range(4)]
        g_flat = sb("g_flat", [P, NG])
        tr_ps = [ctx.enter_context(nc.psum_tensor(f"ln_tr{b}", [P, 512], F32)) for b in range(B)]
        ba_ps = [ctx.enter_context(nc.psum_tensor(f"ln_ba{b}", [P, 512], F32)) for b in range(B)]
        cum_ps = [ctx.enter_context(nc.psum_tensor(f"cum_ps{k}", [P, 512], F32)) for k in range(3)]
        (loaded, st, mv, veps, rs, nm, tr, ht, ba_mm, ba_sb, neg, vec, cum, ex) = (
            sem(n) for n in ("ln_loaded", "ln_st", "ln_mvs", "ln_veps", "ln_rs", "ln_nm", "ln_trs", "ln_ht",
                             "ln_bamm", "ln_basb", "gt_neg", "gt_vec", "gt_cum", "gt_exp"))
        h_out = [sem(f"ln_hout{b}") for b in range(B)]
        ident = sh.masks[:, 0:P]
        block = ctx.enter_context(nc.Block())

        @block.sync
        def _(sp):
            sp.dma_start(w_ba[:], A["L0_attn_W_ba"].rearrange("(k p) n -> p k n", p=P)).then_inc(loaded, 16)
            sp.dma_start(alog[:].rearrange("p a b -> p (a b)"), A["alog"].to_broadcast([P, 2 * HK])).then_inc(loaded, 16)
            sp.dma_start(dtb[:].rearrange("p a b -> p (a b)"), A["dtb"].to_broadcast([P, 2 * HK])).then_inc(loaded, 16)

            def iteration(c):
                for b in range(B):
                    sp.wait_ge(ht, c * 4 + 2 * b + 2)
                    sp.dma_start(sh.h[:, :, bass.ds((c * B + b) * P, P)], h_tile[b][:]).then_inc(h_out[b], 16)
            iterations(sp, CH, iteration)
            for b in range(B):
                sp.wait_ge(h_out[b], 16 * CH)

        @block.vector
        def _(dve):
            def iteration(c):
                for b in range(B):
                    n = c * B + b
                    xt = sh.x[:, bass.ds(c, 1), b, :]
                    dve.bn_stats(stats[b][:], xt).then_inc(st, 1)
                    wait_apart(dve, sh, st, n + 1)
                    dve.bn_aggr(mean_var[b][:], stats[b][:]).then_inc(mv, 1)
                for b in range(B):
                    n = c * B + b
                    xt = sh.x[:, bass.ds(c, 1), b, :]
                    dve.wait_ge(rs, n + 1)
                    dve.tensor_scalar(normed[b][:], xt, mean_var[b][:, 0:1], rstd[b][:],
                                      ALU.subtract, ALU.mult).then_inc(nm, 1)
                for b in range(B):
                    n = c * B + b
                    dve.wait_ge(tr, n + 1)
                    dve.wait_ge(h_out[b], c * 16)
                    dve.wait_ge(ba_mm, n - b)
                    for k in range(KT):
                        dve.tensor_scalar(h_tile[b][:, k, :], tr_ps[b][:, k * P:(k + 1) * P], sh.mod[:, 0, 1, k, b:b + 1],
                                          sh.mod[:, 0, 0, k, b:b + 1], ALU.mult, ALU.add).then_inc(ht, 1)
            iterations(dve, CH, iteration)
            dve.wait_ge(ba_sb, CH * B)
            dve.wait_ge(loaded, 48)
            G = sh.gates[:].rearrange("p s q m -> p s (q m)")
            k = [0]

            def link(ins):
                k[0] += 1
                ins.then_inc(vec, 1)
                dve.wait_ge(vec, k[0])

            w0, w1, w2, w3 = (w[:] for w in work)
            hbr = lambda w: w.rearrange("p (h q r) -> p h q r", h=HK, r=RATIO)
            dve.wait_ge(neg, 1)
            link(dve.tensor_scalar(w0, w0, 1.0, None, ALU.add))
            link(dve.reciprocal(w0, w0))
            link(dve.tensor_scalar(G[:, :, 0:4], w0.rearrange("p (s m) -> p s m", m=M), 0.5, None, ALU.mult))
            for kh in range(HK):
                ins = dve.tensor_tensor(hbr(w1)[:, kh], ba[:, kh, :, :, 1, :].rearrange("p c b r -> p (c b) r"),
                                        dtb[:, kh:kh + 1, :].to_broadcast([P, CH * B, RATIO]), ALU.add)
            link(ins)
            link(dve.scalar_tensor_tensor(w2, w1, -1.0, w1, ALU.mult, ALU.min))
            dve.wait_ge(neg, 2)
            link(dve.tensor_scalar(w3, w2, 2.0, None, ALU.add))
            link(dve.reciprocal(w3, w3))
            link(dve.tensor_tensor(w3, w3, w2, ALU.mult))
            link(dve.tensor_tensor(w2, w3, w3, ALU.mult))
            link(dve.tensor_scalar(w0, w2, 1.0 / 19, 1.0 / 17, ALU.mult, ALU.add))
            for d in (15, 13, 11, 9, 7, 5, 3, 1):
                link(dve.tensor_tensor(w0, w0, w2, ALU.mult))
                link(dve.tensor_scalar(w0, w0, 1.0 / d, None, ALU.add))
            link(dve.tensor_tensor(w0, w0, w3, ALU.mult))
            link(dve.tensor_scalar(w1, w1, 0.0, None, ALU.max))
            link(dve.scalar_tensor_tensor(w0, w0, 2.0, w1, ALU.mult, ALU.add))
            for kh in range(HK):
                ins = dve.scalar_tensor_tensor(hbr(g_flat[:])[:, kh], hbr(w0)[:, kh], -1.0,
                                               alog[:, kh:kh + 1, :].to_broadcast([P, CH * B, RATIO]), ALU.mult, ALU.mult)
            link(ins)
            link(dve.tensor_copy(G[:, :, 4:8], g_flat[:].rearrange("p (s m) -> p s m", m=M)))
            dve.wait_ge(ex, 3)
            e = lambda w: w.rearrange("p (s m) -> p s m", m=M)
            link(dve.tensor_scalar(G[:, :, 8:12], e(w1), -2.0, None, ALU.mult))
            link(dve.tensor_scalar(G[:, :, 12:16], e(w1), float(P) ** -0.5, None, ALU.mult))
            link(dve.tensor_copy(G[:, :, 16:20], e(w2)))
            link(dve.tensor_copy(G[:, :, 20:24], e(w3)))
            link(dve.memset(sh.gates[:].rearrange("p (h c) q m -> p h c (q m)", c=CH)[:, :, CH - 1, 16:24], 0.0))

        @block.gpsimd
        def _(pool):
            def iteration(c):
                for b in range(B):
                    n = c * B + b
                    pool.wait_ge(mv, n + 1)
                    pool.tensor_tensor(rstd[b][:], mean_var[b][:, 1:2], sh.pw[:, 1:2], ALU.add).then_inc(veps, 1)
                    pool.wait_ge(veps, n + 1)
                    pool.tensor_tensor(rstd[b][:], rstd[b][:], sh.pw[:, 0:1], ALU.pow).then_inc(rs, 1)
            iterations(pool, CH, iteration)

        @block.tensor
        def _(pe):
            pe.wait_ge(loaded, 48)
            def iteration(c):
                for b in range(B):
                    n = c * B + b
                    pe.wait_ge(nm, n + 1)
                    pe.wait_ge(ht, c * 4)
                    for k in range(KT):
                        mm = pe.transpose(tr_ps[b][:, k * P:(k + 1) * P], normed[b][:, k * P:(k + 1) * P], ident)
                    mm.then_inc(tr, 1)
                for b in range(B):
                    n = c * B + b
                    pe.wait_ge(ht, c * 4 + 2 * b + 2)
                    pe.wait_ge(ba_sb, n - b)
                    for k in range(KT):
                        mm = pe.matmul(ba_ps[b][:, 0:4 * HK], h_tile[b][:, k, :], w_ba[:, k, :],
                                       start=(k == 0), stop=(k == KT - 1))
                    mm.then_inc(ba_mm, 1)
            iterations(pe, CH, iteration)
            pe.wait_ge(vec, 30)
            for k, lhs in enumerate((sh.masks[:, 3 * P:4 * P], sh.masks[:, 4 * P:5 * P], sh.masks[:, 5 * P:6 * P])):
                pe.matmul(cum_ps[k][:], lhs, g_flat[:], start=True, stop=True).then_inc(cum, 1)

        @block.scalar
        def _(act):
            def iteration(c):
                for b in range(B):
                    act.wait_ge(ba_mm, c * B + b + 1)
                    act.activation(ba[:].rearrange("p h c b q r -> p h c b (q r)")[:, :, bass.ds(c, 1), b, :],
                                   ba_ps[b][:, 0:4 * HK].rearrange("p (h q) -> p h q", h=HK).unsqueeze(2),
                                   ACT.Copy).then_inc(ba_sb, 1)
            iterations(act, CH, iteration)
            act.wait_ge(ba_sb, CH * B)
            act.activation(work[0][:].rearrange("p (s r) -> p s r", r=RATIO),
                           ba[:, :, :, :, 0, :].rearrange("p h c b r -> p (h c b) r"), ACT.Exp, scale=-1.0).then_inc(neg, 1)
            act.wait_ge(loaded, 48)
            act.wait_ge(vec, 5)
            act.activation(work[2][:], work[2][:], ACT.Exp)
            act.activation(alog[:], alog[:], ACT.Exp).then_inc(neg, 1)
            act.wait_ge(vec, 30)
            for k in range(3):
                act.wait_ge(cum, k + 1)
                act.activation(work[1 + k][:], cum_ps[k][:], ACT.Exp).then_inc(ex, 1)


def delta_phase(nc, A, sh, sem):
    with ExitStack() as ctx:
        def sb(name, shape, dt=F32):
            return ctx.enter_context(nc.sbuf_tensor(name, shape, dt))

        raw = sb("raw", [P, 4, B, T + 3])
        w_qkv = sb("w_qkv", [P, KT, QKV])
        w_z = sb("w_z", [P, KT, RATIO * P])
        w_out = sb("w_out", [P, 2, RATIO * DIM])
        norm_w = sb("norm_w_sb", [P, 1])
        h_in = [sb(f"h_in{p}", [P, KT, B, P]) for p in range(2)]
        gate = [sb(f"gate_in{p}", [P, 6, B, RATIO]) for p in range(2)]
        taps = [sb(f"taps{p}", [P, 4, 4]) for p in range(2)]
        conv = sb("conv", [P, 4, B, P])
        qkv = [sb(f"qkv{p}", [P, 4, B, P]) for p in range(2)]
        squares = sb("squares", [P, 2, B, P])
        rnorm = [sb(f"rnorm{p}", [P, 2, B]) for p in range(2)]
        beta_r = [sb(f"beta_r{p}", [P, B, RATIO]) for p in range(2)]
        beta_r2 = [sb(f"beta_r2{p}", [P, B, RATIO]) for p in range(2)]
        ks_scale = [sb(f"ks_scale{p}", [P, B, RATIO]) for p in range(2)]
        qs_scale = [sb(f"qs_scale{p}", [P, B, RATIO]) for p in range(2)]
        g_below = sb("g_below", [P, M, P])
        decay = sb("decay", [P, M, P])
        kkq = sb("kkq", [P, 2, B, P])
        m_neg = [sb(f"m_neg{p}", [P, M, P]) for p in range(2)]
        a_t = [sb(f"a_t{p}", [P, B, RATIO, P]) for p in range(2)]
        z_neg = [sb(f"z_neg{l}", [P, M * P]) for l in range(LEVELS)]
        r_inv = sb("r_inv", [P, M * P])
        t_inv = sb("t_inv", [P, M * P])
        m_cmp = sb("m_cmp", [P, P])
        r_blk = sb("r_blk", [P, M * P])
        r_cmp = sb("r_cmp", [P, P])
        t_cmp = sb("t_cmp", [P, P])
        k_norms = sb("k_norms", [P, B * P + 2 * B])
        k_tok = k_norms[:, 0:B * P].rearrange("p (b d) -> p b d", b=B)
        norms = k_norms[:, B * P:]
        k_dec = [sb(f"k_dec{p}", [P, B, RATIO, P]) for p in range(2)]
        v_beta = sb("v_beta", [P, M, P])
        rhs = sb("rhs", [P, M, P])
        u = sb("u", [P, M, P])
        qs = sb("qs", [P, M, P])
        state = sb("state", [P, B, RATIO, P])
        o = sb("o", [P, M, P])
        z_tanh = sb("z_tanh", [P, M * P])
        z_silu = [sb(f"z_silu{p}", [P, M * P]) for p in range(2)]
        gated = sb("gated", [P, M * P])
        gated_sq = sb("gated_sq", [P, M, P])
        o_norm = sb("o_norm", [P, M])
        o_rnorm = sb("o_rnorm", [P, M])
        scaled = sb("scaled", [P, M, P])
        o_t = sb("o_t", [P, M, P])
        bank = [ctx.enter_context(nc.psum_tensor(f"bank{k}", [P, 512], F32)) for k in range(8)]
        y = sh.y

        ident = sh.masks[:, 0:P]
        below = sh.masks[:, 3 * P + P:5 * P]
        upto = sh.masks[:, 3 * P:4 * P]
        kkq_mask = sh.masks[:, P:3 * P].rearrange("p (a n) -> p a n", a=2)
        ones = sh.masks[:, 5 * P:5 * P + 1]

        ld_const, ld_wqkv, ld_wz, ld_wout = (sem(n) for n in ("ld_const", "ld_wqkv", "ld_wz", "ld_wout"))
        ld_h, ld_taps, ld_gate = ([sem(f"{n}{p}") for p in range(2)] for n in ("ld_h", "ld_taps", "ld_gate"))
        (pe_proj, pe_z, pe_kkq, pe_dd, pe_v, pe_k, pe_dt, pe_lev_e, pe_lev_l, pe_inv_e, pe_inv_l, pe_tr, pe_rt, pe_ks, pe_qs,
         pe_u, pe_s, pe_o, pe_xt, pe_y) = (
            sem("pe_" + n) for n in ("proj", "z", "kkq", "dd", "v", "k", "dt", "lev_e", "lev_l", "inv_e", "inv_l", "tr", "rt",
                                     "ks", "qs", "u", "s", "o", "xt", "y"))
        act_raw, act_conv, act_dec, act_k, act_mc, act_rc, act_rx, act_rt, act_t_l, act_r_l, act_u, act_z, act_xt = (
            sem("act_" + n) for n in ("raw", "conv", "dec", "k", "mc", "rc", "rx", "rt", "t_l", "r_l", "u", "z", "xt"))
        (dve_conv, dve_qkv, dve_kkq, dve_m, dve_v, dve_a, dve_z_e, dve_t, dve_z_l, dve_rhs, dve_qs, dve_s, dve_o, dve_zs,
         dve_red, dve_y, dve_init) = (
            sem("dve_" + n) for n in ("conv", "qkv", "kkq", "m", "v", "a", "z_e", "t", "z_l", "rhs", "qs", "s", "o", "zs",
                                      "red", "y", "init"))
        (pl_sq, pl_rn, pl_sc, pl_g, pl_r, pl_kd, pl_gt, pl_gsq, pl_on, pl_x) = (
            sem("pl_" + n) for n in ("sq", "rn", "sc", "g", "r", "kd", "gt", "gsq", "on", "x"))
        block = ctx.enter_context(nc.Block())

        def turns(eng, body):
            body(0, 0, True, True, False, False)
            body(1, 1, True, True, True, False)
            with eng.Fori(0, (STEPS - 4) // 2) as j:
                body(j * 2 + 2, 0, True, True, True, True)
                body(j * 2 + 3, 1, True, True, True, True)
            body(STEPS - 2, 0, True, True, True, True)
            body(STEPS - 1, 1, False, True, True, True)
            body(STEPS, 0, False, False, True, True)
            body(STEPS + 1, 1, False, False, False, True)

        @block.sync
        def _(sp):
            sp.dma_start(norm_w[:], A["norm_w"]).then_inc(ld_const, 16)

            def chunk(step, kh, c, p, first):
                if not first:
                    sp.wait_ge(pe_z, step - 1)
                sp.dma_start(h_in[p][:], sh.h[:, :, bass.ds(c * (B * P), B * P)].rearrange("p k (b t) -> p k b t", b=B)).then_inc(ld_h[p], 16)
                if not first:
                    sp.wait_ge(dve_conv, (step - 1) * 16)
                sp.dma_start(taps[p][:].rearrange("p a b -> p (a b)"), A["conv_w"][:, bass.ds(kh * 16, 16)]).then_inc(ld_taps[p], 16)
                if not first:
                    sp.wait_ge(dve_s, step - 1)
                    sp.wait_ge(pl_kd, step - 1)
                sp.dma_start(gate[p][:].rearrange("p q b r -> p (q b r)"),
                             sh.gates[:, bass.ds(step, 1)].rearrange("p s q m -> p (s q m)")).then_inc(ld_gate[p], 16)

            def weights(kh, first):
                src = A["L0_attn_W_qkvz"].rearrange("(k p) n -> p k n", p=P)
                if not first:
                    sp.wait_ge(pe_proj, 4 * CH * kh)
                sp.dma_start(w_qkv[:], src[:, :, bass.ds(kh * WCOL, QKV)]).then_inc(ld_wqkv, 16)

            def weights_z(kh, first):
                src = A["L0_attn_W_qkvz"].rearrange("(k p) n -> p k n", p=P)
                if not first:
                    sp.wait_ge(pe_z, CH * kh)
                sp.dma_start(w_z[:], src[:, :, bass.ds(kh * WCOL + QKV, RATIO * P)]).then_inc(ld_wz, 16)

            def weights_out(kh, first):
                src = A["L0_attn_W_out"].rearrange("(h r e) n -> e h r n", e=P, r=RATIO)
                if not first:
                    sp.wait_ge(pe_y, CH * (kh - 1))
                sp.dma_start(w_out[:, bass.ds(kh % 2, 1)].rearrange("p a (r n) -> p (a r) n", r=RATIO),
                             src[:, bass.ds(kh, 1)].rearrange("p a r n -> p (a r) n")).then_inc(ld_wout, 16)

            weights(0, True)
            weights_z(0, True)
            weights_out(0, True)
            for c in range(CH):
                chunk(c, 0, c, c % 2, c < 2)
            def head(kh):
                weights(kh, False)
                chunk(kh * CH, kh, 0, 0, False)
                weights_z(kh, False)
                weights_out(kh, False)
                with sp.Fori(0, CH // 2 - 1) as cc:
                    chunk(kh * CH + cc * 2 + 1, kh, cc * 2 + 1, 1, False)
                    chunk(kh * CH + cc * 2 + 2, kh, cc * 2 + 2, 0, False)
                chunk(kh * CH + CH - 1, kh, CH - 1, 1, False)

            head(1)
            with sp.Fori(2, HK) as kh:
                head(kh)

        EARLY, LATE = 5, 2
        GROWN = len(COMPACT)
        cols = lambda m: slice(m * P, (m + 1) * P)

        @block.tensor
        def _(pe):
            def project(i, p, ct):
                j = ct // 2
                if ct == 0:
                    pe.wait_ge(ld_h[p], 16 * (i // 2 + 1))
                    pe.wait_ge(ld_wqkv, weights_count(i))
                out = bank[j][:, (ct % 2) * B * P:(ct % 2 + 1) * B * P]
                for k in range(KT):
                    mm = pe.matmul(out, w_qkv[:, k, ct * P:(ct + 1) * P], h_in[p][:, k].rearrange("p b t -> p (b t)"),
                                   start=(k == 0), stop=(k == KT - 1))
                mm.then_inc(pe_proj, 1)

            def weights_count(i):
                return 16 * (i // CH + 1)

            def body(i, p, nxt, cur, prev, prev2):
                q = 1 - p

                def level_block(l, n):
                    if l == 1:
                        pe.wait_ge(dve_z_e, EARLY * n + 1)
                        pe.wait_ge(act_mc, n + 1)
                    else:
                        pe.wait_ge(act_rx, GROWN * n + l - 1)
                    pe.wait_ge(dve_t, GROWN * n + l)
                    src = z_neg[0] if l == 1 else r_blk
                    for m in range(M):
                        mm = pe.matmul(bank[6][SB * m:SB * (m + 1), 0:P], m_cmp[:, SB * m:SB * (m + 1)], src[:, cols(m)], start=True, stop=True)
                    mm.then_inc(pe_lev_e, 1)

                def grow_block(l, n):
                    pe.wait_ge(dve_t, GROWN * n + l)
                    pe.wait_ge(dve_z_e, EARLY * n + l + 1)
                    if l == 1:
                        pe.wait_ge(*((act_r_l, LATE * i) if prev else (act_dec, i + 1)))
                    if l == 4 and cur:
                        pe.wait_ge(act_dec, i + 1)
                    for b in range(NB):
                        mm = pe.matmul(bank[7][SB * b:SB * (b + 1), 0:P], t_cmp[:, SB * b:SB * (b + 1)],
                                       z_neg[l][:, b * P:(b + 1) * P], start=True, stop=True)
                    mm.then_inc(pe_inv_e, 1)

                def turn_r_blocks(l):
                    pe.wait_ge(act_rc, GROWN * i + l + 1)
                    if l == 0 and prev:
                        pe.wait_ge(dve_z_l, LATE * i)
                    pe.transpose(bank[6][:, P:2 * P], r_cmp[:], ident).then_inc(pe_tr, 1)

                def turn_r():
                    pe.wait_ge(act_rx, GROWN * i)
                    for m in range(M):
                        mm = pe.transpose(bank[7][:, cols(m)], r_blk[:, cols(m)], ident)
                    mm.then_inc(pe_rt, 1)

                def level_late(l):
                    if l == 5:
                        src = r_blk
                        pe.wait_ge(dve_z_e, EARLY * i)
                    else:
                        src = r_inv
                        pe.wait_ge(act_r_l, LATE * (i - 1) + 1)
                        pe.wait_ge(pl_r, i)
                        if cur:
                            pe.wait_ge(dve_z_e, EARLY * i + 1)
                    for m in range(M):
                        mm = pe.matmul(bank[6][:, m * 64:(m + 1) * 64], m_neg[q][:, m, :],
                                       half(src[:, cols(m)], l, True), start=True, stop=True)
                    mm.then_inc(pe_lev_l, 1)

                def grow_late(l):
                    pe.wait_ge(dve_z_l, LATE * (i - 1) + l - EARLY + 1)
                    if l == 5:
                        pe.wait_ge(act_rt, i)
                    else:
                        pe.wait_ge(act_t_l, i)
                    for m in range(M):
                        mm = pe.matmul(bank[7][:, m * 64:(m + 1) * 64], t_inv[:, cols(m)],
                                       half(z_neg[l][:, cols(m)], l, True), start=True, stop=True)
                    if l < LEVELS - 1:
                        for m in range(M):
                            mm = pe.matmul(bank[7][:, 256 + m * 64:256 + (m + 1) * 64], z_neg[l][:, cols(m)],
                                           half(t_inv[:, cols(m)], l, False), start=True, stop=True)
                    mm.then_inc(pe_inv_l, 1)

                kt = lambda pp, b: qkv[pp][:, 1, b, :]
                qt = lambda pp, b: qkv[pp][:, 0, b, :]
                if not prev and not prev2:
                    pe.wait_ge(ld_const, 16)
                    for ct in range(4):
                        project(0, 0, ct)
                def keys_state():
                    if prev2:
                        pe.wait_ge(dve_s, i - 1)
                    if cur:
                        pe.wait_ge(act_raw, 2 * i + 1)
                    for b in range(B):
                        mm = pe.matmul(bank[0][:, b * 256:(b + 1) * 256], kt(q, b), state[:, b].rearrange("p r e -> p (r e)"),
                                       start=True, stop=True)
                    mm.then_inc(pe_ks, 1)
                    if cur:
                        pe.wait_ge(act_raw, 2 * i + 2)
                    for b in range(B):
                        mm = pe.matmul(bank[1][:, b * 256:(b + 1) * 256], qt(q, b), state[:, b].rearrange("p r e -> p (r e)"),
                                       start=True, stop=True)
                    mm.then_inc(pe_qs, 1)

                def exponents():
                    pe.wait_ge(pl_g, i + 1)
                    if prev:
                        pe.wait_ge(act_rx, GROWN * i - 1)
                    pe.matmul(bank[7][:], upto, g_below[:].rearrange("p m s -> p (m s)"), start=True, stop=True).then_inc(pe_dd, 1)

                def project_z():
                    pe.wait_ge(ld_wz, weights_count(i))
                    if not prev:
                        pe.wait_ge(ld_h[p], 16)
                    else:
                        pe.wait_ge(dve_zs, i)
                    for b in range(B):
                        for k in range(KT):
                            mm = pe.matmul(bank[2][:, b * 256:(b + 1) * 256], h_in[p][:, k, b, :], w_z[:, k, :],
                                           start=(k == 0), stop=(k == KT - 1))
                    mm.then_inc(pe_z, 1)

                def keys_tokens():
                    pe.wait_ge(dve_qkv, 2 * i + 1)
                    if prev2:
                        pe.wait_ge(dve_s, i - 1)
                    for b in range(B):
                        pe.transpose(bank[4][:, b * P:(b + 1) * P], kt(p, b), ident)
                    pe.wait_ge(pl_sq, i + 1)
                    for a in range(2):
                        for b in range(B):
                            mm = pe.matmul(bank[4][:, 256 + a * B + b:257 + a * B + b], squares[:, a, b, :], ones,
                                           start=True, stop=True)
                    mm.then_inc(pe_k, 1)

                def keys_keys():
                    if prev2:
                        pe.wait_ge(dve_o, i - 1)
                    for b in range(B):
                        pe.matmul(bank[5][:, b * P:(b + 1) * P], kt(p, b), kt(p, b), start=True, stop=True)
                    for b in range(B):
                        mm = pe.matmul(bank[5][:, (B + b) * P:(B + b + 1) * P], kt(p, b), qt(p, b), start=True, stop=True)
                    mm.then_inc(pe_kkq, 1)

                def turn_decay():
                    pe.wait_ge(act_dec, i + 1)
                    pe.wait_ge(dve_kkq, i + 1)
                    for m in range(M):
                        mm = pe.transpose(bank[5][:, cols(m)], decay[:, m, :], ident)
                    mm.then_inc(pe_dt, 1)

                def turn_m():
                    pe.wait_ge(dve_m, i + 1)
                    if prev:
                        pe.wait_ge(dve_z_l, LATE * (i - 1) + 1)
                    for m in range(M):
                        mm = pe.transpose(bank[6][:, cols(m)], m_neg[p][:, m, :], ident)
                    mm.then_inc(pe_lev_e, 1)

                def turn_v():
                    pe.wait_ge(dve_qkv, 2 * i + 2)
                    if prev2:
                        pe.wait_ge(act_u, i - 1)
                        pe.wait_ge(dve_y, i - 1)
                    elif prev:
                        pe.wait_ge(dve_v, i)
                    for m in range(M):
                        mm = pe.transpose(bank[3][:, cols(m)], qkv[p][:, 2 + m % RATIO, m // RATIO, :], ident)
                    mm.then_inc(pe_v, 1)

                def updates():
                    pe.wait_ge(dve_rhs, i)
                    pe.wait_ge(act_r_l, LATE * i)
                    if cur:
                        pe.wait_ge(dve_v, i + 1)
                    else:
                        pe.wait_ge(dve_y, i - 1)
                    for m in range(M):
                        mm = pe.matmul(bank[3][:, cols(m)], r_inv[:, cols(m)], rhs[:, m, :], start=True, stop=True)
                    mm.then_inc(pe_u, 1)

                def state_update():
                    pe.wait_ge(act_u, i)
                    pe.wait_ge(pl_kd, i)
                    if cur:
                        pe.wait_ge(act_k, i + 1)
                    for m in range(M):
                        mm = pe.matmul(bank[4][:, cols(m)], k_dec[q][:, m // RATIO, m % RATIO, :], u[:, m, :],
                                       start=True, stop=True)
                    mm.then_inc(pe_s, 1)

                def attend():
                    if cur:
                        pe.wait_ge(dve_a, i + 1)
                    for m in range(M):
                        mm = pe.matmul(bank[5][:, cols(m)], a_t[q][:, m // RATIO, m % RATIO, :], u[:, m, :],
                                       start=True, stop=True)
                    mm.then_inc(pe_o, 1)

                def turn_output():
                    pe.wait_ge(pl_x, i - 1)
                    if cur:
                        pe.wait_ge(dve_zs, i + 1)
                    for m in range(M):
                        mm = pe.transpose(bank[2][:, cols(m)], scaled[:, m, :], ident)
                    mm.then_inc(pe_xt, 1)

                def project_output(b):
                    kh = (i - 2) // CH
                    if b == 0:
                        pe.wait_ge(act_xt, i - 1)
                        if prev:
                            pe.wait_ge(act_u, i)
                        else:
                            pe.wait_ge(dve_y, i - 1)
                        pe.wait_ge(ld_wout, 16 * (kh + 1))
                    for r in range(RATIO):
                        mm = pe.matmul(bank[3][:, b * 256:(b + 1) * 256], o_t[:, b * RATIO + r, :],
                                       w_out[:, bass.ds(kh % 2, 1), r * DIM:(r + 1) * DIM].rearrange("p a n -> p (a n)"),
                                       start=(r == 0), stop=(r == RATIO - 1))
                    if b == B - 1:
                        mm.then_inc(pe_y, 1)

                def project_next(ct):
                    if ct == 0:
                        pe.wait_ge(*((dve_rhs, i) if prev else (act_raw, 1)))
                    if ct == 2:
                        pe.wait_ge(*((dve_qs, i) if prev else (act_raw, 2)))
                    project(i + 1, q, ct)

                if prev:
                    keys_state()
                if cur:
                    exponents()
                if prev:
                    level_block(4, i - 1)
                if cur:
                    keys_tokens()
                if prev:
                    grow_block(4, i - 1)
                if cur:
                    keys_keys()
                if prev:
                    turn_r()
                if cur:
                    project_z()
                if prev:
                    level_late(5)
                if nxt:
                    project_next(0)
                if cur:
                    turn_m()
                if prev:
                    grow_late(5)
                if nxt:
                    project_next(1)
                if prev:
                    level_late(6)
                if cur:
                    turn_decay()
                    turn_v()
                if prev:
                    grow_late(6)
                if cur:
                    turn_r_blocks(0)
                if nxt:
                    project_next(2)
                if cur:
                    level_block(1, i)
                if prev:
                    updates()
                if cur:
                    grow_block(1, i)
                if nxt:
                    project_next(3)
                if cur:
                    turn_r_blocks(1)
                if prev:
                    state_update()
                if cur:
                    level_block(2, i)
                if prev:
                    attend()
                if cur:
                    grow_block(2, i)
                if prev2:
                    turn_output()
                if cur:
                    turn_r_blocks(2)
                    level_block(3, i)
                if prev2:
                    project_output(0)
                if cur:
                    grow_block(3, i)
                if prev2:
                    project_output(1)
                if cur:
                    turn_r_blocks(3)

            turns(pe, body)

        @block.scalar
        def _(act):
            def raw_copy(i, j):
                act.wait_ge(pe_proj, 4 * i + 2 * j + 2)
                c = i % CH
                for a in range(2):
                    mm = act.activation(raw[:, 2 * j + a, :, bass.ds(c * P + 3, P)],
                                        bank[j][:, a * 256:(a + 1) * 256].rearrange("p (b t) -> p b t", b=B), ACT.Copy)
                mm.then_inc(act_raw, 1)

            def conv_tanh(i, p, j):
                act.wait_ge(dve_conv, 16 * i + 8 * j + 8)
                act.activation(qkv[p][:, 2 * j:2 * j + 2].rearrange("p a b t -> p (a b t)"),
                               conv[:, 2 * j:2 * j + 2].rearrange("p a b t -> p (a b t)"), ACT.Tanh, scale=0.5).then_inc(act_conv, 1)

            def body(i, p, nxt, cur, prev, prev2):
                q = 1 - p

                def compact(src, dst, done):
                    for b in range(NB):
                        rows = slice(SB * b, SB * (b + 1))
                        whole = src[rows] if len(src.shape) == 3 else src[rows].rearrange("p (m n) -> p m n", m=M)
                        ins = act.activation(dst[rows].rearrange("p (m c) -> p m c", m=M), whole[:, :, rows], ACT.Copy)
                    ins.then_inc(done, 1)

                def grown(l, n):
                    act.wait_ge(pe_inv_e, GROWN * n + l)
                    if l < GROWN:
                        act.activation(r_cmp[:], bank[7][:, 0:P], ACT.Copy).then_inc(act_rc, 1)
                    for b in range(NB):
                        rows = slice(SB * b, SB * (b + 1))
                        ins = act.activation(r_blk[rows].rearrange("p (m n) -> p m n", m=M)[:, :, rows],
                                             bank[7][rows, 0:P].rearrange("p (m c) -> p m c", m=M), ACT.Copy)
                    ins.then_inc(act_rx, 1)

                def late(l):
                    act.wait_ge(pe_inv_l, LATE * (i - 1) + l - EARLY + 1)
                    act.activation(half(r_inv[:], l, True), bank[7][:, 0:256].rearrange("p (q s) -> p q s", s=1 << l),
                                   ACT.Copy).then_inc(act_r_l, 1)
                    if l < LEVELS - 1:
                        act.activation(half(t_inv[:], l, False), bank[7][:, 256:512].rearrange("p (q s) -> p q s", s=1 << l),
                                       ACT.Copy).then_inc(act_t_l, 1)

                if not prev and not prev2:
                    act.wait_ge(ld_const, 16)
                    act.wait_ge(dve_init, 1)
                    for j in range(2):
                        raw_copy(0, j)
                    conv_tanh(0, 0, 0)
                    conv_tanh(0, 0, 1)
                if cur:
                    act.wait_ge(pe_dd, i + 1)
                    act.activation(decay[:].rearrange("p m s -> p (m s)"), bank[7][:], ACT.Exp).then_inc(act_dec, 1)
                    act.wait_ge(pe_k, i + 1)
                    if prev:
                        act.wait_ge(pl_kd, i)
                    act.activation(k_norms[:], bank[4][:, 0:B * P + 2 * B], ACT.Copy).then_inc(act_k, 1)
                if prev:
                    grown(4, i - 1)
                    act.wait_ge(pe_rt, i)
                    act.activation(t_inv[:], bank[7][:], ACT.Copy).then_inc(act_rt, 1)
                if cur:
                    act.wait_ge(pe_z, i + 1)
                    act.activation(z_tanh[:], bank[2][:], ACT.Tanh, scale=0.5).then_inc(act_z, 1)
                    act.wait_ge(dve_m, i + 1)
                    compact(m_neg[p], m_cmp, act_mc)
                if prev:
                    late(5)
                if cur:
                    act.wait_ge(dve_z_e, EARLY * i + 1)
                    compact(z_neg[0], r_cmp, act_rc)
                if nxt:
                    raw_copy(i + 1, 0)
                if prev:
                    late(6)
                    act.wait_ge(pe_u, i)
                    act.activation(u[:].rearrange("p m e -> p (m e)"), bank[3][:], ACT.Copy).then_inc(act_u, 1)
                if cur:
                    grown(1, i)
                if nxt:
                    raw_copy(i + 1, 1)
                if cur:
                    grown(2, i)
                if prev2:
                    act.wait_ge(pe_xt, i - 1)
                    act.activation(o_t[:].rearrange("p m t -> p (m t)"), bank[2][:], ACT.Copy, scale=norm_w[:]).then_inc(act_xt, 1)
                if nxt:
                    conv_tanh(i + 1, q, 0)
                if cur:
                    grown(3, i)
                if nxt:
                    conv_tanh(i + 1, q, 1)

            turns(act, body)

        @block.vector
        def _(dve):
            def convolve(i, p, j, taps_now):
                c = i % CH
                if 0 in taps_now:
                    dve.wait_ge(act_raw, 2 * i + j + 1)
                    if j == 0:
                        dve.wait_ge(ld_taps[p], 16 * (i // 2 + 1))
                for tap in taps_now:
                    for a in range(2):
                        n = 8 * j + 2 * tap + a
                        src = raw[:, 2 * j + a, :, bass.ds(c * P + tap, P)]
                        dst = conv[:, 2 * j + a]
                        w = taps[p][:, 2 * j + a, tap:tap + 1]
                        if tap == 0:
                            dve.tensor_scalar(dst, src, w, None, ALU.mult).then_inc(dve_conv, 1)
                        else:
                            dve.wait_ge(dve_conv, 16 * i + n - 1)
                            dve.scalar_tensor_tensor(dst, src, w, dst, ALU.mult, ALU.add).then_inc(dve_conv, 1)

            def conv_silu(i, p, j):
                dve.wait_ge(act_conv, 2 * i + j + 1)
                f = lambda t: t[:, 2 * j:2 * j + 2].rearrange("p a b t -> p (a b t)")
                dve.scalar_tensor_tensor(f(qkv[p]), f(qkv[p]), 1.0, f(conv), ALU.add, ALU.mult).then_inc(dve_qkv, 1)

            def join(l, produced, count, done):
                wait_apart(dve, sh, produced, count)
                src = half(bank[6][:], 0, True) if l == 0 else bank[6][:, 0:256].rearrange("p (q s) -> p q s", s=1 << l)
                dve.copy_predicated(half(z_neg[l][:], l, True), sh.level_masks[:, FULL.index(l)].rearrange("p (q s) -> p q s", s=1 << l),
                                    src).then_inc(done, 1)

            def body(i, p, nxt, cur, prev, prev2):
                q = 1 - p

                def join_block(l, n):
                    wait_apart(dve, sh, pe_lev_e, EARLY * n + l + 1)
                    dve.copy_predicated(z_neg[l][:].rearrange("p (b m c) -> p b m c", b=NB, m=M),
                                        sh.block_masks[:, l - 1].rearrange("p (m c) -> p m c", m=M).unsqueeze(1).to_broadcast([P, NB, M, SB]),
                                        bank[6][:, 0:P].rearrange("p (b c) -> p b c", b=NB).unsqueeze(2).to_broadcast([P, NB, M, SB])
                                        ).then_inc(dve_z_e, 1)

                def blocks_t(l):
                    dve.wait_ge(pe_tr, GROWN * i + l + 1)
                    dve.tensor_copy(t_cmp[:], bank[6][:, P:2 * P]).then_inc(dve_t, 1)

                def join_late(l):
                    join(l, pe_lev_l, LATE * (i - 1) + l - EARLY + 1, dve_z_l)

                if not prev and not prev2:
                    dve.memset(raw[:, :, :, 0:3], 0.0)
                    dve.memset(state[:], 0.0)
                    dve.memset(r_blk[:], 0.0)
                    for l in range(LEVELS):
                        dve.tensor_copy(z_neg[l][:].rearrange("p (m n) -> p m n", m=M), ident.unsqueeze(1).to_broadcast([P, M, P]))
                    dve.wait_ge(ld_const, 16)
                    dve.tensor_scalar(norm_w[:], norm_w[:], float(P) ** 0.5, None, ALU.mult)
                    dve.memset(y[:], 0.0).then_inc(dve_init, 1)
                    dve.wait_ge(dve_init, 1)
                    dve.sem_inc(dve_y, 1)
                    for j in range(2):
                        convolve(0, 0, j, range(4))
                    for j in range(2):
                        conv_silu(0, 0, j)
                if prev:
                    join_block(4, i - 1)
                    dve.wait_ge(pl_sc, 4 * i)
                    dve.wait_ge(pe_ks, i)
                    dve.wait_ge(dve_v, i)
                    for m in range(M):
                        mm = dve.scalar_tensor_tensor(rhs[:, m, :], bank[0][:, cols(m)],
                                                      ks_scale[q][:, m // RATIO, m % RATIO:m % RATIO + 1], v_beta[:, m, :],
                                                      ALU.mult, ALU.add)
                    mm.then_inc(dve_rhs, 1)
                    if prev2:
                        dve.wait_ge(dve_o, i - 1)
                    dve.wait_ge(pe_qs, i)
                    dve.tensor_tensor(qs[:], bank[1][:].rearrange("p (m e) -> p m e", m=M),
                                      qs_scale[q][:].rearrange("p b r -> p (b r)").unsqueeze(2).to_broadcast([P, M, P]),
                                      ALU.mult).then_inc(dve_qs, 1)
                if cur:
                    dve.wait_ge(pe_kkq, i + 1)
                    dve.tensor_tensor(kkq[:], bank[5][:].rearrange("p (a b s) -> p a b s", a=2, b=B),
                                      kkq_mask.unsqueeze(2).to_broadcast([P, 2, B, P]), ALU.mult).then_inc(dve_kkq, 1)
                    dve.wait_ge(act_dec, i + 1)
                    dve.wait_ge(dve_kkq, i + 1)
                    dve.wait_ge(pl_sc, 4 * i + 2)
                    for m in range(M):
                        mm = dve.scalar_tensor_tensor(m_neg[p][:, m, :], decay[:, m, :], beta_r2[p][:, m // RATIO, m % RATIO:m % RATIO + 1],
                                                      kkq[:, 0, m // RATIO, :], ALU.mult, ALU.mult)
                    mm.then_inc(dve_m, 1)
                if prev:
                    join_late(5)
                if cur:
                    join(0, pe_lev_e, EARLY * i + 1, dve_z_e)
                if prev2:
                    dve.wait_ge(pl_gsq, i - 1)
                    dve.tensor_reduce(o_norm[:], gated_sq[:], AX.X, ALU.add).then_inc(dve_red, 1)
                if cur:
                    if prev2:
                        dve.wait_ge(pl_gt, i - 1)
                    dve.wait_ge(act_z, i + 1)
                    dve.scalar_tensor_tensor(z_silu[p][:], z_tanh[:], 1.0, bank[2][:], ALU.add, ALU.mult).then_inc(dve_zs, 1)
                if prev:
                    join_late(6)
                if cur:
                    dve.wait_ge(pe_v, i + 1)
                    dve.tensor_tensor(v_beta[:], bank[3][:].rearrange("p (m e) -> p m e", m=M),
                                      beta_r[p][:].rearrange("p b r -> p (b r)").unsqueeze(2).to_broadcast([P, M, P]),
                                      ALU.mult).then_inc(dve_v, 1)
                    blocks_t(0)
                    dve.wait_ge(pe_dt, i + 1)
                    dve.tensor_tensor(a_t[p][:], bank[5][:].rearrange("p (b r t) -> p b r t", b=B, r=RATIO),
                                      kkq[:, 1].unsqueeze(2).to_broadcast([P, B, RATIO, P]), ALU.mult).then_inc(dve_a, 1)
                    join_block(1, i)
                if nxt:
                    convolve(i + 1, q, 0, range(2))
                if cur:
                    blocks_t(1)
                if nxt:
                    convolve(i + 1, q, 0, range(2, 3))
                if cur:
                    join_block(2, i)
                if nxt:
                    convolve(i + 1, q, 0, range(3, 4))
                if prev:
                    dve.wait_ge(pe_s, i)
                    for m in range(M):
                        b, r = m // RATIO, m % RATIO
                        mm = dve.scalar_tensor_tensor(state[:, b, r, :], state[:, b, r, :], gate[q][:, 5, b, r:r + 1],
                                                      bank[4][:, cols(m)], ALU.mult, ALU.add)
                    mm.then_inc(dve_s, 1)
                if cur:
                    blocks_t(2)
                if prev:
                    dve.wait_ge(pe_o, i)
                    dve.wait_ge(dve_qs, i)
                    for b in range(B):
                        mm = dve.scalar_tensor_tensor(o[:, b * RATIO:(b + 1) * RATIO, :], bank[5][:, b * 256:(b + 1) * 256].rearrange("p (r e) -> p r e", r=RATIO),
                                                      rnorm[q][:, 0, b:b + 1], qs[:, b * RATIO:(b + 1) * RATIO, :], ALU.mult, ALU.add)
                    mm.then_inc(dve_o, 1)
                if cur:
                    join_block(3, i)
                if nxt:
                    conv_silu(i + 1, q, 0)
                    convolve(i + 1, q, 1, range(2))
                if cur:
                    blocks_t(3)
                if nxt:
                    convolve(i + 1, q, 1, range(2, 4))
                if prev2:
                    dve.wait_ge(pe_y, i - 1)
                    yt = y[:, bass.ds((i - 2) % CH, 1)].rearrange("p c b d -> p (c b d)")
                    dve.tensor_tensor(yt, bank[3][:], yt, ALU.add).then_inc(dve_y, 1)
                if nxt:
                    conv_silu(i + 1, q, 1)

            turns(dve, body)
            dve.wait_ge(dve_y, STEPS + 1)

        @block.gpsimd
        def _(pool):
            def body(i, p, nxt, cur, prev, prev2):
                q = 1 - p
                def below_sums(n, r, first):
                    pool.wait_ge(ld_gate[r], 16 * (n // 2 + 1))
                    if not first:
                        pool.wait_ge(pe_dd, n)
                    pool.tensor_tensor(g_below[:], below.unsqueeze(1).to_broadcast([P, M, P]),
                                       gate[r][:, 1].rearrange("p b r -> p (b r)").unsqueeze(2).to_broadcast([P, M, P]),
                                       ALU.mult).then_inc(pl_g, 1)

                if cur:
                    pool.wait_ge(dve_qkv, 2 * i + 1)
                    if prev:
                        pool.wait_ge(pe_k, i)
                    pool.tensor_tensor(squares[:].rearrange("p a b t -> p (a b t)"), qkv[p][:, 0:2].rearrange("p a b t -> p (a b t)"),
                                       qkv[p][:, 0:2].rearrange("p a b t -> p (a b t)"), ALU.mult).then_inc(pl_sq, 1)
                    below_sums(i, p, not prev)
                    pool.wait_ge(act_k, i + 1)
                    if prev2:
                        pool.wait_ge(dve_o, i - 1)
                    pool.tensor_tensor(rnorm[p][:].rearrange("p a b -> p (a b)"), norms,
                                       sh.pw[:, 2:3].to_broadcast([P, 4]), ALU.add).then_inc(pl_rn, 1)
                    pool.wait_ge(pl_rn, 2 * i + 1)
                    pool.tensor_tensor(rnorm[p][:].rearrange("p a b -> p (a b)"), rnorm[p][:].rearrange("p a b -> p (a b)"),
                                       sh.pw[:, 0:1].to_broadcast([P, 4]), ALU.pow).then_inc(pl_rn, 1)
                    pool.wait_ge(pl_rn, 2 * i + 2)
                    rk = rnorm[p][:, 1].unsqueeze(2).to_broadcast([P, B, RATIO])
                    rq = rnorm[p][:, 0].unsqueeze(2).to_broadcast([P, B, RATIO])
                    pool.tensor_tensor(beta_r[p][:], gate[p][:, 0], rk, ALU.mult).then_inc(pl_sc, 1)
                    pool.wait_ge(pl_sc, 4 * i + 1)
                    pool.tensor_tensor(beta_r2[p][:], beta_r[p][:], rk, ALU.mult).then_inc(pl_sc, 1)
                    pool.tensor_tensor(qs_scale[p][:], gate[p][:, 3], rq, ALU.mult).then_inc(pl_sc, 1)
                    pool.wait_ge(pl_sc, 4 * i + 3)
                    pool.tensor_tensor(ks_scale[p][:], gate[p][:, 2], beta_r2[p][:], ALU.mult).then_inc(pl_sc, 1)
                if prev:
                    pool.wait_ge(act_rx, GROWN * i)
                    if prev2:
                        pool.wait_ge(pe_u, i - 1)
                    pool.tensor_tensor(half(r_inv[:], 5, False), half(r_blk[:], 5, False),
                                       sh.masks[:, 5 * P:5 * P + SB].unsqueeze(1).to_broadcast([P, 2 * M, SB]), ALU.mult).then_inc(pl_r, 1)
                if prev2:
                    pool.wait_ge(dve_o, i - 1)
                    pool.wait_ge(dve_zs, i - 1)
                    pool.tensor_tensor(gated[:], o[:].rearrange("p m e -> p (m e)"), z_silu[p][:], ALU.mult).then_inc(pl_gt, 1)
                    pool.wait_ge(pl_gt, i - 1)
                    pool.tensor_tensor(gated_sq[:].rearrange("p m e -> p (m e)"), gated[:], gated[:], ALU.mult).then_inc(pl_gsq, 1)
                    pool.wait_ge(dve_red, i - 1)
                    pool.tensor_tensor(o_rnorm[:], o_norm[:], sh.pw[:, 3:4].to_broadcast([P, M]), ALU.add).then_inc(pl_on, 1)
                    pool.wait_ge(pl_on, 2 * i - 3)
                    pool.tensor_tensor(o_rnorm[:], o_rnorm[:], sh.pw[:, 0:1].to_broadcast([P, M]), ALU.pow).then_inc(pl_on, 1)
                    pool.wait_ge(pl_on, 2 * i - 2)
                    pool.tensor_tensor(scaled[:], gated[:].rearrange("p (m e) -> p m e", m=M),
                                       o_rnorm[:].unsqueeze(2).to_broadcast([P, M, P]), ALU.mult).then_inc(pl_x, 1)
                    pool.wait_ge(pl_x, i - 1)
                if cur:
                    if prev2:
                        pool.wait_ge(pe_s, i - 1)
                    pool.tensor_tensor(k_dec[p][:], k_tok.unsqueeze(2).to_broadcast([P, B, RATIO, P]),
                                       gate[p][:, 4].unsqueeze(3).to_broadcast([P, B, RATIO, P]), ALU.mult).then_inc(pl_kd, 1)

            turns(pool, body)


def ln_vector(dve, sh, w, n, src, S):
    dve.bn_stats(sh.stats[w][:], src).then_inc(S.stats, 1)
    wait_apart(dve, sh, S.stats, n + 1)
    dve.bn_aggr(sh.mean_var[w][:], sh.stats[w][:]).then_inc(S.mean, 1)


def ln_pool(pool, sh, w, n, S):
    pool.wait_ge(S.mean, n + 1)
    pool.tensor_tensor(sh.rstd[w][:], sh.mean_var[w][:, 1:2], sh.pw[:, 1:2], ALU.add).then_inc(S.var, 1)
    pool.wait_ge(S.var, n + 1)
    pool.tensor_tensor(sh.rstd[w][:], sh.rstd[w][:], sh.pw[:, 0:1], ALU.pow).then_inc(S.rstd, 1)


def ln_norm(dve, sh, w, n, src, S):
    dve.wait_ge(S.rstd, n + 1)
    dve.tensor_scalar(sh.normed[w][:], src, sh.mean_var[w][:, 0:1], sh.rstd[w][:], ALU.subtract, ALU.mult).then_inc(S.norm, 1)


def ln_turn(pe, sh, w, n, bank, S):
    pe.wait_ge(S.norm, n + 1)
    for k in range(KT):
        mm = pe.transpose(bank[:, k * P:(k + 1) * P], sh.normed[w][:, k * P:(k + 1) * P], sh.masks[:, 0:P])
    mm.then_inc(S.turn, 1)


def ln_modulate(dve, sh, w, n, bank, dst, layer, half_of_layer, b, S):
    dve.wait_ge(S.turn, n + 1)
    for k in range(KT):
        ins = dve.tensor_scalar(dst[:, k, :], bank[:, k * P:(k + 1) * P], sh.mod[:, layer, 3 * half_of_layer + 1, k, b:b + 1],
                                sh.mod[:, layer, 3 * half_of_layer, k, b:b + 1], ALU.mult, ALU.add)
    ins.then_inc(S.h, 1)


class LnSems:
    def __init__(self, sem, name):
        self.stats, self.mean, self.var, self.rstd, self.norm, self.turn, self.h = (
            sem(f"{name}_{n}") for n in ("stats", "mean", "var", "rstd", "norm", "turn", "h"))


W = 4
NT = CH * B
NH = 32
NG = 8
HD = 8
PARTS = 3
SPLITS = 2 * PARTS - 2


def ffn0_phase(nc, A, sh, sem):
    with ExitStack() as ctx:
        def sb(name, shape, dt=F32):
            return ctx.enter_context(nc.sbuf_tensor(name, shape, dt))

        w_up = sb("f0_up", [P, KT, DIM])
        w_down = sb("f0_down", [P, KT, DIM])
        w_exp = sb("f0_exp", [P, KT, DIM])
        w_gate = sb("f0_gate", [P, KT, 8])
        w_q = sb("a_wq", [P, KT, DIM])
        w_k = sb("a_wk", [P, KT, 64])
        w_v = sb("a_wv", [P, KT, 64])
        b_q = sb("a_bq", [P, KT])
        b_k = sb("a_bk", [64, 1])
        b_v = sb("a_bv", [P, 64])
        parts = sb("qk_parts", [P, PARTS, 3, T * B], BF16)
        h_a = [sb(f"f0_ha{w}", [P, KT, P]) for w in range(W)]
        h_b = [sb(f"f0_hb{w}", [P, KT, P]) for w in range(W)]
        up = [sb(f"f0_relu{w}", [P, KT, P]) for w in range(W)]
        shared = [sb(f"f0_shared{w}", [P, DIM]) for w in range(W)]
        tmp = [sb(f"f0_tmp{w}", [P, DIM]) for w in range(W)]
        logits = sb("f0_logits", [P, W, 8])
        top = sb("f0_top", [P, W, 8])
        gap = sb("f0_gap", [P, W])
        r1_in = sb("f0_neg", [P, W])
        r1 = sb("f0_r1", [P, W])
        route = sb("f0_route", [P, W])
        qk = [sb(f"qk{w}", [P, 3, P]) for w in range(W)]
        bank = [[ctx.enter_context(nc.psum_tensor(f"f0_{n}{w}", [P, 512], F32)) for w in range(W)] for n in "ab"]
        neg, loaded, yg, x1, mm_up, relu, mm_down, lg, tops, ex, rt, sh_sb, moe, x2, mm_qkv, qk_sb, v_sb, split, stored, init = (
            sem("f0_" + n) for n in ("neg", "loaded", "yg", "x1", "mm_up", "relu", "mm_down", "lg", "tops", "ex", "rt", "shsb", "moe",
                                     "x2", "mm_qkv", "qk_sb", "v_sb", "split", "stored", "init"))
        SA, SB = LnSems(sem, "f0a"), LnSems(sem, "f0b")
        block = ctx.enter_context(nc.Block())
        tiles = [(w, w // B, w % B) for w in range(W)]

        def xt(c, b, t):
            return t[:, bass.ds(c, 1), b, :].rearrange("p a d -> p (a d)")

        @block.sync
        def _(sp):
            for dst, src in ((w_up[:], A["f0_up"]), (w_down[:], A["f0_down"]), (w_exp[:], A["f0_exp"]), (w_gate[:], A["f0_gate"]),
                             (w_q[:], A["a_wq"]), (w_k[:], A["a_wk"]), (w_v[:], A["a_wv"]), (b_q[:], A["a_bq"]),
                             (b_k[:], A["a_bk"]), (b_v[:], A["a_bv"].to_broadcast([P, 64]))):
                sp.dma_start(dst, src).then_inc(loaded, 16)
            def iteration(it):
                sp.wait_ge(v_sb, (it + 1) * 2 * W)
                for b in range(B):
                    tokens = bass.ds(it * (W // B) * P + b * T, W // B * P)
                    for ct in range(3):
                        rows = P if ct < 2 else 64
                        sp.dma_start(sh.scratch[:, ct * P:ct * P + rows, tokens].rearrange("i p t -> p i t"),
                                     parts[0:rows, :, ct, tokens]).then_inc(stored, 16)
            iterations(sp, NT // W, iteration)
            sp.wait_ge(stored, 16 * 3 * B * (NT // W))

        @block.vector
        def _(dve):
            for w in range(W):
                dve.memset(qk[w][:, 2, :], 0.0)
            dve.memset(sh.v_aug[:], 0.0).then_inc(init, 1)
            dve.wait_ge(init, 1)
            dve.memset(sh.v_aug[:, :, :, HD:HD + 1], 1.0).then_inc(init, 1)
            dve.wait_ge(init, 2)
            dve.wait_ge(loaded, 160)
            def iteration(it):
                for w, dc, b in tiles:
                    c = it * (W // B) + dc
                    dve.tensor_tensor(tmp[w][:], xt(c, b, sh.y), sh.gate[:, 0, 0, b, :], ALU.mult).then_inc(yg, 1)
                for w, dc, b in tiles:
                    c, n = it * (W // B) + dc, it * W + w
                    dve.wait_ge(yg, n + 1)
                    dve.tensor_tensor(xt(c, b, sh.x), xt(c, b, sh.x), tmp[w][:], ALU.add).then_inc(x1, 1)
                for w, dc, b in tiles:
                    c, n = it * (W // B) + dc, it * W + w
                    wait_apart(dve, sh, x1, n + 1)
                    ln_vector(dve, sh, w, n, xt(c, b, sh.x), SA)
                for w, dc, b in tiles:
                    c, n = it * (W // B) + dc, it * W + w
                    ln_norm(dve, sh, w, n, xt(c, b, sh.x), SA)
                for w, dc, b in tiles:
                    ln_modulate(dve, sh, w, it * W + w, bank[0][w], h_a[w], 0, 1, b, SA)
                for w, dc, b in tiles:
                    wait_apart(dve, sh, lg, it * W + w + 1)
                    dve.max(top[:, w, :], logits[:, w, :]).then_inc(tops, 1)
                dve.wait_ge(ex, it + 1)
                dve.tensor_scalar(r1[:], gap[:], 1.0, None, ALU.add).then_inc(rt, 1)
                wait_apart(dve, sh, rt, it * 4 + 1)
                dve.reciprocal(r1[:], r1[:]).then_inc(rt, 1)
                dve.wait_ge(rt, it * 4 + 2)
                dve.tensor_tensor(route[:], gap[:], r1[:], ALU.mult).then_inc(rt, 1)
                dve.wait_ge(rt, it * 4 + 3)
                dve.tensor_tensor(route[:], route[:], r1[:], ALU.add).then_inc(rt, 1)
                dve.wait_ge(rt, it * 4 + 4)
                for w, dc, b in tiles:
                    dve.wait_ge(sh_sb, it * W + w + 1)
                    dve.scalar_tensor_tensor(tmp[w][:], bank[0][w][:, 256:512], route[:, w:w + 1], shared[w][:],
                                             ALU.mult, ALU.add).then_inc(moe, 1)
                for w, dc, b in tiles:
                    n = it * W + w
                    dve.wait_ge(moe, it * 2 * W + w + 1)
                    dve.tensor_tensor(tmp[w][:], tmp[w][:], sh.gate[:, 0, 1, b, :], ALU.mult).then_inc(moe, 1)
                for w, dc, b in tiles:
                    c, n = it * (W // B) + dc, it * W + w
                    dve.wait_ge(moe, it * 2 * W + W + w + 1)
                    dve.tensor_tensor(xt(c, b, sh.x), xt(c, b, sh.x), tmp[w][:], ALU.add).then_inc(x2, 1)
                for w, dc, b in tiles:
                    c, n = it * (W // B) + dc, it * W + w
                    wait_apart(dve, sh, x2, n + 1)
                    ln_vector(dve, sh, w, n, xt(c, b, sh.x), SB)
                for w, dc, b in tiles:
                    c, n = it * (W // B) + dc, it * W + w
                    ln_norm(dve, sh, w, n, xt(c, b, sh.x), SB)
                for w, dc, b in tiles:
                    ln_modulate(dve, sh, w, it * W + w, bank[0][w], h_b[w], 1, 0, b, SB)
                def part(k, dc, b):
                    return parts[:, k, :, bass.ds((it * (W // B) + dc) * P + b * T, P)]

                for w, dc, b in tiles:
                    n = it * W + w
                    dve.wait_ge(qk_sb, n + 1)
                    tile = bass.ds((it * (W // B) + dc) + b * CH, 1)
                    dve.tensor_tensor(sh.v_aug[:, tile, :, 0:HD], bank[1][w][:, 384:448].rearrange("p (a g d) -> p a g d", a=1, g=NG),
                                      b_v[:].rearrange("p (a g d) -> p a g d", a=1, g=NG), ALU.add).then_inc(v_sb, 1)
                    dve.tensor_copy(part(0, dc, b), qk[w][:]).then_inc(split, 1)
                for k in range(1, PARTS):
                    for w, dc, b in tiles:
                        dve.wait_ge(split, it * SPLITS * W + (2 * k - 2) * W + w + 1)
                        dve.tensor_tensor(qk[w][:], qk[w][:], part(k - 1, dc, b), ALU.subtract).then_inc(split, 1)
                    for w, dc, b in tiles:
                        dve.wait_ge(split, it * SPLITS * W + (2 * k - 1) * W + w + 1)
                        dve.tensor_copy(part(k, dc, b), qk[w][:]).then_inc(split if k < PARTS - 1 else v_sb, 1)
            iterations(dve, NT // W, iteration)
            dve.wait_ge(v_sb, 2 * NT)
            dve.wait_ge(x2, NT)

        @block.gpsimd
        def _(pool):
            def iteration(it):
                for w in range(W):
                    ln_pool(pool, sh, w, it * W + w, SA)
                for w in range(W):
                    ln_pool(pool, sh, w, it * W + w, SB)
            iterations(pool, NT // W, iteration)

        @block.scalar
        def _(act):
            act.wait_ge(loaded, 160)
            def iteration(it):
                for w in range(W):
                    n = it * W + w
                    act.wait_ge(mm_up, n + 1)
                    act.activation(logits[:, w, :], bank[1][w][:, 256:264], ACT.Copy).then_inc(lg, 1)
                    act.activation(up[w][:].rearrange("p k t -> p (k t)"), bank[1][w][:, 0:256], ACT.Relu).then_inc(relu, 1)
                for w in range(W):
                    n = it * W + w
                    act.wait_ge(tops, n + 1)
                    act.activation(r1_in[:, w:w + 1], top[:, w, 0:1], ACT.Copy, scale=-1.0).then_inc(neg, 1)
                for w in range(W):
                    act.wait_ge(neg, it * W + w + 1)
                    e = act.activation(gap[:, w:w + 1], top[:, w, 1:2], ACT.Exp, bias=r1_in[:, w:w + 1])
                e.then_inc(ex, 1)
                for w in range(W):
                    n = it * W + w
                    act.wait_ge(mm_down, n + 1)
                    act.activation(shared[w][:], bank[0][w][:, 0:256], ACT.Copy).then_inc(sh_sb, 1)
                for w in range(W):
                    n = it * W + w
                    act.wait_ge(mm_qkv, n + 1)
                    for ct in range(KT):
                        act.activation(qk[w][:, ct, :], bank[1][w][:, ct * P:(ct + 1) * P], ACT.Identity, bias=b_q[:, ct:ct + 1])
                    act.activation(qk[w][0:64, 2, :], bank[1][w][0:64, 256:384], ACT.Identity, bias=b_k[:]).then_inc(qk_sb, 1)
            iterations(act, NT // W, iteration)

        @block.tensor
        def _(pe):
            pe.wait_ge(loaded, 160)
            def iteration(it):
                for w in range(W):
                    ln_turn(pe, sh, w, it * W + w, bank[0][w], SA)
                for w in range(W):
                    n = it * W + w
                    pe.wait_ge(SA.h, n + 1)
                    pe.wait_ge(v_sb, it * 2 * W)
                    for ft in range(2):
                        for k in range(KT):
                            pe.matmul(bank[1][w][:, ft * P:(ft + 1) * P], w_up[:, k, ft * P:(ft + 1) * P], h_a[w][:, k, :],
                                      start=(k == 0), stop=(k == KT - 1))
                    for k in range(KT):
                        mm = pe.matmul(bank[1][w][:, 256:264], h_a[w][:, k, :], w_gate[:, k, :], start=(k == 0), stop=(k == KT - 1))
                    mm.then_inc(mm_up, 1)
                for w in range(W):
                    n = it * W + w
                    pe.wait_ge(relu, n + 1)
                    for k in range(KT):
                        pe.matmul(bank[0][w][:, 0:256], up[w][:, k, :], w_down[:, k, :], start=(k == 0), stop=(k == KT - 1))
                    for k in range(KT):
                        mm = pe.matmul(bank[0][w][:, 256:512], h_a[w][:, k, :], w_exp[:, k, :], start=(k == 0), stop=(k == KT - 1))
                    mm.then_inc(mm_down, 1)
                for w in range(W):
                    ln_turn(pe, sh, w, it * W + w, bank[0][w], SB)
                for w in range(W):
                    n = it * W + w
                    pe.wait_ge(SB.h, n + 1)
                    for ct in range(2):
                        for k in range(KT):
                            pe.matmul(bank[1][w][:, ct * P:(ct + 1) * P], w_q[:, k, ct * P:(ct + 1) * P], h_b[w][:, k, :],
                                      start=(k == 0), stop=(k == KT - 1))
                    for k in range(KT):
                        pe.matmul(bank[1][w][0:64, 256:384], w_k[:, k, :], h_b[w][:, k, :], start=(k == 0), stop=(k == KT - 1))
                    for k in range(KT):
                        mm = pe.matmul(bank[1][w][:, 384:448], h_b[w][:, k, :], w_v[:, k, :], start=(k == 0), stop=(k == KT - 1))
                    mm.then_inc(mm_qkv, 1)
            iterations(pe, NT // W, iteration)


QH = T // 512
KC = T // P
DATA = 96
ROWS = DATA + PARTS
UNITS = B * NG
SLOTS = QH * KC
BUF = 3


def attention_phase(nc, A, sh, sem):
    with ExitStack() as ctx:
        def sb(name, shape, dt=F32):
            return ctx.enter_context(nc.sbuf_tensor(name, shape, dt))

        q_rows = [sb(f"q_rows{p}", [ROWS, QH, 4, 512], BF16) for p in range(BUF)]
        k_rows = [sb(f"k_rows{p}", [ROWS, T], BF16) for p in range(BUF)]
        v_unit = [sb(f"v_unit{p}", [P, KC, 32]) for p in range(BUF)]
        ones_row = sb("ones_row", [PARTS, T], BF16)
        half_max = sb("half_max", [P, QH, 16, 2])
        row_max = [sb(f"row_max{h}", [P, 16]) for h in range(QH)]
        neg_max = [sb(f"neg_max{h}", [16, P]) for h in range(QH)]
        max_part = [[sb(f"max_part{k}_{h}", [16, P], BF16) for h in range(QH)] for k in range(PARTS)]
        probs = [sb(f"probs{p}", [P, 4, 512]) for p in range(2)]
        out_t = [sb(f"out_t{p}", [P, 512]) for p in range(2)]
        rden = sb("rden", [P, 16])
        s_ps = [ctx.enter_context(nc.psum_tensor(f"s_ps{k}", [P, 1024], F32)) for k in range(2)]
        m_ps = [ctx.enter_context(nc.psum_tensor(f"m_ps{k}", [P, 512], F32)) for k in range(2)]
        pv_ps = ctx.enter_context(nc.psum_tensor("pv_ps", [P, 512], F32))
        t_ps = ctx.enter_context(nc.psum_tensor("t_ps", [P, 512], F32))
        ld_q, ld_k = ([sem(f"at_{n}{p}") for p in range(BUF)] for n in ("ldq", "ldk"))
        ld_m = [[sem(f"at_ldm{p}_{h}") for h in range(QH)] for p in range(BUF)]
        init, mm_m, red, rmax, mx_t, nmax, mm_s, exp, mm_pv, o_sb, o_tr, den, att, vcp, ld_one = (
            sem("at_" + n) for n in ("init", "mm_m", "red", "rmax", "mx_t", "nmax", "mm_s", "exp", "mm_pv", "o_sb", "o_tr",
                                     "den", "att", "vcp", "ld_one"))
        block = ctx.enter_context(nc.Block())
        ident = sh.masks[:, 0:P]

        def turns(eng, body):
            for u in range(BUF):
                body(u, u, True, u >= 1, u >= 2)
            with eng.Fori(0, (UNITS - BUF) // BUF) as j:
                for p in range(BUF):
                    body(j * BUF + (BUF + p), p, True, True, True)
            for u in range(UNITS - (UNITS - BUF) % BUF, UNITS + 2):
                body(u, u % BUF, u < UNITS, u <= UNITS, True)

        def cycle(u):
            return u // BUF + 1

        @block.sync
        def _(sp):
            def load(u, p, first):
                b, g = u // NG, u % NG
                if not first:
                    sp.wait_ge(mm_s, (u - (BUF - 1)) * 2 * SLOTS)
                for j in range(PARTS):
                    for i in range(PARTS):
                        r = (j * PARTS + i) * HD
                        if first and r == 64:
                            sp.wait_ge(init, p + 1)
                        for hq in range(QH):
                            sp.dma_start(q_rows[p][r:r + HD, hq],
                                         sh.scratch[i:i + 1, bass.ds(g * 4 * HD, 4 * HD), bass.ds(b * T + hq * 512, 512)]
                                         .rearrange("a (h d) t -> d (a h) t", h=4)).then_inc(ld_q[p], 16)
                        sp.dma_start(k_rows[p][r:r + HD, :],
                                     sh.scratch[j:j + 1, bass.ds(2 * P + g * HD, HD), bass.ds(b * T, T)]
                                     .rearrange("a d t -> (a d) t")).then_inc(ld_k[p], 16)

            def body(u, p, cur, prev, prev2):
                if isinstance(u, int) and u == 0:
                    load(0, 0, True)
                    for b in range(BUF):
                        sp.dma_start(k_rows[b][DATA:ROWS, :], ones_row[:]).then_inc(ld_one, 16)
                if cur and not (isinstance(u, int) and u + 1 >= UNITS):
                    load(u + 1, (p + 1) % BUF, isinstance(u, int) and u + 1 < BUF)
                if cur:
                    for h in range(QH):
                        sp.wait_ge(nmax, (2 * u + h + 1) * 6)
                        for k in range(PARTS):
                            sp.dma_start(q_rows[p][DATA + k:DATA + k + 1, h].rearrange("a h (q t) -> a (h q) t", t=P),
                                         max_part[k][h][:]).then_inc(ld_m[p][h], 16)

            turns(sp, body)

        @block.gpsimd
        def _(pool):
            def body(u, p, cur, prev, prev2):
                if cur:
                    b, g = u // NG, u % NG
                    if not isinstance(u, int) or u >= BUF:
                        pool.wait_ge(mm_pv, (u - (BUF - 1)) * SLOTS)
                    pool.tensor_tensor(v_unit[p][:], sh.v_aug[:, bass.ds(b * CH, CH), bass.ds(g, 1), :].rearrange("p c a d -> p (c a) d"),
                                       sh.masks[:, 5 * P:5 * P + 32].unsqueeze(1).to_broadcast([P, KC, 32]), ALU.mult).then_inc(vcp, 1)

            turns(pool, body)

        @block.tensor
        def _(pe):
            def body(u, p, cur, prev, prev2):
                p1, p2 = (p - 1) % BUF, (p - 2) % BUF

                def maximum(n):
                    if not cur:
                        return
                    t, hf = n // 2, n % 2
                    hq, h, qt = t // 16, t // 4 % 4, t % 4
                    if prev or n >= 2:
                        pe.wait_ge(red, 64 * u + n - 1)
                    pe.matmul(m_ps[n % 2][:], q_rows[p][0:DATA, hq, h, qt * P:(qt + 1) * P],
                              k_rows[p][0:DATA, hf * 512:(hf + 1) * 512], start=True, stop=True).then_inc(mm_m, 1)

                def scores(slot, pair):
                    if not prev:
                        return
                    hq, kc = slot // KC, slot % KC
                    if kc == 0 and pair == 0:
                        pe.wait_ge(ld_m[p1][hq], 48 * cycle(u - 1))
                    if prev2 or slot > 0:
                        pe.wait_ge(exp, 2 * SLOTS * (u - 1) + 2 * slot + pair - 1)
                    for hh in range(2):
                        mm = pe.matmul(s_ps[pair][:, hh * 512:(hh + 1) * 512], k_rows[p1][:, kc * P:(kc + 1) * P],
                                       q_rows[p1][:, hq, 2 * pair + hh, :], start=True, stop=True)
                    mm.then_inc(mm_s, 1)

                def attend(slot, pair):
                    v, buf, there = (u - 1, p1, prev) if slot > 0 else (u - 2, p2, prev2)
                    if not there:
                        return
                    slot = (slot - 1) % SLOTS
                    hq, kc = slot // KC, slot % KC
                    if pair == 0:
                        pe.wait_ge(exp, 2 * SLOTS * v + 2 * slot + 2)
                        pe.wait_ge(vcp, v + 1)
                        if kc == 0 and (prev2 or hq > 0):
                            pe.wait_ge(o_sb, QH * v + hq)
                    for h in (2 * pair, 2 * pair + 1):
                        mm = pe.matmul(pv_ps[32 * h:32 * h + 32, :], v_unit[buf][:, kc, :], probs[slot % 2][:, h, :],
                                       start=(kc == 0), stop=(kc == KC - 1))
                    if pair == 1:
                        mm.then_inc(mm_pv, 1)

                def turn_max(v, hq):
                    pe.wait_ge(rmax, QH * v + hq + 1)
                    pe.transpose(t_ps[0:16, 0:P], row_max[hq][:], ident).then_inc(mx_t, 1)

                def turn_out(v, hq):
                    pe.wait_ge(o_sb, QH * v + hq + 1)
                    for t in range(4):
                        mm = pe.transpose(t_ps[:, t * P:(t + 1) * P], out_t[hq][:, t * P:(t + 1) * P], ident)
                    mm.then_inc(o_tr, 1)

                if cur:
                    pe.wait_ge(ld_q[p], 288 * cycle(u))
                    pe.wait_ge(ld_k[p], 144 * cycle(u))
                if not prev2 and not prev:
                    pe.wait_ge(ld_one, 16 * BUF)
                for slot in range(SLOTS):
                    maximum(4 * slot)
                    scores(slot, 0)
                    maximum(4 * slot + 1)
                    scores(slot, 1)
                    maximum(4 * slot + 2)
                    attend(slot, 0)
                    maximum(4 * slot + 3)
                    attend(slot, 1)
                    if slot == 1 and prev:
                        if prev2:
                            pe.wait_ge(att, QH * (u - 2) + 1)
                        turn_max(u - 1, 1)
                    if slot == 3 and prev2:
                        if prev:
                            pe.wait_ge(nmax, 6 * (QH * (u - 1) + 1) + 1)
                        else:
                            pe.wait_ge(att, QH * (u - 2) + 1)
                        turn_out(u - 2, 1)
                    if slot == 9 and cur:
                        if prev2:
                            pe.wait_ge(att, QH * (u - 2) + 2)
                        elif prev:
                            pe.wait_ge(nmax, 6 * (QH * (u - 1) + 1) + 1)
                        turn_max(u, 0)
                    if slot == 11 and prev:
                        if cur:
                            pe.wait_ge(nmax, 6 * QH * u + 1)
                        else:
                            pe.wait_ge(att, QH * (u - 2) + 2)
                        turn_out(u - 1, 0)

            turns(pe, body)

        @block.scalar
        def _(act):
            def body(u, p, cur, prev, prev2):
                for slot in range(SLOTS):
                    n = SLOTS * (u - 1) + slot
                    if prev:
                        if slot >= 2 or prev2:
                            act.wait_ge(mm_pv, n - 1)
                        for pair in range(2):
                            act.wait_ge(mm_s, 2 * n + pair + 1)
                            act.activation(probs[slot % 2][:, 2 * pair:2 * pair + 2, :].rearrange("p h q -> p (h q)"), s_ps[pair][:],
                                           ACT.Exp, scale=float(HD) ** -0.5).then_inc(exp, 1)
                    if slot % KC == 0 and (prev2 if slot == 0 else prev):
                        k = QH * (u - 1) + slot // KC - 1
                        act.wait_ge(mm_pv, n)
                        if not (isinstance(k, int) and k < 2):
                            act.wait_ge(o_tr, k - 1)
                        act.activation(out_t[(slot // KC - 1) % QH][:], pv_ps[:], ACT.Copy).then_inc(o_sb, 1)

            turns(act, body)

        @block.vector
        def _(dve):
            dve.memset(ones_row[:], 1.0)
            for p in range(BUF):
                dve.memset(k_rows[p][64:DATA, :], 0.0)
                dve.memset(q_rows[p][64:DATA], 0.0).then_inc(init, 1)

            def body(u, p, cur, prev, prev2):
                def output(v, hq, part):
                    n = QH * v + hq
                    b, g = v // NG, v % NG
                    src = t_ps[:].rearrange("p (t d) -> p t d", d=32)
                    if part == 0:
                        wait_apart(dve, sh, o_tr, n + 1)
                        dve.reciprocal(rden[:], src[:, :, HD:HD + 1].rearrange("p t a -> p (t a)")).then_inc(den, 1)
                        return
                    if part == 1:
                        dve.wait_ge(den, n + 1)
                    for t in (2 * part - 2, 2 * part - 1):
                        ins = dve.tensor_tensor(sh.att[:, bass.ds(b * CH + 4 * hq + t, 1), bass.ds(g * 32, 32)].rearrange("p a (h d) -> p (a h) d", h=4),
                                                src[:, 4 * t:4 * t + 4, 0:HD], rden[:, 4 * t:4 * t + 4].unsqueeze(2).to_broadcast([P, 4, HD]),
                                                ALU.mult)
                    if part == 2:
                        ins.then_inc(att, 1)

                def join_halves(v, hq):
                    if hq == 0 or prev2 or prev:
                        dve.wait_ge(red, 64 * v + 32 * (hq + 1))
                    n = QH * v + hq
                    if not (isinstance(n, int) and n < 2):
                        dve.wait_ge(mx_t, n - 1)
                    dve.tensor_tensor(row_max[hq][:], half_max[:, hq, :, 0], half_max[:, hq, :, 1], ALU.max).then_inc(rmax, 1)

                def split_max(v, hq, buf, part):
                    n = QH * v + hq
                    if part == 0:
                        dve.wait_ge(mx_t, n + 1)
                        dve.tensor_scalar(neg_max[hq][:], t_ps[0:16, 0:P], -1.0, None, ALU.mult).then_inc(nmax, 1)
                        return
                    dve.wait_ge(nmax, 6 * n + part)
                    if part == 1 and not (isinstance(v, int) and v == 0):
                        dve.wait_ge(ld_m[(buf - 1) % BUF][hq], 48 * cycle(v - 1))
                    k = part // 2
                    if part % 2:
                        dve.tensor_copy(max_part[k][hq][:], neg_max[hq][:]).then_inc(nmax, 1)
                    else:
                        dve.tensor_tensor(neg_max[hq][:], neg_max[hq][:], max_part[k - 1][hq][:], ALU.subtract).then_inc(nmax, 1)

                for n in range(4 * SLOTS):
                    if cur:
                        dve.wait_ge(mm_m, 64 * u + n + 1)
                        dve.tensor_reduce(half_max[:, n // 32, n // 2 % 16, n % 2:n % 2 + 1], m_ps[n % 2][:], AX.X, ALU.max).then_inc(red, 1)
                    if n == 3 and prev:
                        join_halves(u - 1, 1)
                    if n in range(8, 14) and prev:
                        split_max(u - 1, 1, (p - 1) % BUF, n - 8)
                    if n in range(17, 20) and prev2:
                        output(u - 2, 1, n - 17)
                    if n == 33 and cur:
                        join_halves(u, 0)
                    if n in range(41, 47) and cur:
                        split_max(u, 0, p, n - 41)
                    if n in range(49, 52) and prev:
                        output(u - 1, 0, n - 49)

            turns(dve, body)
            dve.wait_ge(att, QH * UNITS)


E8 = 8
FF = 176
FT = E8 * FF // P


def ffn1_phase(nc, A, sh, sem, out):
    with ExitStack() as ctx:
        def sb(name, shape, dt=F32):
            return ctx.enter_context(nc.sbuf_tensor(name, shape, dt))

        w_o = sb("f1_wo", [P, KT, DIM])
        b_o = sb("f1_bo", [P, DIM])
        w_r = sb("f1_router", [P, KT, E8])
        w_g = sb("f1_wg", [P, KT, FT * P])
        w_u = sb("f1_wu", [P, KT, FT * P])
        w_d = sb("f1_wd", [P, FT, DIM])
        expand = sb("f1_expand", [E8, FT * P])
        iota = sb("f1_iota", [P, E8])
        att_t = [sb(f"f1_att{w}", [P, KT, P]) for w in range(W)]
        tmp = [sb(f"f1_tmp{w}", [P, DIM]) for w in range(W)]
        attended = [sb(f"f1_attended{w}", [P, DIM]) for w in range(W)]
        h_all = sb("f1_h", [P, KT, W * P])
        logits = sb("f1_logits", [P, W, E8])
        top = sb("f1_top", [P, W, 8])
        idx = sb("f1_idx", [P, W, 8], U32)
        idx_f = sb("f1_idxf", [P, W, 8])
        neg = sb("f1_neg", [P, W])
        wt = sb("f1_wt", [P, 3, W])
        comb = sb("f1_comb", [P, 2, W, E8])
        comb_t = sb("f1_combt", [E8, W * P])
        g_tanh = [sb(f"f1_gt{p}", [P, W * P]) for p in range(2)]
        silu = [sb(f"f1_silu{p}", [P, W * P]) for p in range(2)]
        act_c = [sb(f"f1_c{p}", [P, W * P]) for p in range(2)]
        hid = sb("f1_hid", [P, FT, W * P])
        bank = [ctx.enter_context(nc.psum_tensor(f"f1_b{k}", [P, 512], F32)) for k in range(8)]
        copied = sem("f1_copied")
        loaded, tr, at_sb, mm_o, ob, og, x3, mm_r, lg, tops, idxs, ng, ex, rt, cb, ct_ps, ct_sb = (
            sem("f1_" + n) for n in ("loaded", "tr", "at_sb", "mm_o", "ob", "og", "x3", "mm_r", "lg", "tops", "idxs", "ng", "ex",
                                     "rt", "cb", "ct_ps", "ct_sb"))
        mm_g, mm_u, mm_c, tanh, sl, ccp, prod, hd, mm_y, yg, x4, stored = (
            sem("f1_" + n) for n in ("mm_g", "mm_u", "mm_c", "tanh", "sl", "ccp", "prod", "hd", "mm_y", "yg", "x4", "stored"))
        S = LnSems(sem, "f1")
        block = ctx.enter_context(nc.Block())
        tiles = [(w, w // B, w % B) for w in range(W)]
        ITS = NT // W

        def xt(c, b, t):
            return t[:, bass.ds(c, 1), b, :].rearrange("p a d -> p (a d)")

        def turns(eng, first, body):
            first()
            body(0, True)
            with eng.Fori(1, ITS - 1) as it:
                body(it, True)
            body(ITS - 1, False)

        @block.sync
        def _(sp):
            for dst, src in ((w_o[:], A["a_wo"]), (b_o[:], A["a_bo"].to_broadcast([P, DIM])), (w_r[:], A["f1_router"]),
                             (w_g[:], A["f1_wg"]), (w_u[:], A["f1_wu"]), (w_d[:], A["f1_wd"]), (expand[:], A["f1_expand"]),
                             (iota[:], A["f1_iota"])):
                sp.dma_start(dst, src).then_inc(loaded, 16)
            with sp.Fori(0, ITS) as it:
                for w, dc, b in tiles:
                    c = it * (W // B) + dc
                    sp.wait_ge(x4, it * W + w + 1)
                    sp.dma_start(out[b].rearrange("(c p) d -> p c d", p=P)[:, bass.ds(c, 1), :], sh.x[:, bass.ds(c, 1), b, :]).then_inc(stored, 16)
            sp.wait_ge(stored, 16 * NT)

        @block.tensor
        def _(pe):
            pe.wait_ge(loaded, 128)
            ident = sh.masks[:, 0:P]

            def turn_attended(it):
                for w in range(W):
                    pe.wait_ge(copied, it * W + w + 1)
                    for k in range(KT):
                        mm = pe.transpose(bank[4 + w][:, k * P:(k + 1) * P], attended[w][:, k * P:(k + 1) * P], ident)
                    mm.then_inc(tr, 1)

            def project_attended(it):
                for w in range(W):
                    pe.wait_ge(at_sb, it * W + w + 1)
                    for k in range(KT):
                        mm = pe.matmul(bank[4 + w][:, 256:512], att_t[w][:, k, :], w_o[:, k, :], start=(k == 0), stop=(k == KT - 1))
                    mm.then_inc(mm_o, 1)

            def turn_normed(it):
                for w in range(W):
                    pe.wait_ge(ob, it * W + w + 1)
                    ln_turn(pe, sh, w, it * W + w, bank[4 + w], S)

            def route(it):
                for w in range(W):
                    pe.wait_ge(S.h, it * W + w + 1)
                    for k in range(KT):
                        mm = pe.matmul(bank[4 + w][:, 256:264], h_all[:, k, w * P:(w + 1) * P], w_r[:, k, :], start=(k == 0), stop=(k == KT - 1))
                    mm.then_inc(mm_r, 1)

            fronts = (turn_attended, project_attended, turn_normed, route)

            def first():
                for stage in fronts:
                    stage(0)

            def body(it, more):
                def gate_up(f):
                    n = it * FT + f
                    if f < 2:
                        pe.wait_ge(lg, (it + 1) * W)
                    else:
                        pe.wait_ge(hd, n - 1)
                    for bk, wts, s in ((4 + f % 2, w_g, mm_g), (6 + f % 2, w_u, mm_u)):
                        for k in range(KT):
                            mm = pe.matmul(bank[bk][:], wts[:, k, f * P:(f + 1) * P], h_all[:, k, :], start=(k == 0), stop=(k == KT - 1))
                        mm.then_inc(s, 1)

                def spread(f):
                    if f >= 2:
                        pe.wait_ge(ccp, it * FT + f - 1)
                    pe.matmul(bank[f % 2][:], expand[:, f * P:(f + 1) * P], comb_t[:], start=True, stop=True).then_inc(mm_c, 1)

                gate_up(0)
                gate_up(1)
                pe.wait_ge(cb, (it + 1) * 2)
                if not (isinstance(it, int) and it == 0):
                    pe.wait_ge(yg, it * W)
                for w in range(W):
                    mm = pe.transpose(bank[0][0:E8, w * P:(w + 1) * P], comb[:, 0, w, :], ident)
                mm.then_inc(ct_ps, 1)
                pe.wait_ge(ct_sb, it + 1)
                for f in range(FT):
                    spread(f)
                    if f >= 2:
                        gate_up(f)
                pe.wait_ge(hd, (it + 1) * FT)
                pe.wait_ge(ccp, (it + 1) * FT)
                for w in range(W):
                    for f in range(FT):
                        mm = pe.matmul(bank[w][:, 0:256], hid[:, f, w * P:(w + 1) * P], w_d[:, f, :], start=(f == 0), stop=(f == FT - 1))
                    mm.then_inc(mm_y, 1)
                    if more:
                        fronts[w](it + 1)

            turns(pe, first, body)

        @block.scalar
        def _(act):
            act.wait_ge(loaded, 128)

            def front(it):
                for w in range(W):
                    act.wait_ge(tr, it * W + w + 1)
                    act.activation(att_t[w][:].rearrange("p k t -> p (k t)"), bank[4 + w][:, 0:256], ACT.Copy).then_inc(at_sb, 1)
                for w in range(W):
                    act.wait_ge(mm_r, it * W + w + 1)
                    act.activation(logits[:, w, :], bank[4 + w][:, 256:264], ACT.Copy).then_inc(lg, 1)
                for w in range(W):
                    act.wait_ge(tops, it * W + w + 1)
                    act.activation(neg[:, w:w + 1], top[:, w, 0:1], ACT.Copy, scale=-1.0).then_inc(ng, 1)
                for w in range(W):
                    act.wait_ge(ng, it * W + w + 1)
                    e = act.activation(wt[:, 0, w:w + 1], top[:, w, 1:2], ACT.Exp, bias=neg[:, w:w + 1])
                e.then_inc(ex, 1)

            def body(it, more):
                def tanh_of(f):
                    act.wait_ge(mm_g, it * FT + f + 1)
                    act.activation(g_tanh[f % 2][:], bank[4 + f % 2][:], ACT.Tanh, scale=0.5).then_inc(tanh, 1)

                def spread_copy(f):
                    act.wait_ge(mm_c, it * FT + f + 1)
                    if f >= 2:
                        act.wait_ge(hd, it * FT + f - 1)
                    act.activation(act_c[f % 2][:], bank[f % 2][:], ACT.Copy, scale=0.5).then_inc(ccp, 1)

                tanh_of(0)
                tanh_of(1)
                act.wait_ge(ct_ps, it + 1)
                act.activation(comb_t[:], bank[0][0:E8, :], ACT.Copy).then_inc(ct_sb, 1)
                for f in range(FT):
                    spread_copy(f)
                    if f >= 2:
                        tanh_of(f)
                if more:
                    front(it + 1)

            turns(act, lambda: front(0), body)

        @block.gpsimd
        def _(pool):
            def front(it):
                for w in range(W):
                    ln_pool(pool, sh, w, it * W + w, S)

            def body(it, more):
                for f in range(FT):
                    n = it * FT + f
                    pool.wait_ge(sl, n + 1)
                    pool.wait_ge(ccp, n + 1)
                    pool.tensor_tensor(silu[f % 2][:], silu[f % 2][:], act_c[f % 2][:], ALU.mult).then_inc(prod, 1)
                if more:
                    front(it + 1)

            turns(pool, lambda: front(0), body)

        @block.vector
        def _(dve):
            dve.wait_ge(loaded, 128)

            def copy_attended(it):
                if not (isinstance(it, int) and it == 0):
                    dve.wait_ge(x3, it * W)
                for w, dc, b in tiles:
                    c = it * (W // B) + dc
                    dve.tensor_copy(attended[w][:], sh.att[:, bass.ds(b * CH + c, 1), :].rearrange("p a d -> p (a d)")).then_inc(copied, 1)

            def add_attended(it):
                for w, dc, b in tiles:
                    dve.wait_ge(mm_o, it * W + w + 1)
                    dve.tensor_tensor(attended[w][:], bank[4 + w][:, 256:512], b_o[:], ALU.add).then_inc(ob, 1)
                for w, dc, b in tiles:
                    dve.wait_ge(ob, it * W + w + 1)
                    dve.tensor_tensor(attended[w][:], attended[w][:], sh.gate[:, 1, 0, b, :], ALU.mult).then_inc(og, 1)
                for w, dc, b in tiles:
                    c, n = it * (W // B) + dc, it * W + w
                    dve.wait_ge(og, n + 1)
                    dve.tensor_tensor(xt(c, b, sh.x), xt(c, b, sh.x), attended[w][:], ALU.add).then_inc(x3, 1)
                for w, dc, b in tiles:
                    c, n = it * (W // B) + dc, it * W + w
                    wait_apart(dve, sh, x3, n + 1)
                    ln_vector(dve, sh, w, n, xt(c, b, sh.x), S)

            def norm(it):
                for w, dc, b in tiles:
                    ln_norm(dve, sh, w, it * W + w, xt(it * (W // B) + dc, b, sh.x), S)
                for w, dc, b in tiles:
                    ln_modulate(dve, sh, w, it * W + w, bank[4 + w], h_all[:, :, w * P:(w + 1) * P], 1, 1, b, S)

            def choose(it):
                for w in range(W):
                    wait_apart(dve, sh, lg, it * W + w + 1)
                    dve.max(top[:, w, :], logits[:, w, :]).then_inc(tops, 1)
                for w in range(W):
                    wait_apart(dve, sh, tops, it * W + w + 1)
                    dve.max_index(idx[:, w, :], top[:, w, :], logits[:, w, :]).then_inc(idxs, 1)
                dve.wait_ge(idxs, (it + 1) * W)
                dve.tensor_copy(idx_f[:], idx[:]).then_inc(rt, 1)
                dve.wait_ge(ex, it + 1)
                dve.tensor_scalar(wt[:, 1, :], wt[:, 0, :], 1.0, None, ALU.add).then_inc(rt, 1)
                wait_apart(dve, sh, rt, it * 4 + 2)
                dve.reciprocal(wt[:, 1, :], wt[:, 1, :]).then_inc(rt, 1)
                dve.wait_ge(rt, it * 4 + 3)
                dve.tensor_tensor(wt[:, 2, :], wt[:, 0, :], wt[:, 1, :], ALU.mult).then_inc(rt, 1)
                dve.wait_ge(rt, it * 4 + 4)
                for w in range(W):
                    for j in range(2):
                        ins = dve.tensor_scalar(comb[:, j, w, :], iota[:], idx_f[:, w, j:j + 1], wt[:, 1 + j, w:w + 1],
                                                ALU.is_equal, ALU.mult)
                ins.then_inc(cb, 1)
                dve.wait_ge(cb, it * 2 + 1)
                dve.tensor_tensor(comb[:, 0], comb[:, 0], comb[:, 1], ALU.add).then_inc(cb, 1)

            def first():
                copy_attended(0)
                add_attended(0)
                norm(0)
                choose(0)

            def body(it, more):
                def gate_output(w):
                    b = w % B
                    dve.wait_ge(mm_y, it * W + w + 1)
                    if not (isinstance(it, int) and it == 0):
                        dve.wait_ge(x4, it * W)
                    dve.tensor_tensor(tmp[w][:], bank[w][:, 0:256], sh.gate[:, 1, 1, b, :], ALU.mult).then_inc(yg, 1)

                if more:
                    copy_attended(it + 1)
                for f in range(FT + 1):
                    if f < FT:
                        dve.wait_ge(tanh, it * FT + f + 1)
                        if f >= 2:
                            dve.wait_ge(hd, it * FT + f - 1)
                        dve.scalar_tensor_tensor(silu[f % 2][:], g_tanh[f % 2][:], 1.0, bank[4 + f % 2][:], ALU.add, ALU.mult).then_inc(sl, 1)
                    if f > 0:
                        n = it * FT + f - 1
                        dve.wait_ge(prod, n + 1)
                        dve.wait_ge(mm_u, n + 1)
                        if f == 1 and not (isinstance(it, int) and it == 0):
                            dve.wait_ge(mm_y, it * W)
                        dve.tensor_tensor(hid[:, f - 1, :], bank[6 + (f - 1) % 2][:], silu[(f - 1) % 2][:], ALU.mult).then_inc(hd, 1)
                gate_output(0)
                if more:
                    add_attended(it + 1)
                gate_output(1)
                if more:
                    norm(it + 1)
                gate_output(2)
                gate_output(3)
                if more:
                    choose(it + 1)
                for w, dc, b in tiles:
                    c = it * (W // B) + dc
                    dve.wait_ge(yg, it * W + w + 1)
                    dve.tensor_tensor(xt(c, b, sh.x), xt(c, b, sh.x), tmp[w][:], ALU.add).then_inc(x4, 1)

            turns(dve, first, body)


def build(nc, A, out):
    held = []

    def sem(name):
        held.append(nc.alloc_semaphore(name=name))
        return held[-1]

    def phase_end():
        nc.all_engine_barrier()
        nc.clear_and_free_semaphores(held)
        held.clear()
        nc.all_engine_barrier()

    with ExitStack() as top:
        sh = Shared()

        def sb(name, shape, dt=F32):
            return top.enter_context(nc.sbuf_tensor(name, shape, dt))

        sh.apart = top.enter_context(nc.semaphore("apart"))
        sh.masks = sb("masks_sb", [P, 6 * P])
        sh.mod = sb("mod", [P, 2, 6, KT, B])
        sh.gate = sb("mod_gate", [P, 2, 2, B, DIM])
        sh.pw = sb("pw", [P, 4])
        sh.x = sb("x_res", [P, CH, B, DIM])
        sh.scratch = nc.dram_tensor("qk_rows", (PARTS, 2 * P + 64, B * T), BF16, kind="Internal").ap()
        sh.y = sb("y_res", [P, CH, B, DIM])
        with ExitStack() as first:
            sh.level_masks = first.enter_context(nc.sbuf_tensor("level_masks_sb", [P, len(FULL), 256], I32))
            sh.block_masks = first.enter_context(nc.sbuf_tensor("block_masks_sb", [P, len(COMPACT), P], I32))
            setup_phase(nc, A, sh, sem)
            sh.h = first.enter_context(nc.sbuf_tensor("h_res", [P, KT, CH * B * P], F32))
            sh.gates = first.enter_context(nc.sbuf_tensor("gates_sb", [P, STEPS, 6, M], F32))
            ln_phase(nc, A, sh, sem)
            phase_end()
            delta_phase(nc, A, sh, sem)
            phase_end()
        sh.stats = [sb(f"stats{w}", [P, 6]) for w in range(W)]
        sh.mean_var = [sb(f"mean_var{w}", [P, 2]) for w in range(W)]
        sh.rstd = [sb(f"rstd{w}", [P, 1]) for w in range(W)]
        sh.normed = [sb(f"normed{w}", [P, DIM]) for w in range(W)]
        sh.v_aug = sb("v_aug", [P, NT, NG, 32])
        ffn0_phase(nc, A, sh, sem)
        sh.att = sb("attended", [P, NT, DIM])
        attention_phase(nc, A, sh, sem)
        ffn1_phase(nc, A, sh, sem, out)


def layouts(inp):
    a = {k: np.ascontiguousarray(v) for k, v in inp.items()}
    d = {k: a[k] for k in ("L0_attn_hidden_states", "L0_attn_W_qkvz", "L0_attn_W_ba", "L0_attn_W_out", "L0_wmod", "L1_wmod")}
    d["c0"] = a["L0_c"].reshape(B, KT, P).transpose(2, 1, 0)
    d["c1"] = a["L1_c"].reshape(B, KT, P).transpose(2, 1, 0)
    d["alog"] = a["L0_attn_A_log"].reshape(1, 2 * HK)
    d["dtb"] = a["L0_attn_dt_bias"].reshape(1, 2 * HK)
    d["norm_w"] = a["L0_attn_norm_weight"].reshape(P, 1)
    w = a["L0_attn_conv_w"]
    q, k, v = w[:2048].reshape(HK, 1, P, 4), w[2048:4096].reshape(HK, 1, P, 4), w[4096:].reshape(HK, RATIO, P, 4)
    d["conv_w"] = np.concatenate([q, k, v], 1).transpose(2, 0, 1, 3).reshape(P, HK * 16)
    rows = lambda m: m.reshape(KT, P, -1).transpose(1, 0, 2)
    d["f0_up"], d["f0_down"] = rows(a["L0_ffn_W_up"].T), rows(a["L0_ffn_W_down"].T)
    d["f0_exp"], d["f0_gate"] = rows(a["L0_ffn_W_expert"]), rows(a["L0_ffn_W_gate"].T)
    d["a_wq"], d["a_wk"], d["a_wv"], d["a_wo"] = (rows(a["L1_attn_W" + n]) for n in "qkvo")
    d["a_bq"] = a["L1_attn_bq"].reshape(KT, P).T
    d["a_bk"] = a["L1_attn_bk"].reshape(64, 1)
    d["a_bv"], d["a_bo"] = a["L1_attn_bv"].reshape(1, 64), a["L1_attn_bo"].reshape(1, DIM)
    d["f1_router"] = rows(a["L1_ffn_gate_w"])
    d["f1_wg"], d["f1_wu"] = (rows(a["L1_ffn_w_" + n].transpose(1, 0, 2).reshape(DIM, E8 * FF)) for n in ("gate", "up"))
    d["f1_wd"] = a["L1_ffn_w_down"].reshape(FT, P, DIM).transpose(1, 0, 2)
    d["f1_expand"] = np.repeat(np.eye(E8, dtype=np.float32), FF, axis=1)
    d["f1_iota"] = np.tile(np.arange(E8, dtype=np.float32), (P, 1))
    i = np.arange(P)
    le = (i[:, None] <= i[None, :]).astype(np.float32)
    sl = (i[:, None] > i[None, :]).astype(np.float32)
    d["masks"] = np.concatenate([np.eye(P, dtype=np.float32), -2 * sl, le * np.float32(P ** -0.5), le, sl,
                                 np.ones((P, P), np.float32)], 1)
    lm = np.zeros((P, len(FULL), M, 64), np.int32)
    for n, l in enumerate(FULL):
        s = 1 << l
        cols = np.array([c for c in range(P) if (c // s) % 2])
        lm[:, n] = ((i[:, None] // (2 * s) == cols[None, :] // (2 * s)) & ((i[:, None] // s) % 2 == 0))[:, None, :]
    d["level_masks"] = lm.reshape(P, len(FULL), 256)
    bm = np.zeros((P, len(COMPACT), P), np.int32)
    for n, l in enumerate(COMPACT):
        s = 1 << l
        bm[:, n] = ((i[:, None] // (2 * s) == i[None, :] // (2 * s)) & ((i[:, None] // s) % 2 == 0) & ((i[None, :] // s) % 2 == 1))
    d["block_masks"] = bm
    return {k: np.ascontiguousarray(v) for k, v in d.items()}


def kernel(**inputs):
    import concourse.bacc as bacc
    from concourse.bass_utils import run_bass_kernel_spmd

    nc = bacc.Bacc("TRN2", target_bir_lowering=False, num_devices=1)
    arrays = {"in_" + name: a for name, a in layouts(inputs).items()}
    A = {name[3:]: nc.dram_tensor(name, a.shape, mybir.dt.from_np(a.dtype), kind="ExternalInput").ap() for name, a in arrays.items()}
    out = nc.dram_tensor("out", (B, T, DIM), F32, kind="ExternalOutput").ap()
    build(nc, A, out)
    return run_bass_kernel_spmd(nc, [arrays], core_ids=[0]).results[0]["out"]
```
